# Optimizing a Trainium2 kernel written in Bass

```python
import numpy as np
import jax
import jax.numpy as jnp

def _softmax(x, axis=-1):
    return jax.nn.softmax(x, axis=axis)

def _gelu(x):
    return jax.nn.gelu(x, approximate=True)

def _silu(x):
    return jax.nn.silu(x)

def _sigmoid(x):
    return jax.nn.sigmoid(x)

def _layernorm(x, axis=-1, eps=1e-05):
    m = jnp.mean(x, axis=axis, keepdims=True)
    v = jnp.var(x, axis=axis, keepdims=True)
    return (x - m) / jnp.sqrt(v + eps)

def _scatter_add(tgt, idx, src, axis=0):
    return tgt.at[idx].add(src)

def _segment_sum(src, seg, n):
    return jax.ops.segment_sum(src, seg, n)
kernel_name = 'mk_gps_d1_gnn_r8_f30400'

def setup_inputs(seed: int=0):
    np.random.seed(seed)
    _w = jnp.asarray

    def _rec_inputs():
        import jax
        import jax.numpy as jnp
        _gk = jax.random.key(seed)
        x = -0.0002117 + 1 * jax.random.normal(jax.random.fold_in(_gk, 1), (12500, 256), jnp.float32)
        _s = jax.random.randint(jax.random.fold_in(_gk, 2), (100000,), 0, 12500, jnp.int32)
        _d = jax.random.randint(jax.random.fold_in(_gk, 3), (100000,), 0, 12500, jnp.int32)
        _loop = jnp.arange(12500, dtype=jnp.int32)
        src = jnp.concatenate([_s, _d, _loop])
        dst = jnp.concatenate([_d, _s, _loop])
        _o = jnp.argsort(dst, stable=True)
        src = src[_o]
        dst = dst[_o]
        return (x, src, dst)
    x, src, dst = _rec_inputs()

    def _L0_gnn_setup():
        import jax, jax.numpy as jnp
        import numpy as np
        N_NODES = 12500
        N_EDGES = 400000
        D_IN = 256
        D_HID = 256
        D_OUT = 256

        def _sage_conv(x, src, tgt, W_l, b_l, W_r):
            n = x.shape[0]
            msgs = x[src]
            agg = jax.ops.segment_sum(msgs, tgt, num_segments=n)
            deg = jax.ops.segment_sum(jnp.ones((src.shape[0],), x.dtype), tgt, num_segments=n)
            agg = agg / jnp.maximum(deg, 1.0)[:, None]
            return agg @ W_l + b_l + x @ W_r
        key = jax.random.key(seed)
        ks = jax.random.split(key, 8)
        x = jax.random.normal(ks[0], (N_NODES, D_IN), dtype=jnp.float32)
        edge_index = jax.random.randint(ks[1], (2, N_EDGES), 0, N_NODES, dtype=jnp.int64)
        s1 = 1.0 / np.sqrt(D_IN)
        s2 = 1.0 / np.sqrt(D_HID)
        return {'x': x, 'edge_index': edge_index, 'W_l1': jax.random.uniform(ks[2], (D_IN, D_HID), jnp.float32, -s1, s1), 'b1': jnp.zeros((D_HID,), jnp.float32), 'W_r1': jax.random.uniform(ks[3], (D_IN, D_HID), jnp.float32, -s1, s1), 'W_l2': jax.random.uniform(ks[4], (D_HID, D_OUT), jnp.float32, -s2, s2), 'b2': jnp.zeros((D_OUT,), jnp.float32), 'W_r2': jax.random.uniform(ks[5], (D_HID, D_OUT), jnp.float32, -s2, s2)}
    _L0_gnn_all = _L0_gnn_setup()
    _L0_gnn_in = {k: v for k, v in _L0_gnn_all.items() if k in ('W_l1', 'b1', 'W_r1', 'W_l2', 'b2', 'W_r2')}
    del _L0_gnn_all

    def _L0_mix_setup():
        import jax, jax.numpy as jnp
        import numpy as np
        N, F, C, H = (32, 512, 256, 8)
        D = C // H
        EPS_ATTN = 1e-06
        EPS_LN = 1e-05

        def layer_norm(x, g, b):
            mu = jnp.mean(x, axis=-1, keepdims=True)
            var = jnp.var(x, axis=-1, keepdims=True)
            return (x - mu) * jax.lax.rsqrt(var + EPS_LN) * g + b
        key = jax.random.key(seed)
        ks = jax.random.split(key, 8)
        s = 1.0 / np.sqrt(C)
        return {'x': jax.random.normal(ks[0], (N, F, C), jnp.float32), 'Wqkv': jax.random.uniform(ks[1], (3 * C, C), jnp.float32, -s, s), 'ln1_g': jnp.ones((C,), jnp.float32), 'ln1_b': jnp.zeros((C,), jnp.float32), 'W1': jax.random.uniform(ks[2], (C, C), jnp.float32, -s, s), 'b1': jax.random.uniform(ks[3], (C,), jnp.float32, -s, s), 'W2': jax.random.uniform(ks[4], (C, C), jnp.float32, -s, s), 'b2': jax.random.uniform(ks[5], (C,), jnp.float32, -s, s), 'ln2_g': jnp.ones((C,), jnp.float32), 'ln2_b': jnp.zeros((C,), jnp.float32)}
    _L0_mix_all = _L0_mix_setup()
    _L0_mix_in = {k: v for k, v in _L0_mix_all.items() if k in ('Wqkv', 'ln1_g', 'ln1_b', 'W1', 'b1', 'W2', 'b2', 'ln2_g', 'ln2_b')}
    del _L0_mix_all

    def _L0_ffn_setup():
        import jax, jax.numpy as jnp
        import numpy as np
        B, N, D = (16, 512, 256)
        NUM_EXPERTS, TOP_K, HEADS = (4, 2, 4)
        N_EDGES = 131072
        LN_EPS = 1e-05

        def _layernorm(x, g, b):
            mu = x.mean(-1, keepdims=True)
            var = ((x - mu) ** 2).mean(-1, keepdims=True)
            return (x - mu) * jax.lax.rsqrt(var + LN_EPS) * g + b

        def _forward(x, edge_index, W_gat, att_src, att_dst, b_gat, ln_gamma, ln_beta, W1, b1, W2, b2):
            Bc, Nc, Dc = x.shape
            M = Bc * Nc
            x_flat = x.reshape(M, Dc)
            h = (x_flat @ W_gat).reshape(M, HEADS, NUM_EXPERTS)
            loops = jnp.arange(M, dtype=edge_index.dtype)
            src = jnp.concatenate([edge_index[0], loops])
            dst = jnp.concatenate([edge_index[1], loops])
            a_src = (h * att_src).sum(-1)
            a_dst = (h * att_dst).sum(-1)
            e = jax.nn.leaky_relu(a_src[src] + a_dst[dst], negative_slope=0.2)
            e_max = jax.ops.segment_max(e, dst, num_segments=M)
            ee = jnp.exp(e - e_max[dst])
            denom = jax.ops.segment_sum(ee, dst, num_segments=M)
            alpha = ee / (denom[dst] + 1e-16)
            msg = h[src] * alpha[:, :, None]
            agg = jax.ops.segment_sum(msg, dst, num_segments=M).reshape(M, HEADS * NUM_EXPERTS) + b_gat
            scores = _layernorm(agg, ln_gamma, ln_beta).reshape(M, HEADS, NUM_EXPERTS).mean(1)
            scores = scores.reshape(Bc, Nc, NUM_EXPERTS)
            topk_s, topk_i = jax.lax.top_k(scores, TOP_K)
            w = jax.nn.softmax(topk_s, axis=-1)
            out = jnp.zeros_like(x)
            for ei in range(NUM_EXPERTS):
                g = jnp.where(topk_i == ei, w, 0.0).sum(-1)
                hh = jax.nn.gelu(x @ W1[ei] + b1[ei], approximate=False)
                out = out + g[..., None] * (hh @ W2[ei] + b2[ei])
            return out
        key = jax.random.key(seed)
        ks = jax.random.split(key, 8)
        s = 0.05
        return {'x': jax.random.normal(ks[0], (B, N, D), jnp.float32), 'W_gat': jax.random.normal(ks[1], (D, HEADS * NUM_EXPERTS), jnp.float32) * s, 'att_src': jax.random.normal(ks[2], (HEADS, NUM_EXPERTS), jnp.float32) * s, 'att_dst': jax.random.normal(ks[3], (HEADS, NUM_EXPERTS), jnp.float32) * s, 'b_gat': jnp.zeros((HEADS * NUM_EXPERTS,), jnp.float32), 'ln_gamma': jnp.ones((HEADS * NUM_EXPERTS,), jnp.float32), 'ln_beta': jnp.zeros((HEADS * NUM_EXPERTS,), jnp.float32), 'W1': jax.random.normal(ks[4], (NUM_EXPERTS, D, 2 * D), jnp.float32) * s, 'b1': jnp.zeros((NUM_EXPERTS, 2 * D), jnp.float32), 'W2': jax.random.normal(ks[5], (NUM_EXPERTS, 2 * D, D), jnp.float32) * s, 'b2': jnp.zeros((NUM_EXPERTS, D), jnp.float32), 'edge_index': jax.random.randint(ks[6], (2, N_EDGES), 0, B * N, jnp.int32)}
    _L0_ffn_all = _L0_ffn_setup()
    _L0_ffn_in = {k: v for k, v in _L0_ffn_all.items() if k in ('W_gat', 'att_src', 'att_dst', 'b_gat', 'ln_gamma', 'ln_beta', 'W1', 'b1', 'W2', 'b2', 'edge_index')}
    del _L0_ffn_all
    return {'x': x, 'src': src, 'dst': dst, 'L0_gnn_W_l1': _L0_gnn_in['W_l1'], 'L0_gnn_b1': _L0_gnn_in['b1'], 'L0_gnn_W_r1': _L0_gnn_in['W_r1'], 'L0_gnn_W_l2': _L0_gnn_in['W_l2'], 'L0_gnn_b2': _L0_gnn_in['b2'], 'L0_gnn_W_r2': _L0_gnn_in['W_r2'], 'L0_mix_Wqkv': _L0_mix_in['Wqkv'], 'L0_mix_ln1_g': _L0_mix_in['ln1_g'], 'L0_mix_ln1_b': _L0_mix_in['ln1_b'], 'L0_mix_W1': _L0_mix_in['W1'], 'L0_mix_b1': _L0_mix_in['b1'], 'L0_mix_W2': _L0_mix_in['W2'], 'L0_mix_b2': _L0_mix_in['b2'], 'L0_mix_ln2_g': _L0_mix_in['ln2_g'], 'L0_mix_ln2_b': _L0_mix_in['ln2_b'], 'L0_ffn_W_gat': _L0_ffn_in['W_gat'], 'L0_ffn_att_src': _L0_ffn_in['att_src'], 'L0_ffn_att_dst': _L0_ffn_in['att_dst'], 'L0_ffn_b_gat': _L0_ffn_in['b_gat'], 'L0_ffn_ln_gamma': _L0_ffn_in['ln_gamma'], 'L0_ffn_ln_beta': _L0_ffn_in['ln_beta'], 'L0_ffn_W1': _L0_ffn_in['W1'], 'L0_ffn_b1': _L0_ffn_in['b1'], 'L0_ffn_W2': _L0_ffn_in['W2'], 'L0_ffn_b2': _L0_ffn_in['b2'], 'L0_ffn_edge_index': _L0_ffn_in['edge_index']}

def reference(x, src, dst, L0_gnn_W_l1, L0_gnn_b1, L0_gnn_W_r1, L0_gnn_W_l2, L0_gnn_b2, L0_gnn_W_r2, L0_mix_Wqkv, L0_mix_ln1_g, L0_mix_ln1_b, L0_mix_W1, L0_mix_b1, L0_mix_W2, L0_mix_b2, L0_mix_ln2_g, L0_mix_ln2_b, L0_ffn_W_gat, L0_ffn_att_src, L0_ffn_att_dst, L0_ffn_b_gat, L0_ffn_ln_gamma, L0_ffn_ln_beta, L0_ffn_W1, L0_ffn_b1, L0_ffn_W2, L0_ffn_b2, L0_ffn_edge_index):
    import jax
    import jax.numpy as jnp

    def _L0_gnn_ref(x, edge_index, W_l1, b1, W_r1, W_l2, b2, W_r2):
        import jax, jax.numpy as jnp
        import numpy as np
        N_NODES = 12500
        N_EDGES = 400000
        D_IN = 256
        D_HID = 256
        D_OUT = 256

        def _sage_conv(x, src, tgt, W_l, b_l, W_r):
            n = x.shape[0]
            msgs = x[src]
            agg = jax.ops.segment_sum(msgs, tgt, num_segments=n)
            deg = jax.ops.segment_sum(jnp.ones((src.shape[0],), x.dtype), tgt, num_segments=n)
            agg = agg / jnp.maximum(deg, 1.0)[:, None]
            return agg @ W_l + b_l + x @ W_r
        src, tgt = (edge_index[0], edge_index[1])
        h = jax.nn.relu(_sage_conv(x, src, tgt, W_l1, b1, W_r1))
        logits = _sage_conv(h, src, tgt, W_l2, b2, W_r2)
        return logits

    def _L0_mix_ref(x, Wqkv, ln1_g, ln1_b, W1, b1, W2, b2, ln2_g, ln2_b):
        import jax, jax.numpy as jnp
        import numpy as np
        N, F, C, H = (32, 512, 256, 8)
        D = C // H
        EPS_ATTN = 1e-06
        EPS_LN = 1e-05

        def layer_norm(x, g, b):
            mu = jnp.mean(x, axis=-1, keepdims=True)
            var = jnp.var(x, axis=-1, keepdims=True)
            return (x - mu) * jax.lax.rsqrt(var + EPS_LN) * g + b
        n, f, c = x.shape
        qkv = jnp.einsum('nfc,oc->nfo', x, Wqkv)
        q, k, v = jnp.split(qkv, 3, axis=-1)
        q = q.reshape(n, f, H, D)
        k = k.reshape(n, f, H, D)
        v = v.reshape(n, f, H, D)
        q = jax.nn.elu(q) + 1.0
        k = jax.nn.elu(k) + 1.0
        kv = jnp.einsum('nshd,nshm->nhmd', k, v)
        ksum = jnp.sum(k, axis=1)
        z = 1.0 / (jnp.einsum('nlhd,nhd->nlh', q, ksum) + EPS_ATTN)
        t = jnp.einsum('nlhd,nhmd,nlh->nlhm', q, kv, z)
        t = t.reshape(n, f, c)
        x1 = layer_norm(t + x, ln1_g, ln1_b)
        h = jax.nn.gelu(jnp.einsum('nfc,oc->nfo', x1, W1) + b1, approximate=False)
        y = jnp.einsum('nfc,oc->nfo', h, W2) + b2
        return layer_norm(y + x1, ln2_g, ln2_b)

    def _L0_ffn_ref(x, W_gat, att_src, att_dst, b_gat, ln_gamma, ln_beta, W1, b1, W2, b2, edge_index):
        import jax, jax.numpy as jnp
        import numpy as np
        B, N, D = (16, 512, 256)
        NUM_EXPERTS, TOP_K, HEADS = (4, 2, 4)
        N_EDGES = 131072
        LN_EPS = 1e-05

        def _layernorm(x, g, b):
            mu = x.mean(-1, keepdims=True)
            var = ((x - mu) ** 2).mean(-1, keepdims=True)
            return (x - mu) * jax.lax.rsqrt(var + LN_EPS) * g + b

        def _forward(x, edge_index, W_gat, att_src, att_dst, b_gat, ln_gamma, ln_beta, W1, b1, W2, b2):
            Bc, Nc, Dc = x.shape
            M = Bc * Nc
            x_flat = x.reshape(M, Dc)
            h = (x_flat @ W_gat).reshape(M, HEADS, NUM_EXPERTS)
            loops = jnp.arange(M, dtype=edge_index.dtype)
            src = jnp.concatenate([edge_index[0], loops])
            dst = jnp.concatenate([edge_index[1], loops])
            a_src = (h * att_src).sum(-1)
            a_dst = (h * att_dst).sum(-1)
            e = jax.nn.leaky_relu(a_src[src] + a_dst[dst], negative_slope=0.2)
            e_max = jax.ops.segment_max(e, dst, num_segments=M)
            ee = jnp.exp(e - e_max[dst])
            denom = jax.ops.segment_sum(ee, dst, num_segments=M)
            alpha = ee / (denom[dst] + 1e-16)
            msg = h[src] * alpha[:, :, None]
            agg = jax.ops.segment_sum(msg, dst, num_segments=M).reshape(M, HEADS * NUM_EXPERTS) + b_gat
            scores = _layernorm(agg, ln_gamma, ln_beta).reshape(M, HEADS, NUM_EXPERTS).mean(1)
            scores = scores.reshape(Bc, Nc, NUM_EXPERTS)
            topk_s, topk_i = jax.lax.top_k(scores, TOP_K)
            w = jax.nn.softmax(topk_s, axis=-1)
            out = jnp.zeros_like(x)
            for ei in range(NUM_EXPERTS):
                g = jnp.where(topk_i == ei, w, 0.0).sum(-1)
                hh = jax.nn.gelu(x @ W1[ei] + b1[ei], approximate=False)
                out = out + g[..., None] * (hh @ W2[ei] + b2[ei])
            return out
        return _forward(x, edge_index, W_gat, att_src, att_dst, b_gat, ln_gamma, ln_beta, W1, b1, W2, b2)
    edge_index = jnp.stack([src, dst])
    xn = _layernorm(x, axis=-1)
    x = x + _L0_gnn_ref(xn, edge_index, L0_gnn_W_l1, L0_gnn_b1, L0_gnn_W_r1, L0_gnn_W_l2, L0_gnn_b2, L0_gnn_W_r2) + _L0_mix_ref(xn[None], L0_mix_Wqkv, L0_mix_ln1_g, L0_mix_ln1_b, L0_mix_W1, L0_mix_b1, L0_mix_W2, L0_mix_b2, L0_mix_ln2_g, L0_mix_ln2_b)[0]
    x = x + _L0_ffn_ref(_layernorm(x, axis=-1)[None], L0_ffn_W_gat, L0_ffn_att_src, L0_ffn_att_dst, L0_ffn_b_gat, L0_ffn_ln_gamma, L0_ffn_ln_beta, L0_ffn_W1, L0_ffn_b1, L0_ffn_W2, L0_ffn_b2, L0_ffn_edge_index)[0]
    return x

_drawn_inputs = setup_inputs


def setup_inputs(seed=0):
    import zlib

    import numpy as np

    out = dict(_drawn_inputs(seed))
    spreads = {'L0_gnn_b1': (0.0, 0.1),
     'L0_gnn_b2': (0.0, 0.1),
     'L0_mix_ln1_g': (1.0, 0.2),
     'L0_mix_ln1_b': (0.0, 0.1),
     'L0_mix_ln2_g': (1.0, 0.2),
     'L0_mix_ln2_b': (0.0, 0.1),
     'L0_ffn_b_gat': (0.0, 0.1),
     'L0_ffn_ln_gamma': (1.0, 0.2),
     'L0_ffn_ln_beta': (0.0, 0.1),
     'L0_ffn_b1': (0.0, 0.306),
     'L0_ffn_b2': (0.0, 0.1)}
    factors = {'L0_mix_Wqkv': 4.509, 'L0_mix_b1': 6.398, 'L0_ffn_att_src': 2.686, 'L0_ffn_att_dst': 4.324}
    for name, (base, spread) in spreads.items():
        noise = np.random.default_rng([zlib.crc32(name.encode()), seed]).standard_normal(out[name].shape)
        drawn = base * np.exp(spread * noise) if base else spread * noise
        out[name] = jnp.asarray(drawn.astype(out[name].dtype))
    for name, factor in factors.items():
        out[name] = (out[name] * factor).astype(out[name].dtype)
    return out
```

```python
from contextlib import ExitStack

import concourse.bass as bass
import numpy as np
from concourse import mybir

F32 = mybir.dt.float32
BF16 = mybir.dt.bfloat16
I32 = mybir.dt.int32
ALU = mybir.AluOpType
ACT = mybir.ActivationFunctionType
AX = mybir.AxisListType

P = 128
D = 256
N = 12500
T = -(-N // P)
NP = T * P
GE = 212500
RING = 32
GRP = 8
NG = RING // GRP
GC = -(-GE // P // RING) * RING
FE = 131072
FC = FE // P
HB = 12
RB = 4
RB1, RB2 = 2, 1
FCP = T * HB
L = 40
TW = 20
H, DH = 8, 32
E, EH = 4, 4
FH = 512
EPS = 1e-5
NO_NODE = 128 * 127
CHUNK_W = 3 * D

CONST = {}


def shape_constants():
    p = np.arange(P)[:, None]
    f = np.arange(P)[None, :]
    parts = {
        "iota": np.broadcast_to(f, (P, P)),
        "ident": (p == f),
        "before": (p < f),
        "ones": np.ones((P, P)),
        "wbase": np.broadcast_to(-128 * np.arange(T + 1)[None, :], (P, T + 1)),
        "wend": 128 * (p + 1),
        "real": (np.arange(T)[None, :] * P + p) < N,
        "kvmask": np.concatenate([(p // DH == f // DH), (p // DH == np.arange(4)[None, :])], 1),
        "rankmask": np.concatenate([(np.arange(RB * P)[None, :] < k * P + p) for k in range(RB)], 1),
        "slot": np.broadcast_to(np.arange(L)[None, :], (P, L)),
        "eps": np.full((P, 1), EPS),
    }
    at = 0
    for k, v in parts.items():
        CONST[k] = (at, v.shape[1])
        at += v.shape[1]
    return np.ascontiguousarray(np.concatenate([v.astype(np.float32) for v in parts.values()], 1))


ROWS = {}


def row_layout(sizes):
    at = 0
    for k, n in sizes:
        ROWS[k] = (at, n)
        at += n
    return at


ROW_SIZES = [("gnn_b1", D), ("gnn_b2", D), ("ln1_g", D), ("ln1_b", D), ("mix_b2", D), ("ln2_g", D), ("ln2_b", D),
             ("att_src", 16), ("att_dst", 16), ("b_gat", 16), ("gamma", 16), ("beta", 16), ("ffn_b2", E * D)]
NROW = row_layout(ROW_SIZES)


class Step:

    def __init__(self, sem, unit=1, ahead=1):
        self.sem, self.unit, self.ahead = sem, unit, ahead

    def start(self, eng):
        assert self.ahead
        eng.sem_inc(self.sem, self.unit)

    def done(self, t):
        return self.sem, (t + 1 + self.ahead) * self.unit

    def before(self, t):
        assert self.ahead
        return self.sem, (t + 1) * self.unit


def flat(ap):
    return ap.rearrange("p a b -> p (a b)")


def build(nc, io, out, kinds, upto=9):
    ctx = ExitStack()
    with ctx:
        def scratch(name, shape, dt):
            return nc.dram_tensor(name, shape, dt, kind=kinds).ap()

        in_use = []

        def sem(name):
            in_use.append(nc.alloc_semaphore(name))
            return in_use[-1]

        def clear_semaphores():
            nc.clear_and_free_semaphores(list(in_use))
            nc.all_engine_barrier()
            in_use.clear()

        def steps(prefix, names, unit=1):
            return {n: Step(sem(f"{prefix}_{n}"), unit) for n in names}

        def sbuf(stack, name, shape, dt):
            return stack.enter_context(nc.sbuf_tensor(name, shape, dt))

        def psum(stack, name, dt=F32):
            return stack.enter_context(nc.psum_tensor(name, [P, 512 if dt == F32 else 1024], dt))

        table = [scratch(f"split_rows{i}", (NP, CHUNK_W), BF16) for i in range(2)]
        own = [scratch(f"own_rows{i}", (NP, D), F32) for i in range(2)]
        qT_d = scratch("q_transposed", (T, P, 2 * P), F32)
        x2_d = scratch("x_second", (NP, D), F32)
        x2nT_d = scratch("x_second_norm_transposed", (T, P, 2 * P), F32)
        heads_d = scratch("attention_rows", (NP, TW), F32)
        sorted_d = scratch("sorted_edge_rows", (FE + 2 * P, TW), F32)
        experts_d = scratch("expert_rows", (T, P, E * D), F32)
        windows_d = scratch("window_ends", (T + 2, 1), I32)
        degrees_d = scratch("largest_degrees", (T, 1), I32)

        const = sbuf(ctx, "const", [P, io["consts"].shape[1]], F32)
        rows = sbuf(ctx, "rows", [P, NROW], F32)
        ident16 = sbuf(ctx, "ident16", [P, P], BF16)
        ones16 = sbuf(ctx, "ones16", [P, 1], BF16)
        zeros16 = sbuf(ctx, "zeros16", [P, 512], BF16)
        wtab = sbuf(ctx, "wtab", [1, T + 2], I32)
        dtab = sbuf(ctx, "dtab", [1, T], I32)
        deg = sbuf(ctx, "deg", [P, T], F32)
        first = sbuf(ctx, "first", [P, T + 2], F32)
        trow = sbuf(ctx, "trow", [P, T, TW], F32)
        adst = sbuf(ctx, "adst", [P, T, EH], F32)
        pos = sbuf(ctx, "pos", [P, T * RB * (RB1 + RB2)], I32)

        def c(name):
            at, n = CONST[name]
            return const[:, at:at + n]

        def r(name):
            at, n = ROWS[name]
            return rows[:, at:at + n]

        load = sem("load")
        setup = sem("setup")

        early = ctx.enter_context(ExitStack())
        rstd = sbuf(early, "rstd", [P, T], F32)
        nmr = sbuf(early, "nmr", [P, T], F32)
        xs = sbuf(early, "xs", [P, D], F32)
        gdst = sbuf(early, "gdst", [P, GC], F32)
        flo = sbuf(early, "flo", [P, FCP], F32)
        fhi = sbuf(early, "fhi", [P, FCP], F32)
        fdst = sbuf(early, "fdst", [P, FCP], F32)
        wlr2 = sbuf(early, "wlr2", [P, 2, 2 * D], F32)
        kvbd = sbuf(early, "kvbd", [P, 2, P + 4], F32)
        bAGG = psum(early, "bAGG")
        bT = psum(early, "bT")
        bMM = psum(early, "bMM")
        bQ = psum(early, "bQ")
        bKV = psum(early, "bKV")
        bC = psum(early, "bC")
        bP = psum(early, "bP")
        bOT = psum(early, "bOT", BF16)

        with ExitStack() as a:
            X = sbuf(a, "X", [P, T, D], F32)
            wlr1 = sbuf(a, "wlr1", [P, 2, 2 * D], F32)
            stat = sbuf(a, "stat", [P, T, 6], F32)
            mean = sbuf(a, "mean", [P, T], F32)
            var = sbuf(a, "var", [P, T], F32)
            tmp = sbuf(a, "tmp", [P, T], F32)
            xT = sbuf(a, "xT", [P, 2, P], F32)
            uf = sbuf(a, "uf", [P, D], F32)
            ur = sbuf(a, "ur", [P, D], F32)
            us = sbuf(a, "us", [P, 3, D], BF16)
            rs = sbuf(a, "rs", [P, D], F32)
            Olo = sbuf(a, "Olo", [P, HB, P], BF16)
            Ohi = sbuf(a, "Ohi", [P, HB, T], BF16)
            sc = [sbuf(a, f"scan{i}", [P, T], F32) for i in range(2)]
            part = sbuf(a, "part", [P, T], F32)
            lastd = sbuf(a, "lastd", [T, GC], F32)
            idst, ifd, ilo, ihi, lasti = (v[:].bitcast(I32) for v in (gdst, fdst, flo, fhi, lastd))
            cef = sbuf(a, "cef", [T, 1], F32)
            cei = sbuf(a, "cei", [T, 1], I32)
            mdi = sbuf(a, "mdi", [T, 1], I32)
            zi = sbuf(a, "zi", [1, 1], I32)

            s_x = sem("a_x")
            s_idx = sem("a_idx")
            chain = sem("a_chain")
            s_std = sem("a_std")
            s_bn = sem("a_bn")
            A = steps("a", ["xn", "xnT", "xTs", "ur", "uev", "rev", "split", "onehot", "hist", "p1", "p2", "p3"])
            AD = steps("a", ["stU", "stR"], 16)
            s_pre = sem("a_prefix")
            s_tr = sem("a_degT")
            s_out = sem("a_tables")
            s_ready = sem("a_ready")
            with nc.Block() as block:
                @block.sync
                def _(sp):
                    for s in AD.values():
                        s.start(sp)
                    sp.dma_start(const[:], io["consts"]).then_inc(load, 16)
                    x_v = io["x"].rearrange("(t p) d -> p t d", p=P)
                    for k in range(7):
                        n = T // 7
                        sp.dma_start(X[:, k * n:(k + 1) * n, :], x_v[:, k * n:(k + 1) * n, :]).then_inc(s_x, 16)
                    sp.dma_start(idst, io["gnn_dst"]).then_inc(s_idx, 16)
                    sp.dma_start(ifd, io["ffn_dst"]).then_inc(s_idx, 16)
                    sp.dma_start(lasti, io["gnn_dst"][P - 1:P, :].partition_broadcast(T)).then_inc(s_idx, 16)
                    sp.dma_start(wlr1[:], io["wlr1"]).then_inc(load, 16)
                    sp.dma_start(wlr2[:], io["wlr2"]).then_inc(load, 16)
                    sp.dma_start(rows[:], io["rows"].partition_broadcast(P)).then_inc(load, 16)
                    with sp.Fori(0, T) as t:
                        sp.wait_ge(*A["split"].done(t))
                        sp.dma_start(table[0].rearrange("(t p) d -> t p d", p=P)[bass.ds(t, 1)].rearrange("t p d -> (t p) d"), flat(us[:])).then_inc(AD["stU"].sem, 16)
                        sp.wait_ge(*A["rev"].done(t))
                        sp.dma_start(own[0].rearrange("(t p) d -> t p d", p=P)[bass.ds(t, 1)].rearrange("t p d -> (t p) d"), rs[:]).then_inc(AD["stR"].sem, 16)
                    sp.wait_ge(s_ready, 2)
                    sp.dma_start(windows_d[0:1, :], zi[:]).then_inc(s_out, 16)
                    sp.dma_start(windows_d[1:T + 1, :], cei[:]).then_inc(s_out, 16)
                    sp.dma_start(windows_d[T + 1:T + 2, :], cei[T - 1:T, :]).then_inc(s_out, 16)
                    sp.dma_start(degrees_d[:, :], mdi[:]).then_inc(s_out, 16)
                    sp.wait_ge(s_out, 64)
                    sp.dma_start(wtab[:], windows_d.rearrange("t o -> o t")).then_inc(s_out, 16)
                    sp.dma_start(dtab[:], degrees_d.rearrange("t o -> o t")).then_inc(s_out, 16)
                    sp.wait_ge(s_out, 96)
                    for s in AD.values():
                        sp.wait_ge(s.sem, (T + 1) * 16)

                @block.gpsimd
                def _(pool):
                    for s in ("split", "p1", "p2", "p3"):
                        A[s].start(pool)
                    with pool.Fori(0, T) as t:
                        pool.wait_ge(*A["uev"].done(t))
                        pool.wait_ge(*AD["stU"].before(t))
                        pool.sem_inc(setup, 1)
                        pool.tensor_copy(us[:, 0, :], uf[:]).then_inc(A["p1"].sem, 1)
                        pool.wait_ge(*A["p1"].done(t))
                        pool.tensor_tensor(ur[:], uf[:], us[:, 0, :], ALU.subtract).then_inc(A["p2"].sem, 1)
                        pool.wait_ge(*A["p2"].done(t))
                        pool.sem_inc(setup, 1)
                        pool.tensor_copy(us[:, 1, :], ur[:]).then_inc(A["p3"].sem, 1)
                        pool.wait_ge(*A["p3"].done(t))
                        pool.tensor_tensor(us[:, 2, :], ur[:], us[:, 1, :], ALU.subtract).then_inc(A["split"].sem, 1)

                @block.scalar
                def _(act):
                    for s in ("xn", "xTs"):
                        A[s].start(act)
                    act.wait_ge(load, 64)
                    act.activation(ident16[:], c("ident"), ACT.Copy).then_inc(setup, 1)
                    act.wait_ge(chain, 4)
                    act.activation(tmp[:], var[:], ACT.Sqrt, bias=c("eps")).then_inc(s_std, 1)
                    act.wait_ge(chain, 6)
                    with act.Fori(0, T) as t:
                        act.wait_ge(*A["xnT"].before(t))
                        act.activation(xs[:], flat(X[:, bass.ds(t, 1), :]), ACT.Identity, bias=nmr[:, bass.ds(t, 1)],
                                       scale=rstd[:, bass.ds(t, 1)]).then_inc(A["xn"].sem, 1)
                        act.wait_ge(*A["xnT"].done(t))
                        act.wait_ge(*A["ur"].before(t))
                        act.activation(flat(xT[:]), bT[:, 0:D], ACT.Copy).then_inc(A["xTs"].sem, 1)

                @block.tensor
                def _(pe):
                    for s in ("xnT", "ur", "hist"):
                        A[s].start(pe)
                    pe.wait_ge(load, 64)
                    pe.wait_ge(setup, 1)
                    pe.wait_ge(s_idx, 49)
                    pe.matmul(bC[:, 0:T], zeros16[:, 0:P], zeros16[:, 0:T], start=True, stop=False, skip_group_check=True)
                    with pe.Fori(0, T) as t:
                        pe.wait_ge(*A["xn"].done(t))
                        pe.wait_ge(*A["xTs"].before(t))
                        for j in range(2):
                            last = pe.transpose(bT[:, j * P:(j + 1) * P],
                                                xs[:, j * P:(j + 1) * P],
                                                c("ident"))
                        last.then_inc(A["xnT"].sem, 1)
                        pe.wait_ge(*A["onehot"].done(t))
                        for k in range(HB):
                            last = pe.matmul(bC[:, 0:T], Olo[:, k, :], Ohi[:, k, :], start=False, stop=False, skip_group_check=True)
                        last.then_inc(A["hist"].sem, 1)
                        pe.wait_ge(*A["xTs"].done(t))
                        pe.wait_ge(*A["rev"].before(t))
                        for j in range(2):
                            last = pe.matmul(bMM[:], xT[:, j, :], wlr1[:, j, :], start=(j == 0), stop=(j == 1))
                        last.then_inc(A["ur"].sem, 1)
                    pe.wait_ge(s_pre, 1)
                    pe.matmul(bP[:, 0:T], c("before"), deg[:], start=True, stop=True)
                    pe.matmul(bP[:, T:2 * T], c("ones"), deg[:], start=True, stop=True)
                    pe.transpose(bQ[0:T, 0:P], deg[:], c("ident")).then_inc(s_tr, 1)

                @block.vector
                def _(dve):
                    for s in ("uev", "rev", "onehot"):
                        A[s].start(dve)
                    n = [0]

                    def link(ins):
                        n[0] += 1
                        ins.then_inc(chain, 1)
                        dve.wait_ge(chain, n[0])
                    dve.memset(zeros16[:], 0.0)
                    dve.memset(ones16[:], 1.0)
                    dve.memset(zi[:], 0).then_inc(s_idx, 1)
                    dve.wait_ge(s_x, 7 * 16)
                    with dve.Fori(0, T) as t:
                        dve.bn_stats(flat(stat[:, bass.ds(t, 1), :]), flat(X[:, bass.ds(t, 1), :])).then_inc(s_bn, 1)
                    dve.wait_ge(s_bn, T)
                    link(dve.tensor_tensor(mean[:], stat[:, :, 1], stat[:, :, 4], ALU.add))
                    dve.tensor_tensor(tmp[:], stat[:, :, 1], stat[:, :, 4], ALU.subtract)
                    link(dve.tensor_tensor(var[:], stat[:, :, 2], stat[:, :, 5], ALU.add))
                    link(dve.scalar_tensor_tensor(tmp[:], tmp[:], 0.25, tmp[:], ALU.mult, ALU.mult))
                    link(dve.scalar_tensor_tensor(var[:], var[:], 1.0 / D, tmp[:], ALU.mult, ALU.add))
                    dve.wait_ge(s_std, 1)
                    link(dve.reciprocal(rstd[:], tmp[:]))
                    link(dve.scalar_tensor_tensor(nmr[:], mean[:], -0.5, rstd[:], ALU.mult, ALU.mult))
                    dve.wait_ge(s_idx, 49)
                    dve.tensor_copy(gdst[:], idst)
                    dve.tensor_copy(lastd[:], lasti)
                    dve.tensor_scalar(ilo, ifd, 127, None, ALU.bitwise_and)
                    link(dve.tensor_scalar(ihi, ifd, 7, None, ALU.logical_shift_right))
                    dve.tensor_copy(fdst[:], ifd)
                    dve.tensor_copy(flo[:], ilo)
                    link(dve.tensor_copy(fhi[:], ihi))
                    dve.wait_ge(load, 64)
                    link(dve.tensor_scalar(lastd[:], lastd[:], c("wend")[0:T], None, ALU.is_lt, ALU.add, accum_out=cef[:]))
                    dve.tensor_copy(cei[:], cef[:]).then_inc(s_ready, 1)
                    with dve.Fori(0, T) as t:
                        dve.wait_ge(*A["hist"].before(t))
                        dve.tensor_tensor(Olo[:], c("iota").unsqueeze(1).broadcast_to([P, HB, P]),
                                          flo[:, bass.ds(t * HB, HB)].unsqueeze(2).broadcast_to([P, HB, P]), ALU.is_equal)
                        dve.tensor_tensor(Ohi[:], c("iota")[:, 0:T].unsqueeze(1).broadcast_to([P, HB, T]),
                                          fhi[:, bass.ds(t * HB, HB)].unsqueeze(2).broadcast_to([P, HB, T]), ALU.is_equal)\
                           .then_inc(A["onehot"].sem, 1)
                        dve.wait_ge(*A["ur"].done(t))
                        dve.wait_ge(*A["split"].before(t))
                        dve.tensor_copy(uf[:], bMM[:, 0:D]).then_inc(A["uev"].sem, 1)
                        dve.wait_ge(*AD["stR"].before(t))
                        dve.tensor_tensor(rs[:], bMM[:, D:2 * D], r("gnn_b1"), ALU.add).then_inc(A["rev"].sem, 1)
                    dve.wait_ge(A["hist"].sem, T + 1)
                    dve.tensor_copy(deg[:], bC[:, 0:T]).then_inc(s_pre, 1)
                    dve.wait_ge(s_tr, 1)
                    dve.tensor_reduce(mdi[:], bQ[0:T, 0:P], AX.X, ALU.max).then_inc(s_ready, 1)
                    link(dve.memset(sc[0][:, 0:1], 0.0))
                    link(dve.tensor_copy(sc[0][:, 1:T], bP[:, T:2 * T - 1]))
                    link(dve.tensor_copy(part[:], bP[:, 0:T]))
                    a_, b_ = sc
                    k = 1
                    while k < T:
                        dve.tensor_copy(b_[:, 0:k], a_[:, 0:k])
                        link(dve.tensor_tensor(b_[:, k:T], a_[:, k:T], a_[:, 0:T - k], ALU.add))
                        a_, b_ = b_, a_
                        k *= 2
                    dve.memset(first[:, T:T + 2], 0.0)
                    link(dve.tensor_tensor(first[:, 0:T], part[:], a_[:], ALU.add))
        clear_semaphores()
        if upto <= 1:
            return

        ohring = 24

        def gather_pool(pool, G, tab, stop=GC // RING):
            with pool.Fori(0, stop) as i:
                for g in range(NG):
                    pool.wait_ge(G["staged"][g], (i + 1) * 16)
                    pool.wait_ge(G["ringfree"], i * RING + GRP * (g + 1))
                    pool.sem_inc(G["go"], 1)
                    for k in range(GRP):
                        pool.indirect_dma_start(
                            out=G["ring"][:, (g * GRP + k) * CHUNK_W:(g * GRP + k + 1) * CHUNK_W], out_offset=None,
                            in_=tab, in_offset=bass.IndirectOffsetOnAxis(ap=G["idx"][g][:, k:k + 1], axis=0))\
                            .then_inc(G["landed"][g], 16)

        def gather_sync(sp, G):
            for g in range(NG):
                sp.dma_start(G["idx"][g][:], io["gnn_src"][g]).then_inc(G["staged"][g], 16)
            with sp.Fori(0, GC // RING) as i:
                for g in range(NG):
                    sp.wait_ge(G["landed"][g], (i + 1) * GRP * 16)
                    sp.sem_inc(G["have"], GRP)
                    sp.dma_start(G["idx"][g][:], io["gnn_src"][bass.ds((i + 1) * NG + g, 1)].rearrange("g p k -> (g p) k"))\
                        .then_inc(G["staged"][g], 16)
            for g in range(NG):
                sp.wait_ge(G["staged"][g], (GC // RING + 1) * 16)

        def onehots(dve, G, w):
            cs = dve.value_load(wtab[0:1, bass.ds(w, 1)], min_val=0, max_val=GC - 1)
            ce = dve.value_load(wtab[0:1, bass.ds(w + 1, 1)], min_val=0, max_val=GC - 1)
            with dve.Fori(cs, ce + 1) as ch:
                dve.wait_ge(G["pairs"], ch + w + 1)
                dve.tensor_scalar(G["oh"][:, bass.ds(((ch + w) % ohring) * P, P)], c("iota"),
                                  gdst[:, bass.ds(ch, 1)], c("wbase")[:, bass.ds(w, 1)],
                                  ALU.subtract, ALU.is_equal).then_inc(G["onehot"], 1)

        def aggregate(pe, G, w):
            def pair(ch, frees):
                k = ch + w
                pe.wait_ge(G["onehot"], k + 1)
                pe.wait_ge(G["have"], ch + 1)
                hot = G["oh"][:, bass.ds((k % ohring) * P, P)]
                at = (ch % RING) * CHUNK_W
                for j in range(3):
                    last = pe.matmul(bAGG[:, 0:D], hot, G["ring"][:, bass.ds(at + j * D, D)], start=False, stop=False, skip_group_check=True)
                if frees:
                    last.then_inc(G["ringfree"], 1)
                pe.matmul(bAGG[:, D:D + 1], hot, ones16[:], start=False, stop=False, skip_group_check=True)\
                    .then_inc(G["pairs"], 1)
            pe.wait_ge(*G["evict"].before(w))
            pe.matmul(bAGG[:, 0:D + 1], zeros16[:, 0:P], zeros16[:, 0:D + 1], start=True, stop=False, skip_group_check=True)
            cs = pe.value_load(wtab[0:1, bass.ds(w, 1)], min_val=0, max_val=GC - 1)
            ce = pe.value_load(wtab[0:1, bass.ds(w + 1, 1)], min_val=0, max_val=GC - 1)
            pair(cs, False)
            with pe.If(cs < ce):
                with pe.Fori(cs + 1, ce + 1) as ch:
                    pair(ch, True)
            pe.matmul(bAGG[:, D:D + 1], zeros16[:, 0:P], zeros16[:, 0:1], start=False, stop=True, skip_group_check=True)\
                .then_inc(G["sum"].sem, 1)

        def gather_state(stack, prefix):
            G = {"ring": sbuf(stack, f"{prefix}ring", [P, RING * CHUNK_W], BF16),
                 "oh": sbuf(stack, f"{prefix}oh", [P, ohring * P], BF16),
                 "idx": [sbuf(stack, f"{prefix}idx{g}", [P, GRP], I32) for g in range(NG)],
                 "staged": [sem(f"{prefix}staged{g}") for g in range(NG)],
                 "landed": [sem(f"{prefix}landed{g}") for g in range(NG)]}
            for n in ("ringfree", "have", "pairs", "onehot", "go"):
                G[n] = sem(f"{prefix}{n}")
            G["sum"] = Step(sem(f"{prefix}sum"))
            return G

        def rank_state(stack, prefix, n):
            R = {"n": n, "count": sbuf(stack, f"{prefix}count", [P, T], F32)}
            R["b"] = [dict(
                lo=sbuf(stack, f"{prefix}lo{b}", [P, RB, P], BF16), hi=sbuf(stack, f"{prefix}hi{b}", [P, RB, T], BF16),
                loT=sbuf(stack, f"{prefix}loT{b}", [P, RB * P], F32), row=sbuf(stack, f"{prefix}row{b}", [P, RB * P], I32),
                near=sbuf(stack, f"{prefix}near{b}", [P, RB], F32), far=sbuf(stack, f"{prefix}far{b}", [P, RB], F32),
                prod=sbuf(stack, f"{prefix}prod{b}", [P, RB, T], F32), eq=sbuf(stack, f"{prefix}eq{b}", [P, RB * (RB + 1) // 2 * P], BF16),
                s=steps(f"{prefix}rank{b}", ["hot", "count", "turned", "loT", "far", "counted", "prod", "farsum", "near", "pos"]),
                row_in=Step(sem(f"{prefix}row_in{b}"), 16)) for b in range(n)]
            return R

        def rank_start(eng, R, names):
            for B in R["b"]:
                for nme in names:
                    B["s"][nme].start(eng)

        def rank_hot(dve, R, b, w, batch):
            B, s = R["b"][b], R["b"][b]["s"]
            prev = R["b"][b - 1]["s"]["counted"].done(w) if b else R["b"][-1]["s"]["counted"].before(w)
            dve.wait_ge(*s["counted"].before(w))
            dve.tensor_tensor(B["lo"][:], c("iota").unsqueeze(1).broadcast_to([P, RB, P]),
                              flo[:, bass.ds(batch * RB, RB)].unsqueeze(2).broadcast_to([P, RB, P]), ALU.is_equal)
            dve.tensor_tensor(B["hi"][:], c("iota")[:, 0:T].unsqueeze(1).broadcast_to([P, RB, T]),
                              fhi[:, bass.ds(batch * RB, RB)].unsqueeze(2).broadcast_to([P, RB, T]), ALU.is_equal)\
               .then_inc(s["hot"].sem, 1)
            dve.wait_ge(*prev)
            dve.tensor_tensor(R["count"][:], bC[:, 0:T], first[:, 0:T], ALU.add).then_inc(s["count"].sem, 1)

        def rank_turn(pe, R, b, w):
            B, s = R["b"][b], R["b"][b]["s"]
            pe.wait_ge(*s["hot"].done(w))
            pe.wait_ge(*(R["b"][b - 1]["s"]["loT"].done(w) if b else R["b"][-1]["s"]["loT"].before(w)))
            for k in range(RB):
                last = pe.transpose(bOT[:, k * P:(k + 1) * P], B["lo"][:, k, :], ident16[:])
            last.then_inc(s["turned"].sem, 1)

        def rank_turned(act, R, b, w):
            B, s = R["b"][b], R["b"][b]["s"]
            act.wait_ge(*s["turned"].done(w))
            act.wait_ge(*s["far"].before(w))
            act.activation(B["loT"][:], bOT[:, 0:RB * P], ACT.Copy).then_inc(s["loT"].sem, 1)

        def rank_count(pe, R, b, w):
            B, s = R["b"][b], R["b"][b]["s"]
            pe.wait_ge(*s["loT"].done(w))
            pe.wait_ge(*s["count"].done(w))
            pe.wait_ge(*(R["b"][b - 1]["s"]["prod"].done(w) if b else R["b"][-1]["s"]["prod"].before(w)))
            for k in range(RB):
                last = pe.matmul(bP[:, k * T:(k + 1) * T], B["loT"][:, k * P:(k + 1) * P], R["count"][:], start=True, stop=True, skip_group_check=True)
            last.then_inc(s["far"].sem, 1)
            for k in range(RB):
                last = pe.matmul(bC[:, 0:T], B["lo"][:, k, :], B["hi"][:, k, :], start=False, stop=False, skip_group_check=True)
            last.then_inc(s["counted"].sem, 1)

        def rank_near(dve, R, b, w, batch):
            B, s = R["b"][b], R["b"][b]["s"]
            dve.wait_ge(*B["row_in"].done(w))
            dve.wait_ge(*s["pos"].before(w))
            for k in range(RB):
                n = (k + 1) * P
                at = k * (k + 1) // 2 * P
                last = dve.scalar_tensor_tensor(B["eq"][:, at:at + n], B["row"][:, 0:n], fdst[:, bass.ds(batch * RB + k, 1)],
                                                c("rankmask")[:, k * RB * P:k * RB * P + n], ALU.is_equal, ALU.mult,
                                                accum_out=B["near"][:, k:k + 1])
            last.then_inc(s["near"].sem, 1)

        def rank_place(dve, R, b, w, batch):
            B, s = R["b"][b], R["b"][b]["s"]
            dve.wait_ge(*s["far"].done(w))
            dve.tensor_tensor(flat(B["prod"][:]), bP[:, 0:RB * T], flat(B["hi"][:]), ALU.mult).then_inc(s["prod"].sem, 1)
            dve.wait_ge(*s["prod"].done(w))
            dve.tensor_reduce(B["far"][:], B["prod"][:], AX.X, ALU.add).then_inc(s["farsum"].sem, 1)
            dve.wait_ge(*s["farsum"].done(w))
            dve.wait_ge(*s["near"].done(w))
            dve.tensor_tensor(pos[:, bass.ds(batch * RB, RB)], B["near"][:], B["far"][:], ALU.add).then_inc(s["pos"].sem, 1)

        def rank_load(act, R, b, w, batch):
            B, s = R["b"][b], R["b"][b]["s"]
            act.wait_ge(*s["near"].before(w))
            act.dma_start(B["row"][:], io["ffn_dst_rows"][0:1, bass.ds(batch * RB * P, RB * P)].partition_broadcast(P))\
                .then_inc(B["row_in"].sem, 16)

        DVE_RANK = ("hot", "count", "prod", "farsum", "near", "pos")
        PE_RANK = ("turned", "far", "counted")

        def tile_rows(ap, w):
            return ap.rearrange("(t p) d -> t p d", p=P)[bass.ds(w, 1)].rearrange("t p d -> (t p) d")

        with ExitStack() as b:
            G = gather_state(b, "b_")
            R = rank_state(b, "b_", RB1)
            wkv = sbuf(b, "wkv", [P, 2, 2 * D], F32)
            wq = sbuf(b, "wq", [P, 2, D], F32)
            xw = sbuf(b, "xw", [P, D], F32)
            xT = sbuf(b, "xT_b", [P, 2 * P], F32)
            r1 = sbuf(b, "r1", [P, D], F32)
            dg = sbuf(b, "dg", [P, 1], F32)
            rinv = sbuf(b, "rinv", [P, 1], F32)
            h0 = sbuf(b, "h0", [P, D], F32)
            hh = sbuf(b, "hh", [P, D], F32)
            hT = sbuf(b, "hT", [P, 2 * P], F32)
            km = sbuf(b, "km", [P, D], F32)
            ke = sbuf(b, "ke", [P, D], F32)
            kf = sbuf(b, "kf", [P, D], F32)
            vx = sbuf(b, "vx", [P, 2, P + 1], F32)
            qm = sbuf(b, "qm", [P, D], F32)
            qe = sbuf(b, "qe", [P, D], F32)
            qf = sbuf(b, "qf", [P, D], F32)
            uf = sbuf(b, "uf_b", [P, D], F32)
            ur = sbuf(b, "ur_b", [P, D], F32)
            us = sbuf(b, "us_b", [P, 3, D], BF16)
            rs = sbuf(b, "rs_b", [P, D], F32)
            S = steps("b", ["xs", "xTp", "xT", "kv", "q", "km", "qm", "vx", "ke", "qe", "kf", "qf", "KV", "dg", "rinv", "h0", "h",
                            "hTp", "hT", "ur", "uf", "rs", "hi", "r1", "mid", "lo"])
            SD = steps("b", ["inx", "inR", "outq", "outU", "outR"], 16)
            b_load = sem("b_load")
            G["evict"] = S["h0"]
            with nc.Block() as block:
                @block.gpsimd
                def _(pool):
                    gather_pool(pool, G, table[0])

                @block.sync
                def _(sp):
                    sp.dma_start(wkv[:], io["wkv"]).then_inc(b_load, 16)
                    sp.dma_start(wq[:], io["wq"]).then_inc(b_load, 16)
                    gather_sync(sp, G)

                @block.scalar
                def _(act):
                    for n in ("xs", "xT", "ke", "qe", "h", "hT", "hi", "mid"):
                        S[n].start(act)
                    for s in SD.values():
                        s.start(act)
                    for B in R["b"]:
                        B["row_in"].start(act)
                    rank_start(act, R, ("loT",))
                    with act.Fori(0, T) as w:
                        act.wait_ge(*S["xs"].before(w))
                        act.dma_start(xw[:], tile_rows(io["x"], w)).then_inc(SD["inx"].sem, 16)
                        act.wait_ge(*S["h0"].before(w))
                        act.dma_start(r1[:], tile_rows(own[0], w)).then_inc(SD["inR"].sem, 16)
                        for b in range(RB1):
                            rank_load(act, R, b, w, w * RB1 + b)
                        act.wait_ge(*S["xTp"].before(w))
                        act.wait_ge(*SD["inx"].done(w))
                        act.activation(xs[:], xw[:], ACT.Identity, bias=nmr[:, bass.ds(w, 1)],
                                       scale=rstd[:, bass.ds(w, 1)]).then_inc(S["xs"].sem, 1)
                        act.wait_ge(*S["xTp"].done(w))
                        act.wait_ge(*S["q"].before(w))
                        act.activation(xT[:], bT[:, 0:D], ACT.Copy).then_inc(S["xT"].sem, 1)
                        rank_turned(act, R, 0, w)
                        act.wait_ge(*S["km"].done(w))
                        act.activation(ke[:], km[:], ACT.Exp).then_inc(S["ke"].sem, 1)
                        act.wait_ge(*S["qm"].done(w))
                        act.activation(qe[:], qm[:], ACT.Exp).then_inc(S["qe"].sem, 1)
                        act.wait_ge(*S["h0"].done(w))
                        act.activation(hh[:], h0[:], ACT.Relu).then_inc(S["h"].sem, 1)
                        act.wait_ge(*S["hTp"].done(w))
                        act.activation(hT[:], bT[:, 0:D], ACT.Copy).then_inc(S["hT"].sem, 1)
                        rank_turned(act, R, 1, w)
                        act.wait_ge(*S["qf"].done(w))
                        act.dma_start(qT_d[bass.ds(w, 1)].rearrange("t p d -> (t p) d"), qf[:]).then_inc(SD["outq"].sem, 16)
                        act.wait_ge(*S["uf"].done(w))
                        act.wait_ge(*SD["outU"].before(w))
                        act.activation(us[:, 0, :], uf[:], ACT.Copy).then_inc(S["hi"].sem, 1)
                        act.wait_ge(*S["r1"].done(w))
                        act.activation(us[:, 1, :], ur[:], ACT.Copy).then_inc(S["mid"].sem, 1)
                        act.wait_ge(*S["rs"].done(w))
                        act.dma_start(tile_rows(own[1], w), rs[:]).then_inc(SD["outR"].sem, 16)
                        act.wait_ge(*S["mid"].done(w))
                        act.wait_ge(*S["lo"].done(w))
                        act.dma_start(tile_rows(table[1], w), flat(us[:])).then_inc(SD["outU"].sem, 16)
                    for s in SD.values():
                        act.wait_ge(s.sem, (T + 1) * 16)

                @block.tensor
                def _(pe):
                    for n in ("xTp", "kv", "q", "KV", "hTp", "ur"):
                        S[n].start(pe)
                    rank_start(pe, R, ("turned", "far"))
                    R["b"][0]["s"]["counted"].start(pe)
                    G["sum"].start(pe)
                    pe.sem_inc(G["ringfree"], RING)
                    pe.sem_inc(G["pairs"], ohring)
                    pe.wait_ge(b_load, 32)
                    pe.matmul(bC[:, 0:T], zeros16[:, 0:P], zeros16[:, 0:T], start=True, stop=False, skip_group_check=True)\
                        .then_inc(R["b"][-1]["s"]["counted"].sem, 1)
                    pe.matmul(bKV[:, 0:2 * (P + 1)], zeros16[:, 0:P], zeros16[:, 0:2 * (P + 1)], start=True, stop=False, skip_group_check=True)
                    with pe.Fori(0, T) as w:
                        aggregate(pe, G, w)
                        pe.wait_ge(*S["xs"].done(w))
                        pe.wait_ge(*S["hT"].before(w))
                        for j in range(2):
                            last = pe.transpose(bT[:, j * P:(j + 1) * P], xs[:, j * P:(j + 1) * P], c("ident"))
                        last.then_inc(S["xTp"].sem, 1)
                        rank_turn(pe, R, 0, w)
                        pe.wait_ge(*S["xT"].done(w))
                        pe.wait_ge(*S["rs"].before(w))
                        for j in range(2):
                            last = pe.matmul(bMM[:], xT[:, j * P:(j + 1) * P], wkv[:, j, :], start=(j == 0), stop=(j == 1))
                        last.then_inc(S["kv"].sem, 1)
                        pe.wait_ge(*S["qf"].before(w))
                        for o in range(2):
                            for j in range(2):
                                last = pe.matmul(bQ[:, o * P:(o + 1) * P], wq[:, j, o * P:(o + 1) * P],
                                                 xT[:, j * P:(j + 1) * P], start=(j == 0), stop=(j == 1))
                        last.then_inc(S["q"].sem, 1)
                        rank_count(pe, R, 0, w)
                        pe.wait_ge(*S["h"].done(w))
                        for j in range(2):
                            last = pe.transpose(bT[:, j * P:(j + 1) * P], hh[:, j * P:(j + 1) * P], c("ident"))
                        last.then_inc(S["hTp"].sem, 1)
                        rank_turn(pe, R, 1, w)
                        pe.wait_ge(*S["kf"].done(w))
                        for j in range(2):
                            last = pe.matmul(bKV[:, j * (P + 1):(j + 1) * (P + 1)], kf[:, j * P:(j + 1) * P], vx[:, j, :],
                                             start=False, stop=False, skip_group_check=True)
                        last.then_inc(S["KV"].sem, 1)
                        pe.wait_ge(*S["hT"].done(w))
                        for j in range(2):
                            last = pe.matmul(bMM[:], hT[:, j * P:(j + 1) * P], wlr2[:, j, :], start=(j == 0), stop=(j == 1))
                        last.then_inc(S["ur"].sem, 1)
                        rank_count(pe, R, 1, w)

                @block.vector
                def _(dve):
                    for n in ("km", "qm", "vx", "kf", "qf", "dg", "rinv", "h0", "uf", "rs", "r1", "lo"):
                        S[n].start(dve)
                    rank_start(dve, R, DVE_RANK)
                    onehots(dve, G, 0)
                    with dve.Fori(0, T) as w:
                        rank_hot(dve, R, 0, w, w * RB1)
                        dve.wait_ge(*G["sum"].done(w))
                        dve.tensor_scalar(dg[:], bAGG[:, D:D + 1], 1.0, None, ALU.max).then_inc(S["dg"].sem, 1)
                        dve.wait_ge(*S["dg"].done(w))
                        dve.reciprocal(rinv[:], dg[:]).then_inc(S["rinv"].sem, 1)
                        dve.wait_ge(*S["rinv"].done(w))
                        dve.wait_ge(*SD["inR"].done(w))
                        dve.wait_ge(*S["h"].before(w))
                        dve.scalar_tensor_tensor(h0[:], bAGG[:, 0:D], rinv[:], r1[:], ALU.mult, ALU.add).then_inc(S["h0"].sem, 1)
                        dve.wait_ge(*S["kv"].done(w))
                        dve.wait_ge(*S["ke"].before(w))
                        dve.tensor_scalar(km[:], bMM[:, 0:D], 0.0, None, ALU.min).then_inc(S["km"].sem, 1)
                        dve.wait_ge(*S["KV"].before(w))
                        dve.tensor_copy(vx[:, :, 0:P], bMM[:, D:2 * D].rearrange("p (a b) -> p a b", a=2))
                        dve.tensor_copy(vx[:, :, P:P + 1], c("real")[:, bass.ds(w, 1)].unsqueeze(1).broadcast_to([P, 2, 1])).then_inc(S["vx"].sem, 1)
                        dve.wait_ge(*S["q"].done(w))
                        dve.wait_ge(*S["qe"].before(w))
                        dve.tensor_scalar(qm[:], bQ[:, 0:D], 0.0, None, ALU.min).then_inc(S["qm"].sem, 1)
                        rank_hot(dve, R, 1, w, w * RB1 + 1)
                        dve.wait_ge(*S["ke"].done(w))
                        dve.scalar_tensor_tensor(kf[:], bMM[:, 0:D], 0.0, ke[:], ALU.max, ALU.add).then_inc(S["kf"].sem, 1)
                        dve.wait_ge(*S["qe"].done(w))
                        dve.wait_ge(*SD["outq"].before(w))
                        dve.scalar_tensor_tensor(qf[:], bQ[:, 0:D], 0.0, qe[:], ALU.max, ALU.add).then_inc(S["qf"].sem, 1)
                        rank_near(dve, R, 0, w, w * RB1)
                        rank_place(dve, R, 0, w, w * RB1)
                        onehots(dve, G, w + 1)
                        dve.wait_ge(*S["ur"].done(w))
                        dve.wait_ge(*S["hi"].before(w))
                        dve.wait_ge(*S["r1"].before(w))
                        dve.tensor_copy(uf[:], bMM[:, 0:D]).then_inc(S["uf"].sem, 1)
                        dve.wait_ge(*SD["outR"].before(w))
                        dve.tensor_tensor(rs[:], bMM[:, D:2 * D], r("gnn_b2"), ALU.add).then_inc(S["rs"].sem, 1)
                        rank_near(dve, R, 1, w, w * RB1 + 1)
                        dve.wait_ge(*S["hi"].done(w))
                        dve.wait_ge(*S["uf"].done(w))
                        dve.tensor_tensor(ur[:], uf[:], us[:, 0, :], ALU.subtract).then_inc(S["r1"].sem, 1)
                        rank_place(dve, R, 1, w, w * RB1 + 1)
                        dve.wait_ge(*S["mid"].done(w))
                        dve.tensor_tensor(us[:, 2, :], ur[:], us[:, 1, :], ALU.subtract).then_inc(S["lo"].sem, 1)
        clear_semaphores()
        if upto <= 2:
            return

        with ExitStack() as b:
            G = gather_state(b, "c_")
            R = rank_state(b, "c_", RB2)
            w1 = sbuf(b, "w1", [P, 2, D], F32)
            w2 = sbuf(b, "w2", [P, 2, D], F32)
            wg = sbuf(b, "wg", [P, 2, 16], F32)
            mb1 = sbuf(b, "mb1", [P, 2], F32)

            def row_buffer(name, n=D):
                return sbuf(b, name, [P, n], F32)
            xw, r2, qT = row_buffer("xw_c"), row_buffer("r2"), row_buffer("qT")
            dg, rinv, lg, lx = row_buffer("dg_c", 1), row_buffer("rinv_c", 1), row_buffer("lg"), row_buffer("lx")
            den, rden, tz, s1, a1, x1, x1b = (row_buffer("den", 8), row_buffer("rden", 8), row_buffer("tz"), row_buffer("s1"),
                                              row_buffer("a1"), row_buffer("x1"), row_buffer("x1b"))
            x1T, gT, s2, a2, mix = row_buffer("x1T"), row_buffer("gT"), row_buffer("s2"), row_buffer("a2"), row_buffer("mix")
            x2, x2n, x2nT = row_buffer("x2"), row_buffer("x2n"), row_buffer("x2nT")
            LN = [dict(st=row_buffer(f"lnst{i}", 6), mv=row_buffer(f"lnmv{i}", 2), sd=row_buffer(f"lnsd{i}", 1),
                       rs=row_buffer(f"lnrs{i}", 1), s=steps(f"c_ln{i}", ["st", "mv", "sd", "rs"])) for i in range(3)]
            atp = sbuf(b, "atp", [P, T, 16], F32)
            S = steps("c", ["xs", "t", "den", "rden", "tz", "s1", "a1", "x1", "x1b", "x1Tp", "x1T", "h", "g", "y", "s2", "a2", "mix",
                            "dg", "rinv", "lg", "lx", "x2", "x2n", "x2Tp", "x2T", "gat", "gatev"])
            SD = steps("c", ["inx", "inr", "inq", "outx2", "outT"], 16)
            G["evict"] = S["lg"]
            c_load = sem("c_load")
            s_kv = sem("c_kvbd")
            turns = sem("c_turns")
            s_tab = sem("c_table")
            c_out = sem("c_out")

            def norm_stats(dve, i, w, v):
                n = LN[i]
                dve.bn_stats(n["st"][:], v).then_inc(n["s"]["st"].sem, 1)
                dve.wait_ge(*n["s"]["st"].done(w))
                dve.sem_inc(turns, 1)
                dve.bn_aggr(n["mv"][:], n["st"][:]).then_inc(n["s"]["mv"].sem, 1)
                dve.wait_ge(*n["s"]["sd"].done(w))
                dve.reciprocal(n["rs"][:], n["sd"][:]).then_inc(n["s"]["rs"].sem, 1)

            def norm_root(act, i, w):
                n = LN[i]
                act.wait_ge(*n["s"]["mv"].done(w))
                act.activation(n["sd"][:], n["mv"][:, 1:2], ACT.Sqrt, bias=c("eps")).then_inc(n["s"]["sd"].sem, 1)

            with nc.Block() as block:
                @block.gpsimd
                def _(pool):
                    gather_pool(pool, G, table[1])

                @block.sync
                def _(sp):
                    sp.dma_start(w1[:], io["w1"]).then_inc(c_load, 16)
                    sp.dma_start(w2[:], io["w2"]).then_inc(c_load, 16)
                    sp.dma_start(wg[:], io["wgat"]).then_inc(c_load, 16)
                    sp.dma_start(mb1[:], io["mix_b1"]).then_inc(c_load, 16)
                    sp.dma_start(sorted_d[FE:FE + 2 * P, :].rearrange("(p k) d -> p (k d)", p=P),
                                 zeros16[:, 0:4 * TW].bitcast(F32)).then_inc(c_out, 16)
                    gather_sync(sp, G)
                    sp.wait_ge(s_tab, 3)
                    sp.dma_start(heads_d.rearrange("(t p) d -> p t d", p=P), trow[:]).then_inc(c_out, 16)
                    sp.wait_ge(c_out, 32)

                @block.scalar
                def _(act):
                    for n in ("xs", "x1T", "g", "x2T"):
                        S[n].start(act)
                    for s in SD.values():
                        s.start(act)
                    for n in LN:
                        n["s"]["sd"].start(act)
                    for B in R["b"]:
                        B["row_in"].start(act)
                    rank_start(act, R, ("loT",))
                    act.wait_ge(c_load, 64)
                    with act.Fori(0, T) as w:
                        act.wait_ge(*S["t"].before(w))
                        act.dma_start(qT[:], qT_d[bass.ds(w, 1)].rearrange("t p d -> (t p) d")).then_inc(SD["inq"].sem, 16)
                        act.wait_ge(*S["lx"].before(w))
                        act.dma_start(xw[:], tile_rows(io["x"], w)).then_inc(SD["inx"].sem, 16)
                        act.dma_start(r2[:], tile_rows(own[1], w)).then_inc(SD["inr"].sem, 16)
                        rank_load(act, R, 0, w, w + T * RB1)
                        act.wait_ge(*SD["inx"].done(w))
                        act.wait_ge(*S["s1"].before(w))
                        act.activation(xs[:], xw[:], ACT.Identity, bias=nmr[:, bass.ds(w, 1)],
                                       scale=rstd[:, bass.ds(w, 1)]).then_inc(S["xs"].sem, 1)
                        rank_turned(act, R, 0, w)
                        norm_root(act, 0, w)
                        act.wait_ge(*S["x1Tp"].done(w))
                        act.activation(x1T[:], bT[:, 0:D], ACT.Copy).then_inc(S["x1T"].sem, 1)
                        act.wait_ge(*S["h"].done(w))
                        act.activation(gT[:, 0:P], bMM[:, 0:P], ACT.Gelu, bias=mb1[:, 0:1])
                        act.activation(gT[:, P:2 * P], bMM[:, P:2 * P], ACT.Gelu, bias=mb1[:, 1:2]).then_inc(S["g"].sem, 1)
                        norm_root(act, 1, w)
                        norm_root(act, 2, w)
                        act.wait_ge(*S["x2Tp"].done(w))
                        act.wait_ge(*SD["outT"].before(w))
                        act.activation(x2nT[:], bT[:, 0:D], ACT.Copy).then_inc(S["x2T"].sem, 1)
                        act.dma_start(tile_rows(x2_d, w), x2[:]).then_inc(SD["outx2"].sem, 16)
                        act.wait_ge(*S["x2T"].done(w))
                        act.dma_start(x2nT_d[bass.ds(w, 1)].rearrange("t p d -> (t p) d"), x2nT[:]).then_inc(SD["outT"].sem, 16)
                    for s in SD.values():
                        act.wait_ge(s.sem, (T + 1) * 16)

                @block.tensor
                def _(pe):
                    for n in ("t", "x1Tp", "h", "y", "x2Tp", "gat"):
                        S[n].start(pe)
                    rank_start(pe, R, PE_RANK)
                    G["sum"].start(pe)
                    pe.sem_inc(G["ringfree"], RING)
                    pe.sem_inc(G["pairs"], ohring)
                    pe.wait_ge(c_load, 64)
                    pe.wait_ge(s_kv, 1)
                    with pe.Fori(0, T) as w:
                        aggregate(pe, G, w)
                        rank_turn(pe, R, 0, w)
                        pe.wait_ge(*SD["inq"].done(w))
                        pe.wait_ge(*S["tz"].before(w))
                        for j in range(2):
                            last = pe.matmul(bQ[:, j * (P + 4):(j + 1) * (P + 4)], qT[:, j * P:(j + 1) * P], kvbd[:, j, :],
                                             start=True, stop=True, skip_group_check=True)
                        last.then_inc(S["t"].sem, 1)
                        rank_count(pe, R, 0, w)
                        pe.wait_ge(*S["x1"].done(w))
                        pe.wait_ge(*S["x2T"].before(w))
                        for j in range(2):
                            last = pe.transpose(bT[:, j * P:(j + 1) * P], x1[:, j * P:(j + 1) * P], c("ident"))
                        last.then_inc(S["x1Tp"].sem, 1)
                        pe.wait_ge(*S["x1T"].done(w))
                        pe.wait_ge(*S["gatev"].before(w))
                        for o in range(2):
                            for j in range(2):
                                last = pe.matmul(bMM[:, o * P:(o + 1) * P], w1[:, j, o * P:(o + 1) * P],
                                                 x1T[:, j * P:(j + 1) * P], start=(j == 0), stop=(j == 1))
                        last.then_inc(S["h"].sem, 1)
                        pe.wait_ge(*S["g"].done(w))
                        pe.wait_ge(*S["s2"].before(w))
                        for j in range(2):
                            last = pe.matmul(bKV[:, 0:D], gT[:, j * P:(j + 1) * P], w2[:, j, :], start=(j == 0), stop=(j == 1))
                        last.then_inc(S["y"].sem, 1)
                        pe.wait_ge(*S["x2n"].done(w))
                        for j in range(2):
                            last = pe.transpose(bT[:, j * P:(j + 1) * P], x2n[:, j * P:(j + 1) * P], c("ident"))
                        last.then_inc(S["x2Tp"].sem, 1)
                        pe.wait_ge(*S["x2T"].done(w))
                        for j in range(2):
                            last = pe.matmul(bMM[:, 0:16], x2nT[:, j * P:(j + 1) * P], wg[:, j, :], start=(j == 0), stop=(j == 1))
                        last.then_inc(S["gat"].sem, 1)

                @block.vector
                def _(dve):
                    for n in ("den", "rden", "tz", "s1", "a1", "x1", "x1b", "s2", "a2", "mix", "dg", "rinv", "lg", "lx", "x2", "x2n", "gatev"):
                        S[n].start(dve)
                    for n in LN:
                        for k in ("st", "mv", "rs"):
                            n["s"][k].start(dve)
                    rank_start(dve, R, DVE_RANK)
                    for j in range(2):
                        at = j * (P + 1)
                        dve.tensor_tensor(kvbd[:, j, 0:P], bKV[:, at:at + P], c("kvmask")[:, 0:P], ALU.mult)
                        last = dve.tensor_tensor(kvbd[:, j, P:P + 4], bKV[:, at + P:at + P + 1].broadcast_to([P, 4]), c("kvmask")[:, P:P + 4], ALU.mult)
                    last.then_inc(s_kv, 1)
                    onehots(dve, G, 0)
                    with dve.Fori(0, T) as w:
                        batch = w + T * RB1
                        rank_hot(dve, R, 0, w, batch)
                        dve.wait_ge(*G["sum"].done(w))
                        dve.tensor_scalar(dg[:], bAGG[:, D:D + 1], 1.0, None, ALU.max).then_inc(S["dg"].sem, 1)
                        dve.wait_ge(*S["dg"].done(w))
                        dve.reciprocal(rinv[:], dg[:]).then_inc(S["rinv"].sem, 1)
                        dve.wait_ge(*S["rinv"].done(w))
                        dve.wait_ge(*SD["inr"].done(w))
                        dve.scalar_tensor_tensor(lg[:], bAGG[:, 0:D], rinv[:], r2[:], ALU.mult, ALU.add).then_inc(S["lg"].sem, 1)
                        dve.wait_ge(*S["t"].done(w))
                        bq = bQ[:, 0:2 * (P + 4)].rearrange("p (j n) -> p j n", j=2)
                        dve.tensor_scalar(den[:].rearrange("p (j n) -> p j n", j=2), bq[:, :, P:P + 4], 1e-6, None, ALU.add).then_inc(S["den"].sem, 1)
                        dve.wait_ge(*S["den"].done(w))
                        dve.reciprocal(rden[:], den[:]).then_inc(S["rden"].sem, 1)
                        dve.wait_ge(*S["lg"].done(w))
                        dve.wait_ge(*SD["inx"].done(w))
                        dve.tensor_tensor(lx[:], lg[:], xw[:], ALU.add).then_inc(S["lx"].sem, 1)
                        dve.wait_ge(*S["rden"].done(w))
                        dve.tensor_tensor(tz[:].rearrange("p (j h n) -> p j h n", j=2, h=4),
                                          bq[:, :, 0:P].rearrange("p j (h n) -> p j h n", h=4),
                                          rden[:].rearrange("p (j h) -> p j h", j=2).unsqueeze(3).broadcast_to([P, 2, 4, DH]),
                                          ALU.mult).then_inc(S["tz"].sem, 1)
                        dve.wait_ge(*S["tz"].done(w))
                        dve.wait_ge(*S["xs"].done(w))
                        dve.tensor_tensor(s1[:], tz[:], xs[:], ALU.add).then_inc(S["s1"].sem, 1)
                        dve.wait_ge(*S["s1"].done(w))
                        norm_stats(dve, 0, w, s1[:])
                        dve.scalar_tensor_tensor(a1[:], s1[:], LN[0]["mv"][:, 0:1], r("ln1_g"), ALU.subtract, ALU.mult).then_inc(S["a1"].sem, 1)
                        dve.wait_ge(*S["a1"].done(w))
                        dve.wait_ge(*S["x1Tp"].before(w))
                        dve.scalar_tensor_tensor(x1[:], a1[:], LN[0]["rs"][:], r("ln1_b"), ALU.mult, ALU.add).then_inc(S["x1"].sem, 1)
                        rank_near(dve, R, 0, w, batch)
                        rank_place(dve, R, 0, w, batch)
                        dve.wait_ge(*S["x1"].done(w))
                        dve.tensor_tensor(x1b[:], x1[:], r("mix_b2"), ALU.add).then_inc(S["x1b"].sem, 1)
                        dve.wait_ge(*S["y"].done(w))
                        dve.wait_ge(*S["x1b"].done(w))
                        dve.tensor_tensor(s2[:], bKV[:, 0:D], x1b[:], ALU.add).then_inc(S["s2"].sem, 1)
                        dve.wait_ge(*S["s2"].done(w))
                        norm_stats(dve, 1, w, s2[:])
                        dve.scalar_tensor_tensor(a2[:], s2[:], LN[1]["mv"][:, 0:1], r("ln2_g"), ALU.subtract, ALU.mult).then_inc(S["a2"].sem, 1)
                        dve.wait_ge(*S["a2"].done(w))
                        dve.scalar_tensor_tensor(mix[:], a2[:], LN[1]["rs"][:], r("ln2_b"), ALU.mult, ALU.add).then_inc(S["mix"].sem, 1)
                        dve.wait_ge(*S["mix"].done(w))
                        dve.wait_ge(*SD["outx2"].before(w))
                        dve.tensor_tensor(x2[:], mix[:], lx[:], ALU.add).then_inc(S["x2"].sem, 1)
                        dve.wait_ge(*S["x2"].done(w))
                        norm_stats(dve, 2, w, x2[:])
                        dve.wait_ge(*LN[2]["s"]["rs"].done(w))
                        dve.wait_ge(*S["x2Tp"].before(w))
                        dve.tensor_scalar(x2n[:], x2[:], LN[2]["mv"][:, 0:1], LN[2]["rs"][:], ALU.subtract, ALU.mult).then_inc(S["x2n"].sem, 1)
                        onehots(dve, G, w + 1)
                        dve.wait_ge(*S["gat"].done(w))
                        dve.tensor_scalar(trow[:, bass.ds(w, 1), 0:16], bMM[:, 0:16].unsqueeze(1), 1.0, None, ALU.mult).then_inc(S["gatev"].sem, 1)
                    dve.wait_ge(S["gatev"].sem, T + 1)
                    dve.tensor_tensor(atp[:], trow[:, :, 0:16], r("att_src").unsqueeze(1).broadcast_to([P, T, 16]), ALU.mult).then_inc(s_tab, 1)
                    dve.wait_ge(s_tab, 1)
                    dve.tensor_reduce(trow[:, :, 16:20], atp[:].rearrange("p t (h e) -> p t h e", h=EH), AX.X, ALU.add).then_inc(s_tab, 1)
                    dve.wait_ge(s_tab, 2)
                    dve.tensor_tensor(atp[:], trow[:, :, 0:16], r("att_dst").unsqueeze(1).broadcast_to([P, T, 16]), ALU.mult).then_inc(s_tab, 1)
                    dve.wait_ge(s_tab, 3)
                    dve.tensor_reduce(adst[:], atp[:].rearrange("p t (h e) -> p t h e", h=EH), AX.X, ALU.add).then_inc(s_tab, 1)
        early.close()
        clear_semaphores()
        if upto <= 3:
            return

        with ExitStack() as b:
            HALF = 2
            EI = FC // (HALF * GRP)
            got = [sbuf(b, f"got{h}", [P, GRP, TW], F32) for h in range(HALF)]
            isrc = [sbuf(b, f"isrc{h}", [P, GRP], I32) for h in range(HALF)]
            ipos = [sbuf(b, f"ipos{h}", [P, GRP], I32) for h in range(HALF)]
            s_isrc = [sem(f"d_isrc{h}") for h in range(HALF)]
            s_ipos = [sem(f"d_ipos{h}") for h in range(HALF)]
            s_got = [Step(sem(f"d_got{h}"), 16 * GRP, 0) for h in range(HALF)]
            s_put = [Step(sem(f"d_put{h}"), 16 * GRP, 0) for h in range(HALF)]
            go = sem("d_go")
            mw1 = sbuf(b, "mw1", [P, E * 2, FH], F32)
            mw2 = sbuf(b, "mw2", [P, E * 4, D], F32)
            fb1 = sbuf(b, "fb1", [P, E * 4], F32)
            xT = sbuf(b, "xT_d", [P, 2 * P], F32)
            gh = [sbuf(b, f"gh{e}", [P, FH], F32) for e in range(E)]
            Y = sbuf(b, "Y", [P, E * D], F32)
            bH = [psum(b, f"bH{e}") for e in range(E)]
            bY = [psum(b, f"bY{i}") for i in range(2)]
            S = steps("d", [f"h{e}" for e in range(E)] + [f"g{e}" for e in range(E)] + ["y0", "y1", "Y0", "Y1"])
            SD = steps("d", ["in", "out"], 16)
            d_load = sem("d_load")
            with nc.Block() as block:
                @block.gpsimd
                def _(pool):
                    with pool.Fori(0, EI) as i:
                        for h in range(HALF):
                            pool.wait_ge(s_isrc[h], (i + 1) * 16)
                            pool.wait_ge(s_ipos[h], (i + 1) * 16)
                            pool.sem_inc(go, 1)
                            for k in range(GRP):
                                pool.indirect_dma_start(
                                    out=got[h][:, k, :], out_offset=None, in_=heads_d,
                                    in_offset=bass.IndirectOffsetOnAxis(ap=isrc[h][:, k:k + 1], axis=0)).then_inc(s_got[h].sem, 16)
                        for h in range(HALF):
                            pool.wait_ge(s_ipos[h], (i + 1) * 16)
                            pool.wait_ge(*s_got[h].done(i))
                            pool.sem_inc(go, 1)
                            for k in range(GRP):
                                pool.indirect_dma_start(
                                    out=sorted_d, out_offset=bass.IndirectOffsetOnAxis(ap=ipos[h][:, k:k + 1], axis=0),
                                    in_=got[h][:, k, :], in_offset=None).then_inc(s_put[h].sem, 16)
                    for h in range(HALF):
                        pool.wait_ge(s_put[h].sem, EI * 16 * GRP)

                @block.sync
                def _(sp):
                    for h in range(HALF):
                        sp.dma_start(isrc[h][:], io["ffn_src"][h]).then_inc(s_isrc[h], 16)
                        sp.dma_start(ipos[h][:], pos[:, h * GRP:(h + 1) * GRP]).then_inc(s_ipos[h], 16)
                    sp.dma_start(mw1[:], io["moe_w1"]).then_inc(d_load, 16)
                    sp.dma_start(mw2[:], io["moe_w2"]).then_inc(d_load, 16)
                    sp.dma_start(fb1[:], io["moe_b1"]).then_inc(d_load, 16)
                    with sp.Fori(0, EI) as i:
                        for h in range(HALF):
                            sp.wait_ge(*s_got[h].done(i))
                            sp.dma_start(isrc[h][:], io["ffn_src"][bass.ds((i + 1) * HALF + h, 1)].rearrange("g p k -> (g p) k"))\
                                .then_inc(s_isrc[h], 16)
                        for h in range(HALF):
                            sp.wait_ge(*s_put[h].done(i))
                            sp.dma_start(ipos[h][:], pos[:, bass.ds((i + 1) * HALF * GRP + h * GRP, GRP)]).then_inc(s_ipos[h], 16)
                    for h in range(HALF):
                        sp.wait_ge(s_isrc[h], (EI + 1) * 16)
                        sp.wait_ge(s_ipos[h], (EI + 1) * 16)

                @block.scalar
                def _(act):
                    for e in range(E):
                        S[f"g{e}"].start(act)
                    for s in SD.values():
                        s.start(act)
                    act.wait_ge(d_load, 48)
                    with act.Fori(0, T) as t:
                        act.wait_ge(*S[f"h{E - 1}"].before(t))
                        act.dma_start(xT[:], x2nT_d[bass.ds(t, 1)].rearrange("t p d -> (t p) d")).then_inc(SD["in"].sem, 16)
                        for e in range(E):
                            act.wait_ge(*S[f"h{e}"].done(t))
                            act.wait_ge(*S[f"y{e // 2}"].before(t))
                            for f in range(4):
                                last = act.activation(gh[e][:, f * P:(f + 1) * P], bH[e][:, f * P:(f + 1) * P], ACT.Gelu,
                                                      bias=fb1[:, e * 4 + f:e * 4 + f + 1])
                            last.then_inc(S[f"g{e}"].sem, 1)
                        act.wait_ge(*S["Y0"].done(t))
                        act.wait_ge(*S["Y1"].done(t))
                        act.dma_start(experts_d[bass.ds(t, 1)].rearrange("t p d -> (t p) d"), Y[:]).then_inc(SD["out"].sem, 16)
                    act.wait_ge(SD["in"].sem, (T + 1) * 16)
                    act.wait_ge(SD["out"].sem, (T + 1) * 16)

                @block.tensor
                def _(pe):
                    for e in range(E):
                        S[f"h{e}"].start(pe)
                    S["y0"].start(pe)
                    S["y1"].start(pe)
                    pe.wait_ge(d_load, 48)
                    with pe.Fori(0, T) as t:
                        pe.wait_ge(*SD["in"].done(t))
                        for e in range(E):
                            pe.wait_ge(*S[f"g{e}"].before(t))
                            for f in range(4):
                                for j in range(2):
                                    last = pe.matmul(bH[e][:, f * P:(f + 1) * P], mw1[:, e * 2 + j, f * P:(f + 1) * P],
                                                     xT[:, j * P:(j + 1) * P], start=(j == 0), stop=(j == 1))
                            last.then_inc(S[f"h{e}"].sem, 1)
                        for e in range(E):
                            pe.wait_ge(*S[f"g{e}"].done(t))
                            if e % 2 == 0:
                                pe.wait_ge(*S[f"Y{e // 2}"].before(t))
                            for f in range(4):
                                last = pe.matmul(bY[e // 2][:, (e % 2) * D:(e % 2 + 1) * D], gh[e][:, f * P:(f + 1) * P],
                                                 mw2[:, e * 4 + f, :], start=(f == 0), stop=(f == 3))
                            if e % 2:
                                last.then_inc(S[f"y{e // 2}"].sem, 1)

                @block.vector
                def _(dve):
                    S["Y0"].start(dve)
                    S["Y1"].start(dve)
                    with dve.Fori(0, T) as t:
                        dve.wait_ge(*SD["out"].before(t))
                        for i in range(2):
                            dve.wait_ge(*S[f"y{i}"].done(t))
                            dve.tensor_tensor(Y[:, i * 2 * D:(i + 1) * 2 * D], bY[i][:],
                                              r("ffn_b2")[:, i * 2 * D:(i + 1) * 2 * D], ALU.add).then_inc(S[f"Y{i}"].sem, 1)
        clear_semaphores()
        if upto <= 4:
            return

        with ExitStack() as b:
            m = sbuf(b, "m", [P, T, EH], F32)
            den = sbuf(b, "den_e", [P, T, EH], F32)
            agg = sbuf(b, "agg", [P, T, 16], F32)
            idx = [sbuf(b, f"idx_e{i}", [P, 1], I32) for i in range(3)]
            got = [sbuf(b, f"got_e{i}", [P, L * TW], F32) for i in range(2)]
            e0, e1, e2, e3, ee = (sbuf(b, f"e_{i}", [P, L, EH], F32) for i in range(5))
            pen = sbuf(b, "pen", [P, L], F32)
            prod = sbuf(b, "prod_e", [P, L, 16], F32)
            mr, mn, dm, corr, sr, dc = (sbuf(b, f"small{i}", [P, EH], F32) for i in range(6))
            ar, ac = (sbuf(b, f"wide{i}", [P, 16], F32) for i in range(2))
            S = steps("e", ["idx0", "idx1", "idx2", "first", "left"])
            SG = [Step(sem(f"e_got{i}"), 16, 0) for i in range(3)]
            s_init = sem("e_init")
            go = sem("e_go")
            names = ["e0", "e1", "pen", "e2", "mr", "mn", "dm", "e3", "corr", "ee", "sr", "dc", "den", "prod", "ar", "ac", "agg"]
            SR = [steps(f"e_{i}", names) for i in range(3)]

            def gather_block(pool, i, n):
                pool.wait_ge(*S[f"idx{i}"].done(n))
                pool.sem_inc(go, 1)
                pool.indirect_dma_start(out=got[i % 2][:], out_offset=None, in_=sorted_d,
                                        in_offset=bass.IndirectOffsetOnAxis(ap=idx[i][:], axis=0)).then_inc(SG[i].sem, 16)

            def fold(dve, i, t, n, s, count):
                g3 = got[i][:].rearrange("p (l f) -> p l f", f=TW)
                mt = flat(m[:, bass.ds(t, 1), :])
                dt_ = flat(den[:, bass.ds(t, 1), :])
                at = flat(agg[:, bass.ds(t, 1), :])
                dve.wait_ge(*s["e1"].before(n))
                dve.tensor_tensor(e0[:], g3[:, :, 16:20], adst[:, bass.ds(t, 1), :].broadcast_to([P, L, EH]), ALU.add).then_inc(s["e0"].sem, 1)
                dve.tensor_scalar(pen[:], c("slot"), count, -1e30, ALU.is_ge, ALU.mult).then_inc(s["pen"].sem, 1)
                dve.wait_ge(*s["e0"].done(n))
                dve.scalar_tensor_tensor(e1[:], e0[:], 0.2, e0[:], ALU.mult, ALU.max).then_inc(s["e1"].sem, 1)
                dve.wait_ge(*s["e1"].done(n))
                dve.tensor_tensor(e2[:], e1[:], pen[:].unsqueeze(2).broadcast_to([P, L, EH]), ALU.add).then_inc(s["e2"].sem, 1)
                dve.wait_ge(*s["e2"].done(n))
                dve.tensor_reduce(mr[:], e2[:].rearrange("p l h -> p h l"), AX.X, ALU.max).then_inc(s["mr"].sem, 1)
                dve.wait_ge(*s["mr"].done(n))
                dve.tensor_tensor(mn[:], mr[:], mt, ALU.max).then_inc(s["mn"].sem, 1)
                dve.wait_ge(*s["mn"].done(n))
                dve.tensor_tensor(e3[:], e2[:], mn[:].unsqueeze(1).broadcast_to([P, L, EH]), ALU.subtract).then_inc(s["e3"].sem, 1)
                dve.tensor_tensor(dm[:], mt, mn[:], ALU.subtract).then_inc(s["dm"].sem, 1)
                dve.wait_ge(*s["dm"].done(n))
                dve.tensor_scalar(mt, mn[:], 1.0, None, ALU.mult)
                dve.wait_ge(*s["corr"].done(n))
                dve.tensor_tensor(dc[:], dt_, corr[:], ALU.mult).then_inc(s["dc"].sem, 1)
                dve.tensor_tensor(ac[:].rearrange("p (h e) -> p h e", h=EH), at.rearrange("p (h e) -> p h e", h=EH),
                                  corr[:].unsqueeze(2).broadcast_to([P, EH, E]), ALU.mult).then_inc(s["ac"].sem, 1)
                dve.wait_ge(*s["ee"].done(n))
                dve.tensor_tensor(prod[:].rearrange("p l (h e) -> p l h e", h=EH), g3[:, :, 0:16].rearrange("p l (h e) -> p l h e", h=EH),
                                  ee[:].unsqueeze(3).broadcast_to([P, L, EH, E]), ALU.mult).then_inc(s["prod"].sem, 1)
                dve.tensor_reduce(sr[:], ee[:].rearrange("p l h -> p h l"), AX.X, ALU.add).then_inc(s["sr"].sem, 1)
                dve.wait_ge(*s["prod"].done(n))
                dve.tensor_reduce(ar[:], prod[:].rearrange("p l f -> p f l"), AX.X, ALU.add).then_inc(s["ar"].sem, 1)
                dve.wait_ge(*s["sr"].done(n))
                dve.tensor_tensor(dt_, dc[:], sr[:], ALU.add).then_inc(s["den"].sem, 1)
                dve.wait_ge(*s["ar"].done(n))
                dve.tensor_tensor(at, ac[:], ar[:], ALU.add).then_inc(s["agg"].sem, 1)
                dve.wait_ge(*s["agg"].done(n))

            def exps(act, n, s):
                act.wait_ge(*s["dm"].done(n))
                act.activation(corr[:], dm[:], ACT.Exp).then_inc(s["corr"].sem, 1)
                act.wait_ge(*s["e3"].done(n))
                act.activation(flat(ee[:]), flat(e3[:]), ACT.Exp).then_inc(s["ee"].sem, 1)

            ACT_STEPS = ("corr", "ee")

            def extra_rounds(eng, body):
                seen = eng.alloc_register("rounds")
                eng.reg_mov(seen, 0)
                with eng.Fori(0, T) as t:
                    most = eng.value_load(dtab[0:1, bass.ds(t, 1)], min_val=0, max_val=FE)
                    with eng.If(most > L):
                        with eng.Fori(1, (most + (L - 1)) // L) as k:
                            body(t, k, eng.snap(seen, min_val=0, max_val=FE))
                            eng.reg_add(seen, seen, 1)

            with nc.Block() as block:
                @block.gpsimd
                def _(pool):
                    with pool.Fori(0, T // 2) as t2:
                        for i in range(2):
                            gather_block(pool, i, t2)
                    extra_rounds(pool, lambda t, k, n: gather_block(pool, 2, n))

                @block.scalar
                def _(act):
                    for s in SR:
                        for k in ACT_STEPS:
                            s[k].start(act)
                    with act.Fori(0, T // 2) as t2:
                        for i in range(2):
                            exps(act, t2, SR[i])
                    extra_rounds(act, lambda t, k, n: exps(act, n, SR[2]))

                @block.vector
                def _(dve):
                    for s in list(S.values()):
                        s.start(dve)
                    for s in SR:
                        for k in names:
                            if k not in ACT_STEPS:
                                s[k].start(dve)
                    dve.tensor_copy(agg[:], trow[:, :, 0:16])
                    dve.memset(den[:], 1.0)
                    dve.tensor_tensor(m[:], trow[:, :, 16:20], adst[:], ALU.add).then_inc(s_init, 1)
                    dve.wait_ge(s_init, 1)
                    dve.scalar_tensor_tensor(m[:], m[:], 0.2, m[:], ALU.mult, ALU.max).then_inc(s_init, 1)
                    for i in range(2):
                        dve.tensor_copy(idx[i][:], first[:, i:i + 1]).then_inc(S[f"idx{i}"].sem, 1)
                    dve.wait_ge(s_init, 2)
                    with dve.Fori(0, T // 2) as t2:
                        for i in range(2):
                            t = t2 * 2 + i
                            dve.wait_ge(*SG[i].done(t2))
                            fold(dve, i, t, t2, SR[i], deg[:, bass.ds(t, 1)])
                            dve.tensor_scalar(idx[i][:], first[:, bass.ds(t + 2, 1)], 1.0, None, ALU.mult).then_inc(S[f"idx{i}"].sem, 1)

                    def body(t, k, n):
                        ft, dt_ = first[:, bass.ds(t, 1)], deg[:, bass.ds(t, 1)]
                        dve.tensor_scalar(ft, ft, float(L), float(FE), ALU.add, ALU.min).then_inc(S["first"].sem, 1)
                        dve.tensor_scalar(dt_, dt_, float(L), None, ALU.subtract).then_inc(S["left"].sem, 1)
                        dve.wait_ge(*S["first"].done(n))
                        dve.tensor_scalar(idx[2][:], ft, 1.0, None, ALU.mult).then_inc(S["idx2"].sem, 1)
                        dve.wait_ge(*S["left"].done(n))
                        dve.wait_ge(*SG[2].done(n))
                        fold(dve, 0, t, n, SR[2], dt_)
                    extra_rounds(dve, body)
            clear_semaphores()
            if upto <= 5:
                return

            sc = sbuf(b, "sc_f", [P, T, 16], F32)
            sq = sbuf(b, "sq_f", [P, T, 16], F32)
            rd = sbuf(b, "rd_f", [P, T, EH], F32)
            mu, vr, sd, rs = (sbuf(b, f"stat_f{i}", [P, T], F32) for i in range(4))
            score, gate, rank = (sbuf(b, f"score_f{i}", [P, T, E], F32) for i in range(3))
            beats = sbuf(b, "beats", [P, T, E, E], F32)
            Yt = [sbuf(b, f"Yt{i}", [P, E * D], F32) for i in range(2)]
            xt = [sbuf(b, f"xt{i}", [P, D], F32) for i in range(2)]
            acc = [[sbuf(b, f"acc{i}_{e}", [P, D], F32) for e in range(E)] for i in range(2)]
            chain = sem("f_chain")
            s_sd, s_ex = sem("f_sd"), sem("f_ex")
            SF = [steps(f"f{i}", [f"acc{e}" for e in range(E)]) for i in range(2)]
            SIN = [Step(sem(f"f_in{i}"), 32) for i in range(2)]
            SOUT = [Step(sem(f"f_out{i}"), 16) for i in range(2)]

            with nc.Block() as block:
                @block.sync
                def _(sp):
                    for i in range(2):
                        SIN[i].start(sp)
                    with sp.Fori(0, T // 2) as t2:
                        for i in range(2):
                            t = t2 * 2 + i
                            sp.wait_ge(*SF[i][f"acc{E - 1}"].before(t2))
                            sp.dma_start(Yt[i][:], experts_d[bass.ds(t, 1)].rearrange("t p d -> (t p) d")).then_inc(SIN[i].sem, 16)
                            sp.dma_start(xt[i][:], tile_rows(x2_d, t)).then_inc(SIN[i].sem, 16)

                @block.scalar
                def _(act):
                    for i in range(2):
                        SOUT[i].start(act)
                    act.wait_ge(chain, 7)
                    act.activation(sd[:], vr[:], ACT.Sqrt, bias=c("eps")).then_inc(s_sd, 1)
                    act.wait_ge(chain, 16)
                    act.activation(flat(gate[:]), flat(score[:]), ACT.Exp).then_inc(s_ex, 1)
                    with act.Fori(0, T // 2) as t2:
                        for i in range(2):
                            act.wait_ge(*SF[i][f"acc{E - 1}"].done(t2))
                            act.dma_start(tile_rows(out, t2 * 2 + i), acc[i][E - 1][:]).then_inc(SOUT[i].sem, 16)
                    for i in range(2):
                        act.wait_ge(SOUT[i].sem, (T // 2 + 1) * 16)

                @block.vector
                def _(dve):
                    n = [0]

                    def link(ins):
                        n[0] += 1
                        ins.then_inc(chain, 1)
                        dve.wait_ge(chain, n[0])

                    def wide(ap, k):
                        return ap.unsqueeze(2).broadcast_to([P, T, k])

                    for i in range(2):
                        for e in range(E):
                            SF[i][f"acc{e}"].start(dve)
                    dve.memset(beats[:], 0.0)
                    link(dve.tensor_scalar(den[:], den[:], 1e-16, None, ALU.add))
                    link(dve.reciprocal(rd[:], den[:]))
                    link(dve.tensor_tensor(sc[:].rearrange("p t (h e) -> p t h e", h=EH), agg[:].rearrange("p t (h e) -> p t h e", h=EH),
                                           rd[:].unsqueeze(3).broadcast_to([P, T, EH, E]), ALU.mult))
                    link(dve.tensor_tensor(sc[:], sc[:], r("b_gat").unsqueeze(1).broadcast_to([P, T, 16]), ALU.add))
                    link(dve.tensor_reduce(mu[:], sc[:], AX.X, ALU.add))
                    link(dve.scalar_tensor_tensor(sc[:], wide(mu[:], 16), -1.0 / 16, sc[:], ALU.mult, ALU.add))
                    dve.tensor_tensor(sq[:], sc[:], sc[:], ALU.mult).then_inc(s_ex, 1)
                    dve.wait_ge(s_ex, 1)
                    dve.tensor_reduce(mu[:], sq[:], AX.X, ALU.add).then_inc(s_ex, 1)
                    dve.wait_ge(s_ex, 2)
                    link(dve.tensor_scalar(vr[:], mu[:], 1.0 / 16, None, ALU.mult))
                    dve.wait_ge(s_sd, 1)
                    link(dve.reciprocal(rs[:], sd[:]))
                    link(dve.tensor_tensor(sc[:], sc[:], wide(rs[:], 16), ALU.mult))
                    link(dve.tensor_tensor(sc[:], sc[:], r("gamma").unsqueeze(1).broadcast_to([P, T, 16]), ALU.mult))
                    link(dve.tensor_tensor(sc[:], sc[:], r("beta").unsqueeze(1).broadcast_to([P, T, 16]), ALU.add))
                    link(dve.tensor_reduce(rank[:], sc[:].rearrange("p t (h e) -> p t e h", h=EH), AX.X, ALU.add))
                    link(dve.tensor_scalar(score[:], rank[:], 1.0 / EH, None, ALU.mult))
                    for e in range(E):
                        for j in range(E):
                            if j != e:
                                last = dve.tensor_tensor(beats[:, :, e, j], score[:, :, j], score[:, :, e], ALU.is_ge if j < e else ALU.is_gt)
                    link(last)
                    link(dve.tensor_reduce(mu[:], score[:], AX.X, ALU.max))
                    link(dve.tensor_tensor(score[:], score[:], wide(mu[:], E), ALU.subtract))
                    link(dve.tensor_reduce(rank[:], beats[:], AX.X, ALU.add))
                    link(dve.tensor_scalar(rank[:], rank[:], 2.0, None, ALU.is_lt))
                    dve.wait_ge(s_ex, 3)
                    link(dve.tensor_tensor(gate[:], gate[:], rank[:], ALU.mult))
                    link(dve.tensor_reduce(mu[:], gate[:], AX.X, ALU.add))
                    link(dve.reciprocal(rs[:], mu[:]))
                    link(dve.tensor_tensor(gate[:], gate[:], wide(rs[:], E), ALU.mult))
                    with dve.Fori(0, T // 2) as t2:
                        for i in range(2):
                            dve.wait_ge(*SIN[i].done(t2))
                            dve.wait_ge(*SOUT[i].before(t2))
                        for e in range(E):
                            for i in range(2):
                                t = t2 * 2 + i
                                if e:
                                    dve.wait_ge(*SF[i][f"acc{e - 1}"].done(t2))
                                dve.scalar_tensor_tensor(acc[i][e][:], Yt[i][:, e * D:(e + 1) * D], flat(gate[:, bass.ds(t, 1), e:e + 1]),
                                                         xt[i][:] if e == 0 else acc[i][e - 1][:], ALU.mult, ALU.add)\
                                   .then_inc(SF[i][f"acc{e}"].sem, 1)


def layouts(x, src, dst, L0_gnn_W_l1, L0_gnn_b1, L0_gnn_W_r1, L0_gnn_W_l2, L0_gnn_b2, L0_gnn_W_r2, L0_mix_Wqkv,
            L0_mix_ln1_g, L0_mix_ln1_b, L0_mix_W1, L0_mix_b1, L0_mix_W2, L0_mix_b2, L0_mix_ln2_g, L0_mix_ln2_b,
            L0_ffn_W_gat, L0_ffn_att_src, L0_ffn_att_dst, L0_ffn_b_gat, L0_ffn_ln_gamma, L0_ffn_ln_beta,
            L0_ffn_W1, L0_ffn_b1, L0_ffn_W2, L0_ffn_b2, L0_ffn_edge_index):
    def chunks(v, count, fill):
        v = np.concatenate([v, np.full(count * P - v.shape[0], fill, v.dtype)])
        return v.reshape(count, P).T

    def halves(w):
        return w.reshape(2, P, -1).transpose(1, 0, 2)

    gsrc = chunks(src, GC + RING, 0)
    fdst = chunks(L0_ffn_edge_index[1], FCP, NO_NODE)
    rows = {"gnn_b1": L0_gnn_b1, "gnn_b2": L0_gnn_b2, "ln1_g": L0_mix_ln1_g, "ln1_b": L0_mix_ln1_b,
            "mix_b2": L0_mix_b2, "ln2_g": L0_mix_ln2_g, "ln2_b": L0_mix_ln2_b, "att_src": L0_ffn_att_src,
            "att_dst": L0_ffn_att_dst, "b_gat": L0_ffn_b_gat, "gamma": L0_ffn_ln_gamma, "beta": L0_ffn_ln_beta,
            "ffn_b2": L0_ffn_b2}
    return {
        "consts": shape_constants(),
        "x": np.pad(x, ((0, NP - N), (0, 0))),
        "gnn_src": gsrc.reshape(P, (GC + RING) // GRP, GRP).transpose(1, 0, 2),
        "gnn_dst": chunks(dst, GC, NO_NODE),
        "ffn_src": chunks(L0_ffn_edge_index[0], FC + 2 * GRP, 0).reshape(P, FC // GRP + 2, GRP).transpose(1, 0, 2),
        "ffn_dst": fdst,
        "ffn_dst_rows": fdst.T.reshape(1, FCP * P),
        "wlr1": halves(np.concatenate([L0_gnn_W_l1, L0_gnn_W_r1], 1)),
        "wlr2": halves(np.concatenate([L0_gnn_W_l2, L0_gnn_W_r2], 1)),
        "wkv": halves(L0_mix_Wqkv[D:].T),
        "wq": halves(L0_mix_Wqkv[:D].T),
        "w1": halves(L0_mix_W1.T),
        "w2": halves(L0_mix_W2.T),
        "mix_b1": L0_mix_b1.reshape(2, P).T,
        "wgat": halves(L0_ffn_W_gat),
        "moe_w1": L0_ffn_W1.reshape(E, 2, P, FH).transpose(2, 0, 1, 3).reshape(P, E * 2, FH),
        "moe_w2": L0_ffn_W2.reshape(E, 4, P, D).transpose(2, 0, 1, 3).reshape(P, E * 4, D),
        "moe_b1": L0_ffn_b1.reshape(E * 4, P).T,
        "rows": np.concatenate([rows[k].reshape(-1) for k, _ in ROW_SIZES])[None, :],
    }


KINDS = "Internal"
UPTO = 9


def kernel(**inputs):
    import concourse.bacc as _bacc
    from concourse.bass_utils import run_bass_kernel_spmd as _run

    nc = _bacc.Bacc("TRN2", target_bir_lowering=False, num_devices=1)
    arrays, io = {}, {}
    for name, a in layouts(**{k: np.asarray(v) for k, v in inputs.items()}).items():
        a = np.ascontiguousarray(a)
        arrays[f"in_{name}"] = a
        io[name] = nc.dram_tensor(f"in_{name}", a.shape, mybir.dt.from_np(a.dtype), kind="ExternalInput").ap()
    out = nc.dram_tensor("out_0", (NP, D), F32, kind="ExternalOutput").ap()
    build(nc, io, out, KINDS, UPTO)
    r = _run(nc, [arrays], core_ids=[0])
    return r.results[0]["out_0"][:N]
```

```python
from contextlib import ExitStack

import concourse.bass as bass
import numpy as np
from concourse import mybir

F32 = mybir.dt.float32
BF16 = mybir.dt.bfloat16
I32 = mybir.dt.int32
ALU = mybir.AluOpType
ACT = mybir.ActivationFunctionType
AX = mybir.AxisListType

P = 128
D = 256
N = 12500
T = -(-N // P)
NP = T * P
GE = 212500
K = 18
KG = 6
NG = K // KG
KX = 2
GC = -(-(GE + P * K) // P) + 1
GRP = 8
FE = 131072
FC = FE // P
HB = 12
RB = 4
RB1, RB2 = 2, 1
FCP = T * HB
L = 40
TW = 20
H, DH = 8, 32
E, EH = 4, 4
FH = 512
EPS = 1e-5
NO_NODE = 128 * 127
CHUNK_W = 3 * D
SLOT = CHUNK_W + 2

CONST = {}


def shape_constants():
    p = np.arange(P)[:, None]
    f = np.arange(P)[None, :]
    parts = {
        "iota": np.broadcast_to(f, (P, P)),
        "ident": (p == f),
        "before": (p < f),
        "ones": np.ones((P, P)),
        "wbase": np.broadcast_to(-128 * np.arange(T + 1)[None, :], (P, T + 1)),
        "wend": 128 * (p + 1),
        "real": (np.arange(T)[None, :] * P + p) < N,
        "kvmask": np.concatenate([(p // DH == f // DH), (p // DH == np.arange(4)[None, :])], 1),
        "rankmask": np.concatenate([(np.arange(RB * P)[None, :] < k * P + p) for k in range(RB)], 1),
        "slot": np.broadcast_to(np.arange(L)[None, :], (P, L)),
        "eps": np.full((P, 1), EPS),
    }
    at = 0
    for k, v in parts.items():
        CONST[k] = (at, v.shape[1])
        at += v.shape[1]
    return np.ascontiguousarray(np.concatenate([v.astype(np.float32) for v in parts.values()], 1))


ROWS = {}


def row_layout(sizes):
    at = 0
    for k, n in sizes:
        ROWS[k] = (at, n)
        at += n
    return at


ROW_SIZES = [("gnn_b1", D), ("gnn_b2", D), ("ln1_g", D), ("ln1_b", D), ("mix_b2", D), ("ln2_g", D), ("ln2_b", D),
             ("att_src", 16), ("att_dst", 16), ("b_gat", 16), ("gamma", 16), ("beta", 16), ("ffn_b2", E * D)]
NROW = row_layout(ROW_SIZES)


class Step:

    def __init__(self, sem, unit=1, ahead=1):
        self.sem, self.unit, self.ahead = sem, unit, ahead

    def start(self, eng):
        assert self.ahead
        eng.sem_inc(self.sem, self.unit * self.ahead)

    def done(self, t):
        return self.sem, (t + 1 + self.ahead) * self.unit

    def before(self, t):
        assert self.ahead
        return self.sem, (t + self.ahead) * self.unit

    def before2(self, t):
        assert self.ahead == 2
        return self.sem, (t + 1) * self.unit


def flat(ap):
    return ap.rearrange("p a b -> p (a b)")


def build(nc, io, out, kinds, upto=9):
    ctx = ExitStack()
    with ctx:
        def scratch(name, shape, dt):
            return nc.dram_tensor(name, shape, dt, kind=kinds).ap()

        in_use = []

        def sem(name):
            in_use.append(nc.alloc_semaphore(name))
            return in_use[-1]

        def clear_semaphores():
            nc.clear_and_free_semaphores(list(in_use))
            nc.all_engine_barrier()
            in_use.clear()

        def steps(prefix, names, unit=1, ahead=1):
            return {n: Step(sem(f"{prefix}_{n}"), unit, ahead) for n in names}

        def sbuf(stack, name, shape, dt):
            return stack.enter_context(nc.sbuf_tensor(name, shape, dt))

        def psum(stack, name, dt=F32):
            return stack.enter_context(nc.psum_tensor(name, [P, 512 if dt == F32 else 1024], dt))

        table = [scratch(f"split_rows{i}", (NP, CHUNK_W), BF16) for i in range(2)]
        own = [scratch(f"own_rows{i}", (NP, D), F32) for i in range(2)]
        qT_d = scratch("q_transposed", (T, P, 2 * P), F32)
        x2_d = scratch("x_second", (NP, D), F32)
        x2nT_d = scratch("x_second_norm_transposed", (T, P, 2 * P), F32)
        heads_d = scratch("attention_rows", (NP, TW), F32)
        sorted_d = scratch("sorted_edge_rows", (FE + 2 * P, TW), F32)
        experts_d = scratch("expert_rows", (T, P, E * D), F32)
        windows_d = scratch("window_starts", (T + 1, 1), I32)
        degrees_d = scratch("largest_degrees", (T, 1), I32)

        const = sbuf(ctx, "const", [P, io["consts"].shape[1]], F32)
        rows = sbuf(ctx, "rows", [P, NROW], F32)
        ident16 = sbuf(ctx, "ident16", [P, P], BF16)
        ones16 = sbuf(ctx, "ones16", [P, 1], BF16)
        zeros16 = sbuf(ctx, "zeros16", [P, 512], BF16)
        wtab = sbuf(ctx, "wtab", [1, T + 1], I32)
        xtab = sbuf(ctx, "xtab", [1, T], I32)
        dtab = sbuf(ctx, "dtab", [1, T], I32)
        deg = sbuf(ctx, "deg", [P, T], F32)
        first = sbuf(ctx, "first", [P, T + 2], F32)
        trow = sbuf(ctx, "trow", [P, T, TW], F32)
        adst = sbuf(ctx, "adst", [P, T, EH], F32)
        pos = sbuf(ctx, "pos", [P, T * RB * (RB1 + RB2)], I32)

        def c(name):
            at, n = CONST[name]
            return const[:, at:at + n]

        def r(name):
            at, n = ROWS[name]
            return rows[:, at:at + n]

        def tile_rows(ap, w):
            return ap.rearrange("(t p) d -> t p d", p=P)[bass.ds(w, 1)].rearrange("t p d -> (t p) d")

        load = sem("load")
        setup = sem("setup")

        early = ctx.enter_context(ExitStack())
        rstd = sbuf(early, "rstd", [P, T], F32)
        nmr = sbuf(early, "nmr", [P, T], F32)
        xs = sbuf(early, "xs", [P, D], F32)
        flo = sbuf(early, "flo", [P, FCP], F32)
        fhi = sbuf(early, "fhi", [P, FCP], F32)
        fdst = sbuf(early, "fdst", [P, FCP], F32)
        wlr2 = sbuf(early, "wlr2", [P, 2, 2 * D], F32)
        kvbd = sbuf(early, "kvbd", [P, 2, P + 4], F32)
        bAGG = psum(early, "bAGG")
        bT = psum(early, "bT")
        bMM = psum(early, "bMM")
        bQ = psum(early, "bQ")
        bKV = psum(early, "bKV")
        bC = psum(early, "bC")
        bP = psum(early, "bP")
        bOT = psum(early, "bOT", BF16)

        with ExitStack() as a:
            X = sbuf(a, "X", [P, T, D], F32)
            wlr1 = sbuf(a, "wlr1", [P, 2, 2 * D], F32)
            stat = sbuf(a, "stat", [P, T, 6], F32)
            mean = sbuf(a, "mean", [P, T], F32)
            var = sbuf(a, "var", [P, T], F32)
            tmp = sbuf(a, "tmp", [P, T], F32)
            xT = sbuf(a, "xT", [P, 2, P], F32)
            ur = sbuf(a, "ur", [P, 2, D], F32)
            us = sbuf(a, "us", [P, 2 * 3, D], BF16)
            rs = sbuf(a, "rs", [P, 2, D], F32)
            Olo = sbuf(a, "Olo", [P, 2, HB, P], BF16)
            Ohi = sbuf(a, "Ohi", [P, 2, HB, T], BF16)
            sc = [sbuf(a, f"scan{i}", [P, T], F32) for i in range(2)]
            part = sbuf(a, "part", [P, T], F32)
            lastd = sbuf(a, "lastd", [T, GC], F32)
            ifd, ilo, ihi, lasti = (v[:].bitcast(I32) for v in (fdst, flo, fhi, lastd))
            endrow = sbuf(a, "endrow", [T, P], F32)
            iend = endrow[:].bitcast(I32)
            inend = sbuf(a, "inend", [T, 1], F32)
            endf = sbuf(a, "endf", [T, 1], F32)
            endi = sbuf(a, "endi", [T, 1], I32)
            s_endrow = sem("a_endrow")
            s_over = sem("a_over")
            cef = sbuf(a, "cef", [T, 1], F32)
            cei = sbuf(a, "cei", [T, 1], I32)
            mdi = sbuf(a, "mdi", [T, 1], I32)
            zi = sbuf(a, "zi", [1, 1], I32)

            XP = 7
            s_x = [sem(f"a_x{k}") for k in range(XP)]
            s_idx = sem("a_idx")
            chain = sem("a_chain")
            s_std = sem("a_std")
            a_turns = sem("a_turns")
            s_bn = sem("a_bn")
            A = steps("a", ["xn", "xnT", "xTs", "ur", "hi", "mid", "rev", "onehot"])
            A.update(steps("a", ["r1", "split", "hist"], ahead=2))
            AD = steps("a", ["stU", "stR"], 16, ahead=2)
            s_pre = sem("a_prefix")
            s_tr = sem("a_degT")
            s_out = sem("a_tables")
            s_ready = sem("a_ready")
            bUR = [bMM, bKV]
            A_IDX = 3
            with nc.Block() as block:
                @block.sync
                def _(sp):
                    for s in AD.values():
                        s.start(sp)
                    sp.dma_start(const[:], io["consts"]).then_inc(s_idx, 16)
                    sp.dma_start(ifd, io["ffn_dst"]).then_inc(s_idx, 16)
                    sp.dma_start(lasti, io["gnn_dst_ends"].partition_broadcast(T)).then_inc(s_idx, 16)
                    x_v = io["x"].rearrange("(t p) d -> p t d", p=P)
                    for k in range(XP):
                        n = T // XP
                        sp.dma_start(X[:, k * n:(k + 1) * n, :], x_v[:, k * n:(k + 1) * n, :]).then_inc(s_x[k], 16)
                    sp.dma_start(wlr1[:], io["wlr1"]).then_inc(load, 16)
                    sp.dma_start(wlr2[:], io["wlr2"]).then_inc(load, 16)
                    sp.dma_start(rows[:], io["rows"].partition_broadcast(P)).then_inc(load, 16)
                    with sp.Fori(0, T) as t:
                        sp.wait_ge(*A["rev"].done(t))
                        sp.sem_inc(a_turns, 1)
                        sp.wait_ge(*AD["stR"].before(t))
                        sp.sem_inc(a_turns, 1)
                        sp.dma_start(tile_rows(own[0], t), flat(rs[:, bass.ds(t % 2, 1), :])).then_inc(AD["stR"].sem, 16)
                        sp.wait_ge(*A["split"].done(t))
                        sp.sem_inc(a_turns, 1)
                        sp.wait_ge(*AD["stU"].before(t))
                        sp.sem_inc(a_turns, 1)
                        sp.dma_start(tile_rows(table[0], t), flat(us[:, bass.ds((t % 2) * 3, 3), :])).then_inc(AD["stU"].sem, 16)
                    sp.wait_ge(s_ready, 3)
                    sp.dma_start(windows_d[0:1, :], zi[:]).then_inc(s_out, 16)
                    sp.dma_start(windows_d[1:T + 1, :], endi[:]).then_inc(s_out, 16)
                    sp.dma_start(degrees_d[:, :], mdi[:]).then_inc(s_out, 16)
                    sp.wait_ge(s_out, 48)
                    sp.dma_start(wtab[:], windows_d.rearrange("t o -> o t")).then_inc(s_out, 16)
                    sp.dma_start(dtab[:], degrees_d.rearrange("t o -> o t")).then_inc(s_out, 16)
                    sp.wait_ge(s_out, 80)
                    for s in AD.values():
                        sp.wait_ge(s.sem, (T + 2) * 16)

                @block.gpsimd
                def _(pool):
                    A["split"].start(pool)
                    pool.wait_ge(s_ready, 1)
                    pool.indirect_dma_start(out=iend, out_offset=None, in_=io["gnn_dst"].rearrange("o (c p) -> (o c) p", p=P),
                                            in_offset=bass.IndirectOffsetOnAxis(ap=cei[:], axis=0)).then_inc(s_endrow, 16)
                    with pool.Fori(0, T) as t:
                        pool.wait_ge(*A["mid"].done(t))
                        pool.tensor_tensor(us[:, bass.ds((t % 2) * 3 + 2, 1), :], ur[:, bass.ds(t % 2, 1), :],
                                           us[:, bass.ds((t % 2) * 3 + 1, 1), :], ALU.subtract).then_inc(A["split"].sem, 1)

                @block.scalar
                def _(act):
                    for s in ("xn", "xTs", "hi", "mid"):
                        A[s].start(act)
                    act.wait_ge(s_idx, 49)
                    act.activation(ident16[:], c("ident"), ACT.Copy).then_inc(setup, 1)
                    act.wait_ge(chain, 4 + A_IDX)
                    act.activation(tmp[:], var[:], ACT.Sqrt, bias=c("eps")).then_inc(s_std, 1)
                    act.wait_ge(chain, 6 + A_IDX)

                    def normalise(t):
                        act.wait_ge(*A["xnT"].before(t))
                        act.activation(xs[:], flat(X[:, bass.ds(t, 1), :]), ACT.Identity, bias=nmr[:, bass.ds(t, 1)],
                                       scale=rstd[:, bass.ds(t, 1)]).then_inc(A["xn"].sem, 1)

                    def turned(t):
                        act.wait_ge(*A["xnT"].done(t))
                        act.wait_ge(*A["ur"].before(t))
                        act.activation(flat(xT[:]), bT[:, 0:D], ACT.Copy).then_inc(A["xTs"].sem, 1)

                    def high(t, i):
                        act.wait_ge(*A["rev"].done(t))
                        act.wait_ge(*AD["stU"].before2(t))
                        act.activation(flat(us[:, bass.ds(i * 3, 1), :]), bUR[i][:, 0:D], ACT.Copy).then_inc(A["hi"].sem, 1)

                    def middle(t, i):
                        act.wait_ge(*A["r1"].done(t))
                        act.activation(flat(us[:, bass.ds(i * 3 + 1, 1), :]), flat(ur[:, bass.ds(i, 1), :]), ACT.Copy).then_inc(A["mid"].sem, 1)

                    normalise(0)
                    turned(0)
                    normalise(1)
                    turned(1)
                    normalise(2)
                    high(0, 0)

                    def turn(t, i, more):
                        turned(t)
                        if more:
                            normalise(t + 1)
                        high(t - 1, 1 - i)
                        middle(t - 2, i)
                    with act.Fori(1, T // 2 - 1) as t2:
                        turn(t2 * 2, 0, True)
                        turn(t2 * 2 + 1, 1, True)
                    turn(T - 2, 0, True)
                    turn(T - 1, 1, False)
                    high(T - 1, 1)
                    middle(T - 2, 0)
                    middle(T - 1, 1)

                @block.tensor
                def _(pe):
                    for s in ("xnT", "ur", "hist"):
                        A[s].start(pe)
                    pe.wait_ge(load, 48)
                    pe.wait_ge(setup, 1)
                    pe.wait_ge(s_idx, 49)
                    pe.matmul(bC[:, 0:T], zeros16[:, 0:P], zeros16[:, 0:T], start=True, stop=False, skip_group_check=True)
                    with pe.Fori(0, T // 2) as t2:
                        for i in range(2):
                            t = t2 * 2 + i
                            pe.wait_ge(*A["xn"].done(t))
                            pe.wait_ge(*A["xTs"].before(t))
                            for j in range(2):
                                last = pe.transpose(bT[:, j * P:(j + 1) * P], xs[:, j * P:(j + 1) * P], c("ident"))
                            last.then_inc(A["xnT"].sem, 1)
                            pe.wait_ge(*A["onehot"].done(t))
                            for k in range(HB):
                                last = pe.matmul(bC[:, 0:T], Olo[:, i, k, :], Ohi[:, i, k, :], start=False, stop=False, skip_group_check=True)
                            last.then_inc(A["hist"].sem, 1)
                            pe.wait_ge(*A["xTs"].done(t))
                            pe.wait_ge(*A["r1"].before2(t))
                            for j in range(2):
                                last = pe.matmul(bUR[i][:], xT[:, j, :], wlr1[:, j, :], start=(j == 0), stop=(j == 1))
                            last.then_inc(A["ur"].sem, 1)
                    pe.wait_ge(s_pre, 1)
                    pe.matmul(bP[:, 0:T], c("before"), deg[:], start=True, stop=True)
                    pe.matmul(bP[:, T:2 * T], c("ones"), deg[:], start=True, stop=True)
                    pe.transpose(bQ[0:T, 0:P], deg[:], c("ident")).then_inc(s_tr, 1)

                @block.vector
                def _(dve):
                    for s in ("r1", "rev", "onehot"):
                        A[s].start(dve)
                    n = [0]

                    def link(ins):
                        n[0] += 1
                        ins.then_inc(chain, 1)
                        dve.wait_ge(chain, n[0])
                    dve.memset(zeros16[:], 0.0)
                    dve.memset(ones16[:], 1.0)
                    dve.memset(zi[:], 0).then_inc(s_idx, 1)
                    dve.wait_ge(s_idx, 49)
                    dve.tensor_copy(lastd[:], lasti)
                    dve.tensor_scalar(ilo, ifd, 127, None, ALU.bitwise_and)
                    link(dve.tensor_scalar(ihi, ifd, 7, None, ALU.logical_shift_right))
                    dve.tensor_copy(fdst[:], ifd)
                    dve.tensor_copy(flo[:], ilo)
                    link(dve.tensor_copy(fhi[:], ihi))
                    link(dve.tensor_scalar(lastd[:], lastd[:], c("wend")[0:T], None, ALU.is_lt, ALU.add, accum_out=cef[:]))
                    dve.tensor_copy(cei[:], cef[:]).then_inc(s_ready, 1)
                    for k in range(XP):
                        dve.wait_ge(s_x[k], 16)
                        with dve.Fori(k * (T // XP), (k + 1) * (T // XP)) as t:
                            dve.bn_stats(flat(stat[:, bass.ds(t, 1), :]), flat(X[:, bass.ds(t, 1), :])).then_inc(s_bn, 1)
                    dve.wait_ge(s_bn, T)
                    link(dve.tensor_tensor(mean[:], stat[:, :, 1], stat[:, :, 4], ALU.add))
                    dve.tensor_tensor(tmp[:], stat[:, :, 1], stat[:, :, 4], ALU.subtract)
                    link(dve.tensor_tensor(var[:], stat[:, :, 2], stat[:, :, 5], ALU.add))
                    link(dve.scalar_tensor_tensor(tmp[:], tmp[:], 0.25, tmp[:], ALU.mult, ALU.mult))
                    link(dve.scalar_tensor_tensor(var[:], var[:], 1.0 / D, tmp[:], ALU.mult, ALU.add))
                    dve.wait_ge(s_std, 1)
                    link(dve.reciprocal(rstd[:], tmp[:]))
                    link(dve.scalar_tensor_tensor(nmr[:], mean[:], -0.5, rstd[:], ALU.mult, ALU.mult))

                    def count_lo(t, i):
                        dve.wait_ge(*A["hist"].before2(t))
                        dve.tensor_tensor(Olo[:, i], c("iota").unsqueeze(1).broadcast_to([P, HB, P]),
                                          flo[:, bass.ds(t * HB, HB)].unsqueeze(2).broadcast_to([P, HB, P]), ALU.is_equal)

                    def count_hi(t, i):
                        dve.tensor_tensor(Ohi[:, i], c("iota")[:, 0:T].unsqueeze(1).broadcast_to([P, HB, T]),
                                          fhi[:, bass.ds(t * HB, HB)].unsqueeze(2).broadcast_to([P, HB, T]), ALU.is_equal)\
                           .then_inc(A["onehot"].sem, 1)

                    def evict(t, i, more):
                        dve.wait_ge(*A["ur"].done(t))
                        dve.wait_ge(*AD["stR"].before2(t))
                        dve.tensor_tensor(rs[:, i], bUR[i][:, D:2 * D], r("gnn_b1"), ALU.add).then_inc(A["rev"].sem, 1)
                        if more:
                            count_lo(t + 2, i)
                        dve.wait_ge(*A["hi"].done(t))
                        dve.wait_ge(*A["split"].before2(t))
                        dve.tensor_tensor(ur[:, i], bUR[i][:, 0:D], us[:, i * 3, :], ALU.subtract).then_inc(A["r1"].sem, 1)
                        if more:
                            count_hi(t + 2, i)

                    for t in range(2):
                        count_lo(t, t)
                        count_hi(t, t)
                    dve.wait_ge(load, 48)
                    with dve.Fori(0, T // 2 - 1) as t2:
                        for i in range(2):
                            evict(t2 * 2 + i, i, True)
                    evict(T - 2, 0, False)
                    evict(T - 1, 1, False)
                    dve.wait_ge(s_endrow, 16)
                    link(dve.tensor_copy(endrow[:], iend))
                    link(dve.tensor_scalar(endrow[:], endrow[:], c("wend")[0:T], None, ALU.is_lt, ALU.add, accum_out=inend[:]))
                    link(dve.scalar_tensor_tensor(endf[:], cef[:], float(P), inend[:], ALU.mult, ALU.add))
                    dve.tensor_copy(endi[:], endf[:]).then_inc(s_ready, 1)
                    dve.wait_ge(A["hist"].sem, T + 2)
                    dve.tensor_copy(deg[:], bC[:, 0:T]).then_inc(s_pre, 1)
                    dve.wait_ge(s_tr, 1)
                    dve.tensor_reduce(mdi[:], bQ[0:T, 0:P], AX.X, ALU.max).then_inc(s_ready, 1)
                    link(dve.memset(sc[0][:, 0:1], 0.0))
                    link(dve.tensor_copy(sc[0][:, 1:T], bP[:, T:2 * T - 1]))
                    link(dve.tensor_copy(part[:], bP[:, 0:T]))
                    a_, b_ = sc
                    k = 1
                    while k < T:
                        dve.tensor_copy(b_[:, 0:k], a_[:, 0:k])
                        link(dve.tensor_tensor(b_[:, k:T], a_[:, k:T], a_[:, 0:T - k], ALU.add))
                        a_, b_ = b_, a_
                        k *= 2
                    dve.memset(first[:, T:T + 2], 0.0)
                    link(dve.tensor_tensor(first[:, 0:T], part[:], a_[:], ALU.add))
                    over = [b_[0:1, 0:T], a_[0:1, 0:T]]
                    dve.wait_ge(s_out, 80)
                    dve.tensor_tensor(over[0], wtab[:, 1:T + 1], wtab[:, 0:T], ALU.subtract).then_inc(s_over, 1)
                    dve.wait_ge(s_over, 1)
                    dve.tensor_scalar(over[1], over[0], float(P * K), 0.0, ALU.subtract, ALU.max).then_inc(s_over, 1)
                    dve.wait_ge(s_over, 2)
                    dve.tensor_copy(xtab[:], over[1]).then_inc(s_over, 1)
                    dve.wait_ge(s_over, 3)
        clear_semaphores()
        if upto <= 1:
            return

        def gather_state(stack, prefix):
            G = {"ring": sbuf(stack, f"{prefix}ring", [P, 2, K, SLOT], BF16),
                 "hot": sbuf(stack, f"{prefix}hot", [P, 2 * K, P], BF16),
                 "src": sbuf(stack, f"{prefix}src", [P, 2 * K], I32),
                 "dst": sbuf(stack, f"{prefix}dst", [P, 2 * K], I32),
                 "rel": sbuf(stack, f"{prefix}rel", [P, K], F32),
                 "landed": [[sem(f"{prefix}landed{i}{g}") for g in range(NG)] for i in range(2)],
                 "have_src": sem(f"{prefix}have_src"), "have_dst": sem(f"{prefix}have_dst"),
                 "rel_s": Step(sem(f"{prefix}rel")), "hot_s": Step(sem(f"{prefix}onehot")),
                 "used": sem(f"{prefix}used"), "go": sem(f"{prefix}go"), "sp_go": sem(f"{prefix}sp_go"),
                 "sum": Step(sem(f"{prefix}sum")),
                 "ones_s": sem(f"{prefix}ones_set"),
                 "xring": sbuf(stack, f"{prefix}xring", [P, KX, SLOT], BF16),
                 "xhot": sbuf(stack, f"{prefix}xhot", [P, KX, P], BF16),
                 "xsrc": sbuf(stack, f"{prefix}xsrc", [P, KX], I32),
                 "xdst": sbuf(stack, f"{prefix}xdst", [P, KX], I32),
                 "xrel": sbuf(stack, f"{prefix}xrel", [P, KX], F32),
                 "xhave_src": sem(f"{prefix}xhave_src"), "xhave_dst": sem(f"{prefix}xhave_dst"),
                 "xlanded": sem(f"{prefix}xlanded"), "xrel_s": sem(f"{prefix}xrel"),
                 "xhot_s": sem(f"{prefix}xonehot"), "xused": Step(sem(f"{prefix}xused"))}
            return G

        def edges_over(eng, w):
            return eng.value_load(xtab[0:1, bass.ds(w, 1)], min_val=0, max_val=GE)

        def extra_rounds(eng, seen, over, body):
            with eng.If(over > 0):
                with eng.Fori(0, (over + (P * KX - 1)) // (P * KX)) as k:
                    body(k, eng.snap(seen, min_val=0, max_val=GE))
                    eng.reg_add(seen, seen, 1)

        def counter(eng, name):
            seen = eng.alloc_register(name)
            eng.reg_mov(seen, 0)
            return seen

        def gather_sync(sp, G, prefix):
            seen = counter(sp, f"{prefix}sp_rounds")
            at_round = counter(sp, f"{prefix}sp_at")

            def edges(name, at, k):
                return io[name][0:1, bass.ds(at, P * k)].rearrange("o (p c) -> (o p) c", p=P)

            def stage(i, w, turn):
                at = sp.value_load(wtab[0:1, bass.ds(w, 1)], min_val=0, max_val=GE)
                if turn is not None:
                    for g in range(NG):
                        sp.wait_ge(G["landed"][i][g], turn * KG * 16)
                    sp.sem_inc(G["sp_go"], 1)
                    sp.wait_ge(*G["hot_s"].before(w - 1))
                    sp.sem_inc(G["sp_go"], 1)
                    sp.wait_ge(G["have_src"], w * 16)
                    sp.wait_ge(G["have_dst"], w * 16)
                elif i:
                    sp.wait_ge(G["have_src"], 16)
                    sp.wait_ge(G["have_dst"], 16)
                sp.sem_inc(G["sp_go"], 1)
                sp.dma_start(G["src"][:, i * K:(i + 1) * K], edges("gnn_src", at, K)).then_inc(G["have_src"], 16)
                sp.dma_start(G["dst"][:, i * K:(i + 1) * K], edges("gnn_dst", at, K)).then_inc(G["have_dst"], 16)

            def extra(w):
                at = sp.value_load(wtab[0:1, bass.ds(w, 1)], min_val=0, max_val=GE)

                def body(k, n):
                    sp.wait_ge(*G["xused"].before(n))
                    sp.sem_inc(G["sp_go"], 1)
                    sp.reg_mov(at_round, sp.snap(at + k * (P * KX) + P * K))
                    place = sp.snap(at_round, min_val=0, max_val=GE)
                    sp.dma_start(G["xsrc"][:], edges("gnn_src", place, KX)).then_inc(G["xhave_src"], 16)
                    sp.dma_start(G["xdst"][:], edges("gnn_dst", place, KX)).then_inc(G["xhave_dst"], 16)
                    sp.wait_ge(G["xhave_src"], (n + 1) * 16)
                    sp.wait_ge(G["xhave_dst"], (n + 1) * 16)
                    sp.sem_inc(G["sp_go"], 1)
                extra_rounds(sp, seen, edges_over(sp, w), body)

            stage(0, 0, None)
            stage(1, 1, None)
            extra(0)
            with sp.Fori(1, T // 2) as t2:
                for i in range(2):
                    stage(i, t2 * 2 + i, t2)
                    extra(t2 * 2 + i - 1)
            extra(T - 1)
            sp.wait_ge(G["have_src"], T * 16)
            sp.wait_ge(G["have_dst"], T * 16)

        def gather_pool(pool, G, tab, prefix):
            seen = counter(pool, f"{prefix}pool_rounds")

            def gather(out, idx, s):
                pool.indirect_dma_start(out=out, out_offset=None, in_=tab,
                                        in_offset=bass.IndirectOffsetOnAxis(ap=idx, axis=0)).then_inc(s, 16)

            def body(k, n):
                pool.wait_ge(G["xhave_src"], (n + 1) * 16)
                pool.sem_inc(G["go"], 1)
                for x in range(KX):
                    gather(G["xring"][:, x, 0:CHUNK_W], G["xsrc"][:, x:x + 1], G["xlanded"])

            pool.wait_ge(G["ones_s"], 1)
            with pool.Fori(0, T // 2) as t2:
                for i in range(2):
                    w = t2 * 2 + i
                    over = edges_over(pool, w)
                    pool.wait_ge(G["have_src"], (w + 1) * 16)
                    pool.wait_ge(G["used"], w + 1)
                    pool.sem_inc(G["go"], 1)
                    for k in range(K):
                        gather(G["ring"][:, i, k, 0:CHUNK_W], G["src"][:, i * K + k:i * K + k + 1], G["landed"][i][k // KG])
                    extra_rounds(pool, seen, over, body)

        def hot_start(dve, G):
            dve.memset(G["ring"][:, :, :, CHUNK_W:SLOT], 1.0)
            dve.memset(G["xring"][:, :, CHUNK_W:SLOT], 1.0).then_inc(G["ones_s"], 1)
            G["rel_s"].start(dve)
            G["hot_s"].start(dve)

        def onehots(dve, G, w):
            at = (w % 2) * K
            dve.wait_ge(G["have_dst"], (w + 1) * 16)
            dve.wait_ge(*G["hot_s"].before(w))
            dve.tensor_scalar(G["rel"][:], G["dst"][:, bass.ds(at, K)], c("wbase")[:, bass.ds(w, 1)], None, ALU.add)\
               .then_inc(G["rel_s"].sem, 1)
            dve.wait_ge(*G["rel_s"].done(w))
            dve.wait_ge(G["used"], w + 1)
            dve.tensor_tensor(G["hot"][:, bass.ds(at, K), :], c("iota").unsqueeze(1).broadcast_to([P, K, P]),
                              G["rel"][:].unsqueeze(2).broadcast_to([P, K, P]), ALU.is_equal).then_inc(G["hot_s"].sem, 1)

        def extra_onehots(dve, G, seen, w, over):
            def body(k, n):
                dve.wait_ge(G["xhave_dst"], (n + 1) * 16)
                dve.wait_ge(*G["xused"].before(n))
                dve.tensor_scalar(G["xrel"][:], G["xdst"][:], c("wbase")[:, bass.ds(w, 1)], None, ALU.add).then_inc(G["xrel_s"], 1)
                dve.wait_ge(G["xrel_s"], n + 1)
                dve.tensor_tensor(G["xhot"][:], c("iota").unsqueeze(1).broadcast_to([P, KX, P]),
                                  G["xrel"][:].unsqueeze(2).broadcast_to([P, KX, P]), ALU.is_equal).then_inc(G["xhot_s"], 1)
            extra_rounds(dve, seen, over, body)

        def add_rows(pe, hot, row, first_one):
            pe.matmul(bAGG[:, 0:D + 1], hot, row[:, 2 * D:3 * D + 1], start=first_one, stop=False, skip_group_check=True)
            pe.matmul(bAGG[:, 0:D], hot, row[:, 0:D], start=False, stop=False, skip_group_check=True)
            return pe.matmul(bAGG[:, 0:D], hot, row[:, D:2 * D], start=False, stop=False, skip_group_check=True)

        def aggregate(pe, G, w, i, turn, g):
            if g == 0:
                pe.wait_ge(*G["evict"].before(w))
                pe.wait_ge(*G["hot_s"].done(w))
            pe.wait_ge(G["landed"][i][g], (turn + 1) * KG * 16)
            for k in range(g * KG, (g + 1) * KG):
                last = add_rows(pe, G["hot"][:, i * K + k, :], G["ring"][:, i, k, :], k == 0)
            if g == NG - 1:
                last.then_inc(G["used"], 1)

        def aggregate_end(pe, G, seen, w, over):
            def body(k, n):
                pe.wait_ge(G["xhot_s"], n + 1)
                pe.wait_ge(G["xlanded"], (n + 1) * KX * 16)
                for x in range(KX):
                    last = add_rows(pe, G["xhot"][:, x, :], G["xring"][:, x, :], False)
                last.then_inc(G["xused"].sem, 1)
            extra_rounds(pe, seen, over, body)
            pe.matmul(bAGG[:, D:D + 1], zeros16[:, 0:P], zeros16[:, 0:1], start=False, stop=True, skip_group_check=True)\
                .then_inc(G["sum"].sem, 1)

        def gather_start(pe, G):
            G["sum"].start(pe)
            G["xused"].start(pe)
            pe.sem_inc(G["used"], 2)

        def over_windows(eng, body):
            with eng.Fori(0, T - 2) as w:
                body(w, w + 1, True)
            body(T - 2, T - 1, False)
            body(T - 1, None, False)

        def rank_state(stack, prefix, n):
            R = {"n": n, "count": sbuf(stack, f"{prefix}count", [P, T], F32)}
            R["b"] = [dict(
                lo=sbuf(stack, f"{prefix}lo{b}", [P, RB, P], BF16), hi=sbuf(stack, f"{prefix}hi{b}", [P, RB, T], BF16),
                loT=sbuf(stack, f"{prefix}loT{b}", [P, RB * P], F32), row=sbuf(stack, f"{prefix}row{b}", [P, RB * P], I32),
                near=sbuf(stack, f"{prefix}near{b}", [P, RB], F32), far=sbuf(stack, f"{prefix}far{b}", [P, RB], F32),
                prod=sbuf(stack, f"{prefix}prod{b}", [P, RB, T], F32), eq=sbuf(stack, f"{prefix}eq{b}", [P, RB * (RB + 1) // 2 * P], BF16),
                s=steps(f"{prefix}rank{b}", ["hot", "count", "turned", "loT", "far", "counted", "prod", "farsum", "near", "pos"]),
                row_in=Step(sem(f"{prefix}row_in{b}"), 16)) for b in range(n)]
            return R

        def rank_start(eng, R, names):
            for B in R["b"]:
                for nme in names:
                    B["s"][nme].start(eng)

        def rank_hot(dve, R, b, w, batch):
            B, s = R["b"][b], R["b"][b]["s"]
            dve.wait_ge(*s["counted"].before(w))
            dve.tensor_tensor(B["lo"][:], c("iota").unsqueeze(1).broadcast_to([P, RB, P]),
                              flo[:, bass.ds(batch * RB, RB)].unsqueeze(2).broadcast_to([P, RB, P]), ALU.is_equal)
            dve.tensor_tensor(B["hi"][:], c("iota")[:, 0:T].unsqueeze(1).broadcast_to([P, RB, T]),
                              fhi[:, bass.ds(batch * RB, RB)].unsqueeze(2).broadcast_to([P, RB, T]), ALU.is_equal)\
               .then_inc(s["hot"].sem, 1)

        def rank_base(dve, R, b, w):
            s = R["b"][b]["s"]
            prev = R["b"][b - 1]["s"]["counted"].done(w) if b else R["b"][-1]["s"]["counted"].before(w)
            dve.wait_ge(*prev)
            dve.tensor_tensor(R["count"][:], bC[:, 0:T], first[:, 0:T], ALU.add).then_inc(s["count"].sem, 1)

        def rank_turn(pe, R, b, w):
            B, s = R["b"][b], R["b"][b]["s"]
            pe.wait_ge(*s["hot"].done(w))
            pe.wait_ge(*(R["b"][b - 1]["s"]["loT"].done(w) if b else R["b"][-1]["s"]["loT"].before(w)))
            for k in range(RB):
                last = pe.transpose(bOT[:, k * P:(k + 1) * P], B["lo"][:, k, :], ident16[:])
            last.then_inc(s["turned"].sem, 1)

        def rank_turned(act, R, b, w):
            B, s = R["b"][b], R["b"][b]["s"]
            act.wait_ge(*s["turned"].done(w))
            act.wait_ge(*s["far"].before(w))
            act.activation(B["loT"][:], bOT[:, 0:RB * P], ACT.Copy).then_inc(s["loT"].sem, 1)

        def rank_count(pe, R, b, w):
            B, s = R["b"][b], R["b"][b]["s"]
            pe.wait_ge(*s["loT"].done(w))
            pe.wait_ge(*s["count"].done(w))
            pe.wait_ge(*(R["b"][b - 1]["s"]["prod"].done(w) if b else R["b"][-1]["s"]["prod"].before(w)))
            for k in range(RB):
                last = pe.matmul(bP[:, k * T:(k + 1) * T], B["loT"][:, k * P:(k + 1) * P], R["count"][:], start=True, stop=True, skip_group_check=True)
            last.then_inc(s["far"].sem, 1)
            for k in range(RB):
                last = pe.matmul(bC[:, 0:T], B["lo"][:, k, :], B["hi"][:, k, :], start=False, stop=False, skip_group_check=True)
            last.then_inc(s["counted"].sem, 1)

        def rank_near(dve, R, b, w, batch):
            B, s = R["b"][b], R["b"][b]["s"]
            dve.wait_ge(*B["row_in"].done(w))
            dve.wait_ge(*s["pos"].before(w))
            for k in range(RB):
                n = (k + 1) * P
                at = k * (k + 1) // 2 * P
                last = dve.scalar_tensor_tensor(B["eq"][:, at:at + n], B["row"][:, 0:n], fdst[:, bass.ds(batch * RB + k, 1)],
                                                c("rankmask")[:, k * RB * P:k * RB * P + n], ALU.is_equal, ALU.mult,
                                                accum_out=B["near"][:, k:k + 1])
            last.then_inc(s["near"].sem, 1)

        def rank_place(dve, R, b, w, batch):
            B, s = R["b"][b], R["b"][b]["s"]
            dve.wait_ge(*s["far"].done(w))
            dve.tensor_tensor(flat(B["prod"][:]), bP[:, 0:RB * T], flat(B["hi"][:]), ALU.mult).then_inc(s["prod"].sem, 1)
            dve.wait_ge(*s["prod"].done(w))
            dve.tensor_reduce(B["far"][:], B["prod"][:], AX.X, ALU.add).then_inc(s["farsum"].sem, 1)
            dve.wait_ge(*s["farsum"].done(w))
            dve.wait_ge(*s["near"].done(w))
            dve.tensor_tensor(pos[:, bass.ds(batch * RB, RB)], B["near"][:], B["far"][:], ALU.add).then_inc(s["pos"].sem, 1)

        def rank_load(act, R, b, w, batch):
            B, s = R["b"][b], R["b"][b]["s"]
            act.wait_ge(*s["near"].before(w))
            act.dma_start(B["row"][:], io["ffn_dst_rows"][0:1, bass.ds(batch * RB * P, RB * P)].partition_broadcast(P))\
                .then_inc(B["row_in"].sem, 16)

        DVE_RANK = ("hot", "count", "prod", "farsum", "near", "pos")
        PE_RANK = ("turned", "far", "counted")

        with ExitStack() as b:
            G = gather_state(b, "b_")
            R = rank_state(b, "b_", RB1)
            wkv = sbuf(b, "wkv", [P, 2, 2 * D], F32)
            wq = sbuf(b, "wq", [P, 2, D], F32)
            xw = sbuf(b, "xw", [P, D], F32)
            xT = sbuf(b, "xT_b", [P, 2 * P], F32)
            r1 = sbuf(b, "r1", [P, D], F32)
            dg = sbuf(b, "dg", [P, 1], F32)
            rinv = sbuf(b, "rinv", [P, 1], F32)
            h0 = sbuf(b, "h0", [P, D], F32)
            hh = sbuf(b, "hh", [P, D], F32)
            hT = sbuf(b, "hT", [P, 2 * P], F32)
            km = sbuf(b, "km", [P, D], F32)
            ke = sbuf(b, "ke", [P, D], F32)
            kf = sbuf(b, "kf", [P, D], F32)
            vx = sbuf(b, "vx", [P, 2, P + 1], F32)
            qm = sbuf(b, "qm", [P, D], F32)
            qe = sbuf(b, "qe", [P, D], F32)
            qf = sbuf(b, "qf", [P, D], F32)
            ur = sbuf(b, "ur_b", [P, D], F32)
            us = sbuf(b, "us_b", [P, 3, D], BF16)
            rs = sbuf(b, "rs_b", [P, D], F32)
            S = steps("b", ["xs", "xTp", "xT", "kv", "q", "km", "qm", "vx", "ke", "qe", "kf", "qf", "KV", "dg", "rinv", "h0", "h",
                            "hTp", "hT", "ur", "rs", "hi", "r1", "mid", "lo"])
            SD = steps("b", ["inx", "inR", "outq", "outU", "outR"], 16)
            b_load = sem("b_load")
            G["evict"] = S["h0"]
            with nc.Block() as block:
                @block.gpsimd
                def _(pool):
                    gather_pool(pool, G, table[0], "b_")

                @block.sync
                def _(sp):
                    sp.dma_start(wkv[:], io["wkv"]).then_inc(b_load, 16)
                    sp.dma_start(wq[:], io["wq"]).then_inc(b_load, 16)
                    gather_sync(sp, G, "b_")

                @block.scalar
                def _(act):
                    for n in ("xs", "xT", "ke", "qe", "h", "hT", "hi", "mid"):
                        S[n].start(act)
                    for s in SD.values():
                        s.start(act)
                    for B in R["b"]:
                        B["row_in"].start(act)
                    rank_start(act, R, ("loT",))

                    def load_x(t):
                        act.wait_ge(*S["xs"].before(t))
                        act.dma_start(xw[:], tile_rows(io["x"], t)).then_inc(SD["inx"].sem, 16)

                    def load_own(t):
                        act.wait_ge(*S["h0"].before(t))
                        act.dma_start(r1[:], tile_rows(own[0], t)).then_inc(SD["inR"].sem, 16)

                    def normalise(t):
                        act.wait_ge(*S["xTp"].before(t))
                        act.wait_ge(*SD["inx"].done(t))
                        act.activation(xs[:], xw[:], ACT.Identity, bias=nmr[:, bass.ds(t, 1)],
                                       scale=rstd[:, bass.ds(t, 1)]).then_inc(S["xs"].sem, 1)

                    def turned(t):
                        act.wait_ge(*S["xTp"].done(t))
                        act.wait_ge(*S["q"].before(t))
                        act.activation(xT[:], bT[:, 0:D], ACT.Copy).then_inc(S["xT"].sem, 1)

                    def body(w, v, more):
                        if v is not None:
                            load_x(v)
                        act.wait_ge(*S["h0"].done(w))
                        act.wait_ge(*S["hTp"].before(w))
                        act.activation(hh[:], h0[:], ACT.Relu).then_inc(S["h"].sem, 1)
                        if v is not None:
                            load_own(v)
                        act.wait_ge(*S["km"].done(w))
                        act.activation(ke[:], km[:], ACT.Exp).then_inc(S["ke"].sem, 1)
                        act.wait_ge(*S["qm"].done(w))
                        act.activation(qe[:], qm[:], ACT.Exp).then_inc(S["qe"].sem, 1)
                        rank_turned(act, R, 0, w)
                        act.wait_ge(*S["hTp"].done(w))
                        act.activation(hT[:], bT[:, 0:D], ACT.Copy).then_inc(S["hT"].sem, 1)
                        if v is not None:
                            normalise(v)
                        act.wait_ge(*S["qf"].done(w))
                        act.dma_start(qT_d[bass.ds(w, 1)].rearrange("t p d -> (t p) d"), qf[:]).then_inc(SD["outq"].sem, 16)
                        rank_turned(act, R, 1, w)
                        if v is not None:
                            turned(v)
                            rank_load(act, R, 0, v, v * RB1)
                        act.wait_ge(*S["rs"].done(w))
                        act.wait_ge(*SD["outU"].before(w))
                        act.activation(us[:, 0, :], bMM[:, 0:D], ACT.Copy).then_inc(S["hi"].sem, 1)
                        act.dma_start(tile_rows(own[1], w), rs[:]).then_inc(SD["outR"].sem, 16)
                        act.wait_ge(*S["r1"].done(w))
                        act.activation(us[:, 1, :], ur[:], ACT.Copy).then_inc(S["mid"].sem, 1)
                        act.wait_ge(*S["mid"].done(w))
                        act.wait_ge(*S["lo"].done(w))
                        act.dma_start(tile_rows(table[1], w), flat(us[:])).then_inc(SD["outU"].sem, 16)
                        if v is not None:
                            rank_load(act, R, 1, v, v * RB1 + 1)

                    load_x(0)
                    load_own(0)
                    rank_load(act, R, 0, 0, 0)
                    rank_load(act, R, 1, 0, 1)
                    normalise(0)
                    turned(0)
                    over_windows(act, body)
                    for s in SD.values():
                        act.wait_ge(s.sem, (T + 1) * 16)

                @block.tensor
                def _(pe):
                    for n in ("xTp", "kv", "q", "KV", "hTp", "ur"):
                        S[n].start(pe)
                    rank_start(pe, R, ("turned", "far"))
                    R["b"][0]["s"]["counted"].start(pe)
                    gather_start(pe, G)
                    seen = counter(pe, "b_pe_rounds")
                    pe.wait_ge(b_load, 32)
                    pe.matmul(bC[:, 0:T], zeros16[:, 0:P], zeros16[:, 0:T], start=True, stop=False, skip_group_check=True)\
                        .then_inc(R["b"][-1]["s"]["counted"].sem, 1)
                    pe.matmul(bKV[:, 0:2 * (P + 1)], zeros16[:, 0:P], zeros16[:, 0:2 * (P + 1)], start=True, stop=False, skip_group_check=True)

                    def turn_x(t):
                        pe.wait_ge(*S["xs"].done(t))
                        pe.wait_ge(*S["hT"].before(t))
                        for j in range(2):
                            last = pe.transpose(bT[:, j * P:(j + 1) * P], xs[:, j * P:(j + 1) * P], c("ident"))
                        last.then_inc(S["xTp"].sem, 1)

                    def body(w, v, i, turn):
                        over = edges_over(pe, v) if v is not None else None
                        pe.wait_ge(*S["xT"].done(w))
                        pe.wait_ge(*S["r1"].before(w))
                        for j in range(2):
                            last = pe.matmul(bMM[:], xT[:, j * P:(j + 1) * P], wkv[:, j, :], start=(j == 0), stop=(j == 1))
                        last.then_inc(S["kv"].sem, 1)
                        pe.wait_ge(*S["qf"].before(w))
                        for o in range(2):
                            for j in range(2):
                                last = pe.matmul(bQ[:, o * P:(o + 1) * P], wq[:, j, o * P:(o + 1) * P],
                                                 xT[:, j * P:(j + 1) * P], start=(j == 0), stop=(j == 1))
                        last.then_inc(S["q"].sem, 1)
                        if v is not None:
                            aggregate(pe, G, v, i, turn, 0)
                        rank_turn(pe, R, 0, w)
                        pe.wait_ge(*S["h"].done(w))
                        for j in range(2):
                            last = pe.transpose(bT[:, j * P:(j + 1) * P], hh[:, j * P:(j + 1) * P], c("ident"))
                        last.then_inc(S["hTp"].sem, 1)
                        if v is not None:
                            aggregate(pe, G, v, i, turn, 1)
                        rank_count(pe, R, 0, w)
                        pe.wait_ge(*S["kf"].done(w))
                        pe.wait_ge(*S["vx"].done(w))
                        for j in range(2):
                            last = pe.matmul(bKV[:, j * (P + 1):(j + 1) * (P + 1)], kf[:, j * P:(j + 1) * P], vx[:, j, :],
                                             start=False, stop=False, skip_group_check=True)
                        last.then_inc(S["KV"].sem, 1)
                        pe.wait_ge(*S["hT"].done(w))
                        for j in range(2):
                            last = pe.matmul(bMM[:], hT[:, j * P:(j + 1) * P], wlr2[:, j, :], start=(j == 0), stop=(j == 1))
                        last.then_inc(S["ur"].sem, 1)
                        rank_turn(pe, R, 1, w)
                        if v is not None:
                            turn_x(v)
                            aggregate(pe, G, v, i, turn, 2)
                        rank_count(pe, R, 1, w)
                        if v is not None:
                            aggregate_end(pe, G, seen, v, over)

                    turn_x(0)
                    for g in range(NG):
                        aggregate(pe, G, 0, 0, 0, g)
                    aggregate_end(pe, G, seen, 0, edges_over(pe, 0))
                    with pe.Fori(0, T // 2 - 1) as t2:
                        body(t2 * 2, t2 * 2 + 1, 1, t2)
                        body(t2 * 2 + 1, t2 * 2 + 2, 0, t2 + 1)
                    body(T - 2, T - 1, 1, T // 2 - 1)
                    body(T - 1, None, None, None)

                @block.vector
                def _(dve):
                    for n in ("km", "qm", "vx", "kf", "qf", "dg", "rinv", "h0", "rs", "r1", "lo"):
                        S[n].start(dve)
                    rank_start(dve, R, DVE_RANK)
                    hot_start(dve, G)
                    seen = counter(dve, "b_dve_rounds")

                    def body(w, v, more):
                        over = edges_over(dve, v) if v is not None else None
                        dve.wait_ge(*G["sum"].done(w))
                        dve.tensor_scalar(dg[:], bAGG[:, D:D + 1], 1.0, None, ALU.max).then_inc(S["dg"].sem, 1)
                        dve.wait_ge(*S["dg"].done(w))
                        dve.reciprocal(rinv[:], dg[:]).then_inc(S["rinv"].sem, 1)
                        dve.wait_ge(*S["rinv"].done(w))
                        dve.wait_ge(*SD["inR"].done(w))
                        dve.wait_ge(*S["h"].before(w))
                        dve.scalar_tensor_tensor(h0[:], bAGG[:, 0:D], rinv[:], r1[:], ALU.mult, ALU.add).then_inc(S["h0"].sem, 1)
                        dve.wait_ge(*S["kv"].done(w))
                        dve.wait_ge(*S["ke"].before(w))
                        dve.tensor_scalar(km[:], bMM[:, 0:D], 0.0, None, ALU.min).then_inc(S["km"].sem, 1)
                        dve.wait_ge(*S["KV"].before(w))
                        dve.tensor_copy(vx[:, :, 0:P], bMM[:, D:2 * D].rearrange("p (a b) -> p a b", a=2))
                        dve.tensor_copy(vx[:, :, P:P + 1], c("real")[:, bass.ds(w, 1)].unsqueeze(1).broadcast_to([P, 2, 1])).then_inc(S["vx"].sem, 1)
                        dve.wait_ge(*S["ke"].done(w))
                        dve.scalar_tensor_tensor(kf[:], bMM[:, 0:D], 0.0, ke[:], ALU.max, ALU.add).then_inc(S["kf"].sem, 1)
                        dve.wait_ge(*S["q"].done(w))
                        dve.wait_ge(*S["qe"].before(w))
                        dve.tensor_scalar(qm[:], bQ[:, 0:D], 0.0, None, ALU.min).then_inc(S["qm"].sem, 1)
                        rank_hot(dve, R, 0, w, w * RB1)
                        rank_base(dve, R, 0, w)
                        if more:
                            onehots(dve, G, w + 2)
                        dve.wait_ge(*S["qe"].done(w))
                        dve.wait_ge(*SD["outq"].before(w))
                        dve.scalar_tensor_tensor(qf[:], bQ[:, 0:D], 0.0, qe[:], ALU.max, ALU.add).then_inc(S["qf"].sem, 1)
                        rank_hot(dve, R, 1, w, w * RB1 + 1)
                        rank_near(dve, R, 0, w, w * RB1)
                        rank_place(dve, R, 0, w, w * RB1)
                        rank_base(dve, R, 1, w)
                        dve.wait_ge(*S["ur"].done(w))
                        dve.wait_ge(*SD["outR"].before(w))
                        dve.tensor_tensor(rs[:], bMM[:, D:2 * D], r("gnn_b2"), ALU.add).then_inc(S["rs"].sem, 1)
                        rank_near(dve, R, 1, w, w * RB1 + 1)
                        dve.wait_ge(*S["hi"].done(w))
                        dve.tensor_tensor(ur[:], bMM[:, 0:D], us[:, 0, :], ALU.subtract).then_inc(S["r1"].sem, 1)
                        dve.wait_ge(*S["mid"].done(w))
                        dve.tensor_tensor(us[:, 2, :], ur[:], us[:, 1, :], ALU.subtract).then_inc(S["lo"].sem, 1)
                        rank_place(dve, R, 1, w, w * RB1 + 1)
                        if v is not None:
                            extra_onehots(dve, G, seen, v, over)

                    onehots(dve, G, 0)
                    onehots(dve, G, 1)
                    extra_onehots(dve, G, seen, 0, edges_over(dve, 0))
                    over_windows(dve, body)
        clear_semaphores()
        if upto <= 2:
            return

        with ExitStack() as b:
            G = gather_state(b, "c_")
            R = rank_state(b, "c_", RB2)
            w1 = sbuf(b, "w1", [P, 2, D], F32)
            w2 = sbuf(b, "w2", [P, 2, D], F32)
            wg = sbuf(b, "wg", [P, 2, 16], F32)
            mb1 = sbuf(b, "mb1", [P, 2], F32)

            def row_buffer(name, n=D):
                return sbuf(b, name, [P, n], F32)
            xw, r2, qT = row_buffer("xw_c", 2 * D), row_buffer("r2"), row_buffer("qT")
            dg, rinv, lg, lx = row_buffer("dg_c", 1), row_buffer("rinv_c", 1), row_buffer("lg"), row_buffer("lx")
            den, rden, tz, s1, a1, x1, x1b = (row_buffer("den", 8), row_buffer("rden", 8), row_buffer("tz"), row_buffer("s1"),
                                              row_buffer("a1"), row_buffer("x1"), row_buffer("x1b"))
            x1T, gT, s2, a2, mix = row_buffer("x1T"), row_buffer("gT"), row_buffer("s2"), row_buffer("a2"), row_buffer("mix")
            x2, x2n, x2nT = row_buffer("x2"), row_buffer("x2n"), row_buffer("x2nT")
            LN = [dict(st=row_buffer(f"lnst{i}", 6), mv=row_buffer(f"lnmv{i}", 2), sd=row_buffer(f"lnsd{i}", 1),
                       rs=row_buffer(f"lnrs{i}", 1), s=steps(f"c_ln{i}", ["st", "mv", "sd", "rs"])) for i in range(3)]
            atp = sbuf(b, "atp", [P, T, 16], F32)
            S = steps("c", ["xs", "t", "den", "rden", "tz", "s1", "a1", "x1", "x1b", "x1Tp", "x1T", "h", "g", "y", "s2", "a2", "mix",
                            "dg", "rinv", "lg", "lx", "x2", "x2n", "x2Tp", "x2T", "gat", "gatev"])
            SD = steps("c", ["inx", "inr", "inq", "outx2", "outT"], 16)
            G["evict"] = S["lg"]
            c_load = sem("c_load")
            s_kv = sem("c_kvbd")
            turns = sem("c_turns")
            s_tab = sem("c_table")
            c_out = sem("c_out")

            def norm_stats(dve, i, t, v):
                n = LN[i]
                dve.bn_stats(n["st"][:], v).then_inc(n["s"]["st"].sem, 1)
                dve.wait_ge(*n["s"]["st"].done(t))
                dve.sem_inc(turns, 1)
                dve.bn_aggr(n["mv"][:], n["st"][:]).then_inc(n["s"]["mv"].sem, 1)

            def norm_scale(dve, i, t):
                n = LN[i]
                dve.wait_ge(*n["s"]["sd"].done(t))
                dve.reciprocal(n["rs"][:], n["sd"][:]).then_inc(n["s"]["rs"].sem, 1)

            def norm_root(act, i, t):
                n = LN[i]
                act.wait_ge(*n["s"]["mv"].done(t))
                act.activation(n["sd"][:], n["mv"][:, 1:2], ACT.Sqrt, bias=c("eps")).then_inc(n["s"]["sd"].sem, 1)

            with nc.Block() as block:
                @block.gpsimd
                def _(pool):
                    gather_pool(pool, G, table[1], "c_")

                @block.sync
                def _(sp):
                    sp.dma_start(w1[:], io["w1"]).then_inc(c_load, 16)
                    sp.dma_start(w2[:], io["w2"]).then_inc(c_load, 16)
                    sp.dma_start(wg[:], io["wgat"]).then_inc(c_load, 16)
                    sp.dma_start(mb1[:], io["mix_b1"]).then_inc(c_load, 16)
                    sp.dma_start(sorted_d[FE:FE + 2 * P, :].rearrange("(p k) d -> p (k d)", p=P),
                                 zeros16[:, 0:4 * TW].bitcast(F32)).then_inc(c_out, 16)
                    gather_sync(sp, G, "c_")
                    sp.wait_ge(s_tab, 3)
                    sp.dma_start(heads_d.rearrange("(t p) d -> p t d", p=P), trow[:]).then_inc(c_out, 16)
                    sp.wait_ge(c_out, 32)

                @block.scalar
                def _(act):
                    for n in ("xs", "x1T", "g", "x2T"):
                        S[n].start(act)
                    for s in SD.values():
                        s.start(act)
                    for n in LN:
                        n["s"]["sd"].start(act)
                    for B in R["b"]:
                        B["row_in"].start(act)
                    rank_start(act, R, ("loT",))

                    def x_at(t):
                        return xw[:, bass.ds((t % 2) * D, D)]

                    def load_x(t):
                        act.dma_start(x_at(t), tile_rows(io["x"], t)).then_inc(SD["inx"].sem, 16)

                    def load_q(t):
                        act.dma_start(qT[:], qT_d[bass.ds(t, 1)].rearrange("t p d -> (t p) d")).then_inc(SD["inq"].sem, 16)

                    def load_r(t):
                        act.dma_start(r2[:], tile_rows(own[1], t)).then_inc(SD["inr"].sem, 16)

                    def body(w, v, more):
                        if v is not None:
                            act.wait_ge(*SD["inx"].done(v))
                            act.wait_ge(*S["s1"].before(v))
                            act.activation(xs[:], x_at(v), ACT.Identity, bias=nmr[:, bass.ds(v, 1)],
                                           scale=rstd[:, bass.ds(v, 1)]).then_inc(S["xs"].sem, 1)
                        if w is not None:
                            norm_root(act, 1, w)
                        if v is not None:
                            norm_root(act, 0, v)
                        if w is not None:
                            norm_root(act, 2, w)
                            rank_turned(act, R, 0, w)
                        if v is not None:
                            act.wait_ge(*S["x1Tp"].done(v))
                            act.activation(x1T[:], bT[:, 0:D], ACT.Copy).then_inc(S["x1T"].sem, 1)
                            act.wait_ge(*S["h"].done(v))
                            act.activation(gT[:, 0:P], bMM[:, 0:P], ACT.Gelu, bias=mb1[:, 0:1])
                            act.activation(gT[:, P:2 * P], bMM[:, P:2 * P], ACT.Gelu, bias=mb1[:, 1:2]).then_inc(S["g"].sem, 1)
                        if w is not None:
                            act.dma_start(tile_rows(x2_d, w), x2[:]).then_inc(SD["outx2"].sem, 16)
                            if more:
                                act.wait_ge(*S["lx"].done(w))
                                act.wait_ge(*SD["inx"].done(v))
                                load_x(w + 2)
                        if v is not None:
                            act.wait_ge(*S["lx"].before(v))
                            load_r(v)
                            if w is None or more:
                                act.wait_ge(*S["t"].done(v))
                                load_q(v + 1)
                            if w is not None:
                                rank_load(act, R, 0, v, v + T * RB1)
                        if w is not None:
                            act.wait_ge(*S["x2Tp"].done(w))
                            act.wait_ge(*SD["outT"].before(w))
                            act.activation(x2nT[:], bT[:, 0:D], ACT.Copy).then_inc(S["x2T"].sem, 1)
                            act.wait_ge(*S["x2T"].done(w))
                            act.dma_start(x2nT_d[bass.ds(w, 1)].rearrange("t p d -> (t p) d"), x2nT[:]).then_inc(SD["outT"].sem, 16)

                    act.wait_ge(c_load, 64)
                    load_x(0)
                    act.wait_ge(*SD["inx"].done(0))
                    load_x(1)
                    load_q(0)
                    rank_load(act, R, 0, 0, T * RB1)
                    body(None, 0, False)
                    over_windows(act, body)
                    for s in SD.values():
                        act.wait_ge(s.sem, (T + 1) * 16)

                @block.tensor
                def _(pe):
                    for n in ("t", "x1Tp", "h", "y", "x2Tp", "gat"):
                        S[n].start(pe)
                    rank_start(pe, R, PE_RANK)
                    gather_start(pe, G)
                    seen = counter(pe, "c_pe_rounds")
                    pe.wait_ge(c_load, 64)
                    pe.wait_ge(s_kv, 1)

                    def body(w, v, i, turn):
                        over = edges_over(pe, v) if v is not None else None
                        prev = 0 if w is None else w
                        if v is not None:
                            pe.wait_ge(*SD["inq"].done(v))
                            pe.wait_ge(*S["tz"].before(v))
                            for j in range(2):
                                last = pe.matmul(bQ[:, j * (P + 4):(j + 1) * (P + 4)], qT[:, j * P:(j + 1) * P], kvbd[:, j, :],
                                                 start=True, stop=True, skip_group_check=True)
                            last.then_inc(S["t"].sem, 1)
                            aggregate(pe, G, v, i, turn, 0)
                        if w is not None:
                            rank_turn(pe, R, 0, w)
                        if v is not None:
                            pe.wait_ge(*S["x1"].done(v))
                            pe.wait_ge(*S["x2T"].before(prev))
                            for j in range(2):
                                last = pe.transpose(bT[:, j * P:(j + 1) * P], x1[:, j * P:(j + 1) * P], c("ident"))
                            last.then_inc(S["x1Tp"].sem, 1)
                        if w is not None:
                            rank_count(pe, R, 0, w)
                        if v is not None:
                            pe.wait_ge(*S["x1T"].done(v))
                            pe.wait_ge(*S["gatev"].before(prev))
                            for o in range(2):
                                for j in range(2):
                                    last = pe.matmul(bMM[:, o * P:(o + 1) * P], w1[:, j, o * P:(o + 1) * P],
                                                     x1T[:, j * P:(j + 1) * P], start=(j == 0), stop=(j == 1))
                            last.then_inc(S["h"].sem, 1)
                            aggregate(pe, G, v, i, turn, 1)
                            pe.wait_ge(*S["g"].done(v))
                            pe.wait_ge(*S["s2"].before(v))
                            for j in range(2):
                                last = pe.matmul(bKV[:, 0:D], gT[:, j * P:(j + 1) * P], w2[:, j, :], start=(j == 0), stop=(j == 1))
                            last.then_inc(S["y"].sem, 1)
                        if w is not None:
                            pe.wait_ge(*S["x2n"].done(w))
                            for j in range(2):
                                last = pe.transpose(bT[:, j * P:(j + 1) * P], x2n[:, j * P:(j + 1) * P], c("ident"))
                            last.then_inc(S["x2Tp"].sem, 1)
                        if v is not None:
                            aggregate(pe, G, v, i, turn, 2)
                        if w is not None:
                            pe.wait_ge(*S["x2T"].done(w))
                            for j in range(2):
                                last = pe.matmul(bMM[:, 0:16], x2nT[:, j * P:(j + 1) * P], wg[:, j, :], start=(j == 0), stop=(j == 1))
                            last.then_inc(S["gat"].sem, 1)
                        if v is not None:
                            aggregate_end(pe, G, seen, v, over)

                    body(None, 0, 0, 0)
                    with pe.Fori(0, T // 2 - 1) as t2:
                        body(t2 * 2, t2 * 2 + 1, 1, t2)
                        body(t2 * 2 + 1, t2 * 2 + 2, 0, t2 + 1)
                    body(T - 2, T - 1, 1, T // 2 - 1)
                    body(T - 1, None, None, None)

                @block.vector
                def _(dve):
                    for n in ("den", "rden", "tz", "s1", "a1", "x1", "x1b", "s2", "a2", "mix", "dg", "rinv", "lg", "lx", "x2", "x2n", "gatev"):
                        S[n].start(dve)
                    for n in LN:
                        for k in ("st", "mv", "rs"):
                            n["s"][k].start(dve)
                    rank_start(dve, R, DVE_RANK)
                    hot_start(dve, G)
                    seen = counter(dve, "c_dve_rounds")
                    for j in range(2):
                        at = j * (P + 1)
                        dve.tensor_tensor(kvbd[:, j, 0:P], bKV[:, at:at + P], c("kvmask")[:, 0:P], ALU.mult)
                        last = dve.tensor_tensor(kvbd[:, j, P:P + 4], bKV[:, at + P:at + P + 1].broadcast_to([P, 4]), c("kvmask")[:, P:P + 4], ALU.mult)
                    last.then_inc(s_kv, 1)
                    bq = bQ[:, 0:2 * (P + 4)].rearrange("p (j n) -> p j n", j=2)

                    def body(w, v, more):
                        over = edges_over(dve, v) if v is not None else None
                        if w is not None:
                            dve.wait_ge(*S["y"].done(w))
                            dve.wait_ge(*S["x1b"].done(w))
                            dve.tensor_tensor(s2[:], bKV[:, 0:D], x1b[:], ALU.add).then_inc(S["s2"].sem, 1)
                            dve.wait_ge(*G["sum"].done(w))
                            dve.tensor_scalar(dg[:], bAGG[:, D:D + 1], 1.0, None, ALU.max).then_inc(S["dg"].sem, 1)
                            dve.wait_ge(*S["s2"].done(w))
                            dve.bn_stats(LN[1]["st"][:], s2[:]).then_inc(LN[1]["s"]["st"].sem, 1)
                            dve.wait_ge(*S["dg"].done(w))
                            dve.reciprocal(rinv[:], dg[:]).then_inc(S["rinv"].sem, 1)
                            dve.wait_ge(*LN[1]["s"]["st"].done(w))
                            dve.sem_inc(turns, 1)
                            dve.bn_aggr(LN[1]["mv"][:], LN[1]["st"][:]).then_inc(LN[1]["s"]["mv"].sem, 1)
                            rank_hot(dve, R, 0, w, w + T * RB1)
                            dve.wait_ge(*S["rinv"].done(w))
                            dve.wait_ge(*SD["inr"].done(w))
                            dve.scalar_tensor_tensor(lg[:], bAGG[:, 0:D], rinv[:], r2[:], ALU.mult, ALU.add).then_inc(S["lg"].sem, 1)
                        if v is not None:
                            dve.wait_ge(*S["t"].done(v))
                            dve.tensor_scalar(den[:].rearrange("p (j n) -> p j n", j=2), bq[:, :, P:P + 4], 1e-6, None, ALU.add).then_inc(S["den"].sem, 1)
                        if w is not None:
                            dve.wait_ge(*LN[1]["s"]["mv"].done(w))
                            dve.scalar_tensor_tensor(a2[:], s2[:], LN[1]["mv"][:, 0:1], r("ln2_g"), ALU.subtract, ALU.mult).then_inc(S["a2"].sem, 1)
                        if v is not None:
                            dve.wait_ge(*S["den"].done(v))
                            dve.reciprocal(rden[:], den[:]).then_inc(S["rden"].sem, 1)
                        if w is not None:
                            norm_scale(dve, 1, w)
                        if v is not None:
                            dve.wait_ge(*S["rden"].done(v))
                            dve.tensor_tensor(tz[:].rearrange("p (j h n) -> p j h n", j=2, h=4),
                                              bq[:, :, 0:P].rearrange("p j (h n) -> p j h n", h=4),
                                              rden[:].rearrange("p (j h) -> p j h", j=2).unsqueeze(3).broadcast_to([P, 2, 4, DH]),
                                              ALU.mult).then_inc(S["tz"].sem, 1)
                        if w is not None:
                            dve.wait_ge(*S["lg"].done(w))
                            dve.wait_ge(*SD["inx"].done(w))
                            dve.tensor_tensor(lx[:], lg[:], xw[:, bass.ds((w % 2) * D, D)], ALU.add).then_inc(S["lx"].sem, 1)
                            dve.wait_ge(*S["a2"].done(w))
                            dve.wait_ge(*LN[1]["s"]["rs"].done(w))
                            dve.scalar_tensor_tensor(mix[:], a2[:], LN[1]["rs"][:], r("ln2_b"), ALU.mult, ALU.add).then_inc(S["mix"].sem, 1)
                        if v is not None:
                            dve.wait_ge(*S["tz"].done(v))
                            dve.wait_ge(*S["xs"].done(v))
                            dve.tensor_tensor(s1[:], tz[:], xs[:], ALU.add).then_inc(S["s1"].sem, 1)
                        if w is not None:
                            dve.wait_ge(*S["mix"].done(w))
                            dve.wait_ge(*S["lx"].done(w))
                            dve.wait_ge(*SD["outx2"].before(w))
                            dve.tensor_tensor(x2[:], mix[:], lx[:], ALU.add).then_inc(S["x2"].sem, 1)
                        if v is not None:
                            dve.wait_ge(*S["s1"].done(v))
                            norm_stats(dve, 0, v, s1[:])
                        if w is not None:
                            dve.wait_ge(*S["x2"].done(w))
                            norm_stats(dve, 2, w, x2[:])
                        if v is not None:
                            dve.wait_ge(*LN[0]["s"]["mv"].done(v))
                            dve.scalar_tensor_tensor(a1[:], s1[:], LN[0]["mv"][:, 0:1], r("ln1_g"), ALU.subtract, ALU.mult).then_inc(S["a1"].sem, 1)
                            norm_scale(dve, 0, v)
                            dve.wait_ge(*S["a1"].done(v))
                            dve.wait_ge(*S["x1Tp"].before(v))
                            dve.wait_ge(*LN[0]["s"]["rs"].done(v))
                            dve.scalar_tensor_tensor(x1[:], a1[:], LN[0]["rs"][:], r("ln1_b"), ALU.mult, ALU.add).then_inc(S["x1"].sem, 1)
                        if w is not None:
                            norm_scale(dve, 2, w)
                            rank_base(dve, R, 0, w)
                            dve.wait_ge(*LN[2]["s"]["rs"].done(w))
                            dve.wait_ge(*S["x2Tp"].before(w))
                            dve.tensor_scalar(x2n[:], x2[:], LN[2]["mv"][:, 0:1], LN[2]["rs"][:], ALU.subtract, ALU.mult).then_inc(S["x2n"].sem, 1)
                        if v is not None:
                            dve.wait_ge(*S["x1"].done(v))
                            dve.wait_ge(*S["s2"].before(v))
                            dve.tensor_tensor(x1b[:], x1[:], r("mix_b2"), ALU.add).then_inc(S["x1b"].sem, 1)
                        if more:
                            onehots(dve, G, w + 2)
                        if w is not None:
                            rank_near(dve, R, 0, w, w + T * RB1)
                            rank_place(dve, R, 0, w, w + T * RB1)
                            dve.wait_ge(*S["gat"].done(w))
                            dve.tensor_scalar(trow[:, bass.ds(w, 1), 0:16], bMM[:, 0:16].unsqueeze(1), 1.0, None, ALU.mult).then_inc(S["gatev"].sem, 1)
                        if v is not None:
                            extra_onehots(dve, G, seen, v, over)

                    onehots(dve, G, 0)
                    onehots(dve, G, 1)
                    body(None, 0, False)
                    over_windows(dve, body)
                    dve.wait_ge(S["gatev"].sem, T + 1)
                    dve.tensor_tensor(atp[:], trow[:, :, 0:16], r("att_src").unsqueeze(1).broadcast_to([P, T, 16]), ALU.mult).then_inc(s_tab, 1)
                    dve.wait_ge(s_tab, 1)
                    dve.tensor_reduce(trow[:, :, 16:20], atp[:].rearrange("p t (h e) -> p t h e", h=EH), AX.X, ALU.add).then_inc(s_tab, 1)
                    dve.wait_ge(s_tab, 2)
                    dve.tensor_tensor(atp[:], trow[:, :, 0:16], r("att_dst").unsqueeze(1).broadcast_to([P, T, 16]), ALU.mult).then_inc(s_tab, 1)
                    dve.wait_ge(s_tab, 3)
                    dve.tensor_reduce(adst[:], atp[:].rearrange("p t (h e) -> p t h e", h=EH), AX.X, ALU.add).then_inc(s_tab, 1)
        early.close()
        clear_semaphores()
        if upto <= 3:
            return

        with ExitStack() as b:
            HALF = 2
            EI = FC // (HALF * GRP)
            got = [sbuf(b, f"got{h}", [P, GRP, TW], F32) for h in range(HALF)]
            isrc = [sbuf(b, f"isrc{h}", [P, GRP], I32) for h in range(HALF)]
            ipos = [sbuf(b, f"ipos{h}", [P, GRP], I32) for h in range(HALF)]
            s_isrc = [sem(f"d_isrc{h}") for h in range(HALF)]
            s_ipos = [sem(f"d_ipos{h}") for h in range(HALF)]
            s_got = [Step(sem(f"d_got{h}"), 16 * GRP, 0) for h in range(HALF)]
            s_put = [Step(sem(f"d_put{h}"), 16 * GRP, 0) for h in range(HALF)]
            go = sem("d_go")
            mw1 = sbuf(b, "mw1", [P, E * 2, FH], F32)
            mw2 = sbuf(b, "mw2", [P, E * 4, D], F32)
            fb1 = sbuf(b, "fb1", [P, E * 4], F32)
            xT = sbuf(b, "xT_d", [P, 2 * P], F32)
            gh = [sbuf(b, f"gh{e}", [P, FH], F32) for e in range(E)]
            Y = sbuf(b, "Y", [P, E * D], F32)
            bH = [psum(b, f"bH{e}") for e in range(E)]
            bY = [psum(b, f"bY{i}") for i in range(2)]
            S = steps("d", [f"h{e}" for e in range(E)] + [f"g{e}" for e in range(E)] + ["y0", "y1", "Y0", "Y1"])
            SD = steps("d", ["in", "out"], 16)
            d_load = sem("d_load")
            with nc.Block() as block:
                @block.gpsimd
                def _(pool):
                    with pool.Fori(0, EI) as i:
                        for h in range(HALF):
                            pool.wait_ge(s_isrc[h], (i + 1) * 16)
                            pool.wait_ge(s_ipos[h], (i + 1) * 16)
                            pool.sem_inc(go, 1)
                            for k in range(GRP):
                                pool.indirect_dma_start(
                                    out=got[h][:, k, :], out_offset=None, in_=heads_d,
                                    in_offset=bass.IndirectOffsetOnAxis(ap=isrc[h][:, k:k + 1], axis=0)).then_inc(s_got[h].sem, 16)
                        for h in range(HALF):
                            pool.wait_ge(s_ipos[h], (i + 1) * 16)
                            pool.wait_ge(*s_got[h].done(i))
                            pool.sem_inc(go, 1)
                            for k in range(GRP):
                                pool.indirect_dma_start(
                                    out=sorted_d, out_offset=bass.IndirectOffsetOnAxis(ap=ipos[h][:, k:k + 1], axis=0),
                                    in_=got[h][:, k, :], in_offset=None).then_inc(s_put[h].sem, 16)
                    for h in range(HALF):
                        pool.wait_ge(s_put[h].sem, EI * 16 * GRP)

                @block.sync
                def _(sp):
                    for h in range(HALF):
                        sp.dma_start(isrc[h][:], io["ffn_src"][h]).then_inc(s_isrc[h], 16)
                        sp.dma_start(ipos[h][:], pos[:, h * GRP:(h + 1) * GRP]).then_inc(s_ipos[h], 16)
                    sp.dma_start(mw1[:], io["moe_w1"]).then_inc(d_load, 16)
                    sp.dma_start(mw2[:], io["moe_w2"]).then_inc(d_load, 16)
                    sp.dma_start(fb1[:], io["moe_b1"]).then_inc(d_load, 16)
                    with sp.Fori(0, EI) as i:
                        for h in range(HALF):
                            sp.wait_ge(*s_got[h].done(i))
                            sp.dma_start(isrc[h][:], io["ffn_src"][bass.ds((i + 1) * HALF + h, 1)].rearrange("g p k -> (g p) k"))\
                                .then_inc(s_isrc[h], 16)
                        for h in range(HALF):
                            sp.wait_ge(*s_put[h].done(i))
                            sp.dma_start(ipos[h][:], pos[:, bass.ds((i + 1) * HALF * GRP + h * GRP, GRP)]).then_inc(s_ipos[h], 16)
                    for h in range(HALF):
                        sp.wait_ge(s_isrc[h], (EI + 1) * 16)
                        sp.wait_ge(s_ipos[h], (EI + 1) * 16)

                @block.scalar
                def _(act):
                    for e in range(E):
                        S[f"g{e}"].start(act)
                    for s in SD.values():
                        s.start(act)
                    act.wait_ge(d_load, 48)
                    with act.Fori(0, T) as t:
                        act.wait_ge(*S[f"h{E - 1}"].before(t))
                        act.dma_start(xT[:], x2nT_d[bass.ds(t, 1)].rearrange("t p d -> (t p) d")).then_inc(SD["in"].sem, 16)
                        for e in range(E):
                            act.wait_ge(*S[f"h{e}"].done(t))
                            act.wait_ge(*S[f"y{e // 2}"].before(t))
                            for f in range(4):
                                last = act.activation(gh[e][:, f * P:(f + 1) * P], bH[e][:, f * P:(f + 1) * P], ACT.Gelu,
                                                      bias=fb1[:, e * 4 + f:e * 4 + f + 1])
                            last.then_inc(S[f"g{e}"].sem, 1)
                        act.wait_ge(*S["Y0"].done(t))
                        act.wait_ge(*S["Y1"].done(t))
                        act.dma_start(experts_d[bass.ds(t, 1)].rearrange("t p d -> (t p) d"), Y[:]).then_inc(SD["out"].sem, 16)
                    act.wait_ge(SD["in"].sem, (T + 1) * 16)
                    act.wait_ge(SD["out"].sem, (T + 1) * 16)

                @block.tensor
                def _(pe):
                    for e in range(E):
                        S[f"h{e}"].start(pe)
                    S["y0"].start(pe)
                    S["y1"].start(pe)
                    pe.wait_ge(d_load, 48)
                    with pe.Fori(0, T) as t:
                        pe.wait_ge(*SD["in"].done(t))
                        for e in range(E):
                            pe.wait_ge(*S[f"g{e}"].before(t))
                            for f in range(4):
                                for j in range(2):
                                    last = pe.matmul(bH[e][:, f * P:(f + 1) * P], mw1[:, e * 2 + j, f * P:(f + 1) * P],
                                                     xT[:, j * P:(j + 1) * P], start=(j == 0), stop=(j == 1))
                            last.then_inc(S[f"h{e}"].sem, 1)
                        for e in range(E):
                            pe.wait_ge(*S[f"g{e}"].done(t))
                            if e % 2 == 0:
                                pe.wait_ge(*S[f"Y{e // 2}"].before(t))
                            for f in range(4):
                                last = pe.matmul(bY[e // 2][:, (e % 2) * D:(e % 2 + 1) * D], gh[e][:, f * P:(f + 1) * P],
                                                 mw2[:, e * 4 + f, :], start=(f == 0), stop=(f == 3))
                            if e % 2:
                                last.then_inc(S[f"y{e // 2}"].sem, 1)

                @block.vector
                def _(dve):
                    S["Y0"].start(dve)
                    S["Y1"].start(dve)
                    with dve.Fori(0, T) as t:
                        dve.wait_ge(*SD["out"].before(t))
                        for i in range(2):
                            dve.wait_ge(*S[f"y{i}"].done(t))
                            dve.tensor_tensor(Y[:, i * 2 * D:(i + 1) * 2 * D], bY[i][:],
                                              r("ffn_b2")[:, i * 2 * D:(i + 1) * 2 * D], ALU.add).then_inc(S[f"Y{i}"].sem, 1)
        clear_semaphores()
        if upto <= 4:
            return

        with ExitStack() as b:
            m = sbuf(b, "m", [P, T, EH], F32)
            den = sbuf(b, "den_e", [P, T, EH], F32)
            agg = sbuf(b, "agg", [P, T, 16], F32)
            idx = [sbuf(b, f"idx_e{i}", [P, 1], I32) for i in range(3)]
            got = [sbuf(b, f"got_e{i}", [P, L * TW], F32) for i in range(2)]
            e0, e1, e2, e3, ee = (sbuf(b, f"e_{i}", [P, L, EH], F32) for i in range(5))
            pen = sbuf(b, "pen", [P, L], F32)
            prod = sbuf(b, "prod_e", [P, L, 16], F32)
            mr, mn, dm, corr, sr, dc = (sbuf(b, f"small{i}", [P, EH], F32) for i in range(6))
            ar, ac = (sbuf(b, f"wide{i}", [P, 16], F32) for i in range(2))
            S = steps("e", ["idx0", "idx1", "idx2", "first", "left"])
            SG = [Step(sem(f"e_got{i}"), 16, 0) for i in range(3)]
            s_init = sem("e_init")
            go = sem("e_go")
            names = ["e0", "e1", "pen", "e2", "mr", "mn", "dm", "e3", "corr", "ee", "sr", "dc", "den", "prod", "ar", "ac", "agg"]
            SR = [steps(f"e_{i}", names) for i in range(3)]

            def gather_block(pool, i, n):
                pool.wait_ge(*S[f"idx{i}"].done(n))
                pool.sem_inc(go, 1)
                pool.indirect_dma_start(out=got[i % 2][:], out_offset=None, in_=sorted_d,
                                        in_offset=bass.IndirectOffsetOnAxis(ap=idx[i][:], axis=0)).then_inc(SG[i].sem, 16)

            def fold(dve, i, t, n, s, count):
                g3 = got[i][:].rearrange("p (l f) -> p l f", f=TW)
                mt = flat(m[:, bass.ds(t, 1), :])
                dt_ = flat(den[:, bass.ds(t, 1), :])
                at = flat(agg[:, bass.ds(t, 1), :])
                dve.wait_ge(*s["e1"].before(n))
                dve.tensor_tensor(e0[:], g3[:, :, 16:20], adst[:, bass.ds(t, 1), :].broadcast_to([P, L, EH]), ALU.add).then_inc(s["e0"].sem, 1)
                dve.tensor_scalar(pen[:], c("slot"), count, -1e30, ALU.is_ge, ALU.mult).then_inc(s["pen"].sem, 1)
                dve.wait_ge(*s["e0"].done(n))
                dve.scalar_tensor_tensor(e1[:], e0[:], 0.2, e0[:], ALU.mult, ALU.max).then_inc(s["e1"].sem, 1)
                dve.wait_ge(*s["e1"].done(n))
                dve.tensor_tensor(e2[:], e1[:], pen[:].unsqueeze(2).broadcast_to([P, L, EH]), ALU.add).then_inc(s["e2"].sem, 1)
                dve.wait_ge(*s["e2"].done(n))
                dve.tensor_reduce(mr[:], e2[:].rearrange("p l h -> p h l"), AX.X, ALU.max).then_inc(s["mr"].sem, 1)
                dve.wait_ge(*s["mr"].done(n))
                dve.tensor_tensor(mn[:], mr[:], mt, ALU.max).then_inc(s["mn"].sem, 1)
                dve.wait_ge(*s["mn"].done(n))
                dve.tensor_tensor(e3[:], e2[:], mn[:].unsqueeze(1).broadcast_to([P, L, EH]), ALU.subtract).then_inc(s["e3"].sem, 1)
                dve.tensor_tensor(dm[:], mt, mn[:], ALU.subtract).then_inc(s["dm"].sem, 1)
                dve.wait_ge(*s["dm"].done(n))
                dve.tensor_scalar(mt, mn[:], 1.0, None, ALU.mult)
                dve.wait_ge(*s["corr"].done(n))
                dve.tensor_tensor(dc[:], dt_, corr[:], ALU.mult).then_inc(s["dc"].sem, 1)
                dve.tensor_tensor(ac[:].rearrange("p (h e) -> p h e", h=EH), at.rearrange("p (h e) -> p h e", h=EH),
                                  corr[:].unsqueeze(2).broadcast_to([P, EH, E]), ALU.mult).then_inc(s["ac"].sem, 1)
                dve.wait_ge(*s["ee"].done(n))
                dve.tensor_tensor(prod[:].rearrange("p l (h e) -> p l h e", h=EH), g3[:, :, 0:16].rearrange("p l (h e) -> p l h e", h=EH),
                                  ee[:].unsqueeze(3).broadcast_to([P, L, EH, E]), ALU.mult).then_inc(s["prod"].sem, 1)
                dve.tensor_reduce(sr[:], ee[:].rearrange("p l h -> p h l"), AX.X, ALU.add).then_inc(s["sr"].sem, 1)
                dve.wait_ge(*s["prod"].done(n))
                dve.tensor_reduce(ar[:], prod[:].rearrange("p l f -> p f l"), AX.X, ALU.add).then_inc(s["ar"].sem, 1)
                dve.wait_ge(*s["sr"].done(n))
                dve.tensor_tensor(dt_, dc[:], sr[:], ALU.add).then_inc(s["den"].sem, 1)
                dve.wait_ge(*s["ar"].done(n))
                dve.tensor_tensor(at, ac[:], ar[:], ALU.add).then_inc(s["agg"].sem, 1)
                dve.wait_ge(*s["agg"].done(n))

            def exps(act, n, s):
                act.wait_ge(*s["dm"].done(n))
                act.activation(corr[:], dm[:], ACT.Exp).then_inc(s["corr"].sem, 1)
                act.wait_ge(*s["e3"].done(n))
                act.activation(flat(ee[:]), flat(e3[:]), ACT.Exp).then_inc(s["ee"].sem, 1)

            ACT_STEPS = ("corr", "ee")

            def node_rounds(eng, body):
                seen = eng.alloc_register("rounds")
                eng.reg_mov(seen, 0)
                with eng.Fori(0, T) as t:
                    most = eng.value_load(dtab[0:1, bass.ds(t, 1)], min_val=0, max_val=FE)
                    with eng.If(most > L):
                        with eng.Fori(1, (most + (L - 1)) // L) as k:
                            body(t, k, eng.snap(seen, min_val=0, max_val=FE))
                            eng.reg_add(seen, seen, 1)

            with nc.Block() as block:
                @block.gpsimd
                def _(pool):
                    with pool.Fori(0, T // 2) as t2:
                        for i in range(2):
                            gather_block(pool, i, t2)
                    node_rounds(pool, lambda t, k, n: gather_block(pool, 2, n))

                @block.scalar
                def _(act):
                    for s in SR:
                        for k in ACT_STEPS:
                            s[k].start(act)
                    with act.Fori(0, T // 2) as t2:
                        for i in range(2):
                            exps(act, t2, SR[i])
                    node_rounds(act, lambda t, k, n: exps(act, n, SR[2]))

                @block.vector
                def _(dve):
                    for s in list(S.values()):
                        s.start(dve)
                    for s in SR:
                        for k in names:
                            if k not in ACT_STEPS:
                                s[k].start(dve)
                    dve.tensor_copy(agg[:], trow[:, :, 0:16])
                    dve.memset(den[:], 1.0)
                    dve.tensor_tensor(m[:], trow[:, :, 16:20], adst[:], ALU.add).then_inc(s_init, 1)
                    dve.wait_ge(s_init, 1)
                    dve.scalar_tensor_tensor(m[:], m[:], 0.2, m[:], ALU.mult, ALU.max).then_inc(s_init, 1)
                    for i in range(2):
                        dve.tensor_copy(idx[i][:], first[:, i:i + 1]).then_inc(S[f"idx{i}"].sem, 1)
                    dve.wait_ge(s_init, 2)
                    with dve.Fori(0, T // 2) as t2:
                        for i in range(2):
                            t = t2 * 2 + i
                            dve.wait_ge(*SG[i].done(t2))
                            fold(dve, i, t, t2, SR[i], deg[:, bass.ds(t, 1)])
                            dve.tensor_scalar(idx[i][:], first[:, bass.ds(t + 2, 1)], 1.0, None, ALU.mult).then_inc(S[f"idx{i}"].sem, 1)

                    def body(t, k, n):
                        ft, dt_ = first[:, bass.ds(t, 1)], deg[:, bass.ds(t, 1)]
                        dve.tensor_scalar(ft, ft, float(L), float(FE), ALU.add, ALU.min).then_inc(S["first"].sem, 1)
                        dve.tensor_scalar(dt_, dt_, float(L), None, ALU.subtract).then_inc(S["left"].sem, 1)
                        dve.wait_ge(*S["first"].done(n))
                        dve.tensor_scalar(idx[2][:], ft, 1.0, None, ALU.mult).then_inc(S["idx2"].sem, 1)
                        dve.wait_ge(*S["left"].done(n))
                        dve.wait_ge(*SG[2].done(n))
                        fold(dve, 0, t, n, SR[2], dt_)
                    node_rounds(dve, body)
            clear_semaphores()
            if upto <= 5:
                return

            sc = sbuf(b, "sc_f", [P, T, 16], F32)
            sq = sbuf(b, "sq_f", [P, T, 16], F32)
            rd = sbuf(b, "rd_f", [P, T, EH], F32)
            mu, vr, sd, rs = (sbuf(b, f"stat_f{i}", [P, T], F32) for i in range(4))
            score, gate, rank = (sbuf(b, f"score_f{i}", [P, T, E], F32) for i in range(3))
            beats = sbuf(b, "beats", [P, T, E, E], F32)
            Yt = [sbuf(b, f"Yt{i}", [P, E * D], F32) for i in range(2)]
            xt = [sbuf(b, f"xt{i}", [P, D], F32) for i in range(2)]
            acc = [[sbuf(b, f"acc{i}_{e}", [P, D], F32) for e in range(E)] for i in range(2)]
            chain = sem("f_chain")
            s_sd, s_ex = sem("f_sd"), sem("f_ex")
            SF = [steps(f"f{i}", [f"acc{e}" for e in range(E)]) for i in range(2)]
            SIN = [Step(sem(f"f_in{i}"), 32) for i in range(2)]
            SOUT = [Step(sem(f"f_out{i}"), 16) for i in range(2)]

            with nc.Block() as block:
                @block.sync
                def _(sp):
                    for i in range(2):
                        SIN[i].start(sp)
                    with sp.Fori(0, T // 2) as t2:
                        for i in range(2):
                            t = t2 * 2 + i
                            sp.wait_ge(*SF[i][f"acc{E - 1}"].before(t2))
                            sp.dma_start(Yt[i][:], experts_d[bass.ds(t, 1)].rearrange("t p d -> (t p) d")).then_inc(SIN[i].sem, 16)
                            sp.dma_start(xt[i][:], tile_rows(x2_d, t)).then_inc(SIN[i].sem, 16)

                @block.scalar
                def _(act):
                    for i in range(2):
                        SOUT[i].start(act)
                    act.wait_ge(chain, 7)
                    act.activation(sd[:], vr[:], ACT.Sqrt, bias=c("eps")).then_inc(s_sd, 1)
                    act.wait_ge(chain, 16)
                    act.activation(flat(gate[:]), flat(score[:]), ACT.Exp).then_inc(s_ex, 1)
                    with act.Fori(0, T // 2) as t2:
                        for i in range(2):
                            act.wait_ge(*SF[i][f"acc{E - 1}"].done(t2))
                            act.dma_start(tile_rows(out, t2 * 2 + i), acc[i][E - 1][:]).then_inc(SOUT[i].sem, 16)
                    for i in range(2):
                        act.wait_ge(SOUT[i].sem, (T // 2 + 1) * 16)

                @block.vector
                def _(dve):
                    n = [0]

                    def link(ins):
                        n[0] += 1
                        ins.then_inc(chain, 1)
                        dve.wait_ge(chain, n[0])

                    def wide(ap, k):
                        return ap.unsqueeze(2).broadcast_to([P, T, k])

                    for i in range(2):
                        for e in range(E):
                            SF[i][f"acc{e}"].start(dve)
                    dve.memset(beats[:], 0.0)
                    link(dve.tensor_scalar(den[:], den[:], 1e-16, None, ALU.add))
                    link(dve.reciprocal(rd[:], den[:]))
                    link(dve.tensor_tensor(sc[:].rearrange("p t (h e) -> p t h e", h=EH), agg[:].rearrange("p t (h e) -> p t h e", h=EH),
                                           rd[:].unsqueeze(3).broadcast_to([P, T, EH, E]), ALU.mult))
                    link(dve.tensor_tensor(sc[:], sc[:], r("b_gat").unsqueeze(1).broadcast_to([P, T, 16]), ALU.add))
                    link(dve.tensor_reduce(mu[:], sc[:], AX.X, ALU.add))
                    link(dve.scalar_tensor_tensor(sc[:], wide(mu[:], 16), -1.0 / 16, sc[:], ALU.mult, ALU.add))
                    dve.tensor_tensor(sq[:], sc[:], sc[:], ALU.mult).then_inc(s_ex, 1)
                    dve.wait_ge(s_ex, 1)
                    dve.tensor_reduce(mu[:], sq[:], AX.X, ALU.add).then_inc(s_ex, 1)
                    dve.wait_ge(s_ex, 2)
                    link(dve.tensor_scalar(vr[:], mu[:], 1.0 / 16, None, ALU.mult))
                    dve.wait_ge(s_sd, 1)
                    link(dve.reciprocal(rs[:], sd[:]))
                    link(dve.tensor_tensor(sc[:], sc[:], wide(rs[:], 16), ALU.mult))
                    link(dve.tensor_tensor(sc[:], sc[:], r("gamma").unsqueeze(1).broadcast_to([P, T, 16]), ALU.mult))
                    link(dve.tensor_tensor(sc[:], sc[:], r("beta").unsqueeze(1).broadcast_to([P, T, 16]), ALU.add))
                    link(dve.tensor_reduce(rank[:], sc[:].rearrange("p t (h e) -> p t e h", h=EH), AX.X, ALU.add))
                    link(dve.tensor_scalar(score[:], rank[:], 1.0 / EH, None, ALU.mult))
                    for e in range(E):
                        for j in range(E):
                            if j != e:
                                last = dve.tensor_tensor(beats[:, :, e, j], score[:, :, j], score[:, :, e], ALU.is_ge if j < e else ALU.is_gt)
                    link(last)
                    link(dve.tensor_reduce(mu[:], score[:], AX.X, ALU.max))
                    link(dve.tensor_tensor(score[:], score[:], wide(mu[:], E), ALU.subtract))
                    link(dve.tensor_reduce(rank[:], beats[:], AX.X, ALU.add))
                    link(dve.tensor_scalar(rank[:], rank[:], 2.0, None, ALU.is_lt))
                    dve.wait_ge(s_ex, 3)
                    link(dve.tensor_tensor(gate[:], gate[:], rank[:], ALU.mult))
                    link(dve.tensor_reduce(mu[:], gate[:], AX.X, ALU.add))
                    link(dve.reciprocal(rs[:], mu[:]))
                    link(dve.tensor_tensor(gate[:], gate[:], wide(rs[:], E), ALU.mult))
                    with dve.Fori(0, T // 2) as t2:
                        for i in range(2):
                            dve.wait_ge(*SIN[i].done(t2))
                            dve.wait_ge(*SOUT[i].before(t2))
                        for e in range(E):
                            for i in range(2):
                                t = t2 * 2 + i
                                if e:
                                    dve.wait_ge(*SF[i][f"acc{e - 1}"].done(t2))
                                dve.scalar_tensor_tensor(acc[i][e][:], Yt[i][:, e * D:(e + 1) * D], flat(gate[:, bass.ds(t, 1), e:e + 1]),
                                                         xt[i][:] if e == 0 else acc[i][e - 1][:], ALU.mult, ALU.add)\
                                   .then_inc(SF[i][f"acc{e}"].sem, 1)


def layouts(x, src, dst, L0_gnn_W_l1, L0_gnn_b1, L0_gnn_W_r1, L0_gnn_W_l2, L0_gnn_b2, L0_gnn_W_r2, L0_mix_Wqkv,
            L0_mix_ln1_g, L0_mix_ln1_b, L0_mix_W1, L0_mix_b1, L0_mix_W2, L0_mix_b2, L0_mix_ln2_g, L0_mix_ln2_b,
            L0_ffn_W_gat, L0_ffn_att_src, L0_ffn_att_dst, L0_ffn_b_gat, L0_ffn_ln_gamma, L0_ffn_ln_beta,
            L0_ffn_W1, L0_ffn_b1, L0_ffn_W2, L0_ffn_b2, L0_ffn_edge_index):
    def chunks(v, count, fill):
        v = np.concatenate([v, np.full(count * P - v.shape[0], fill, v.dtype)])
        return v.reshape(count, P).T

    def halves(w):
        return w.reshape(2, P, -1).transpose(1, 0, 2)

    gdst = chunks(dst, GC, NO_NODE)
    fdst = chunks(L0_ffn_edge_index[1], FCP, NO_NODE)
    rows = {"gnn_b1": L0_gnn_b1, "gnn_b2": L0_gnn_b2, "ln1_g": L0_mix_ln1_g, "ln1_b": L0_mix_ln1_b,
            "mix_b2": L0_mix_b2, "ln2_g": L0_mix_ln2_g, "ln2_b": L0_mix_ln2_b, "att_src": L0_ffn_att_src,
            "att_dst": L0_ffn_att_dst, "b_gat": L0_ffn_b_gat, "gamma": L0_ffn_ln_gamma, "beta": L0_ffn_ln_beta,
            "ffn_b2": L0_ffn_b2}
    return {
        "consts": shape_constants(),
        "x": np.pad(x, ((0, NP - N), (0, 0))),
        "gnn_src": chunks(src, GC, 0).T.reshape(1, -1),
        "gnn_dst": gdst.T.reshape(1, -1),
        "gnn_dst_ends": gdst[P - 1:P],
        "ffn_src": chunks(L0_ffn_edge_index[0], FC + 2 * GRP, 0).reshape(P, FC // GRP + 2, GRP).transpose(1, 0, 2),
        "ffn_dst": fdst,
        "ffn_dst_rows": fdst.T.reshape(1, FCP * P),
        "wlr1": halves(np.concatenate([L0_gnn_W_l1, L0_gnn_W_r1], 1)),
        "wlr2": halves(np.concatenate([L0_gnn_W_l2, L0_gnn_W_r2], 1)),
        "wkv": halves(L0_mix_Wqkv[D:].T),
        "wq": halves(L0_mix_Wqkv[:D].T),
        "w1": halves(L0_mix_W1.T),
        "w2": halves(L0_mix_W2.T),
        "mix_b1": L0_mix_b1.reshape(2, P).T,
        "wgat": halves(L0_ffn_W_gat),
        "moe_w1": L0_ffn_W1.reshape(E, 2, P, FH).transpose(2, 0, 1, 3).reshape(P, E * 2, FH),
        "moe_w2": L0_ffn_W2.reshape(E, 4, P, D).transpose(2, 0, 1, 3).reshape(P, E * 4, D),
        "moe_b1": L0_ffn_b1.reshape(E * 4, P).T,
        "rows": np.concatenate([rows[k].reshape(-1) for k, _ in ROW_SIZES])[None, :],
    }


KINDS = "Internal"
UPTO = 9


def kernel(**inputs):
    import concourse.bacc as _bacc
    from concourse.bass_utils import run_bass_kernel_spmd as _run

    nc = _bacc.Bacc("TRN2", target_bir_lowering=False, num_devices=1)
    arrays, io = {}, {}
    for name, a in layouts(**{k: np.asarray(v) for k, v in inputs.items()}).items():
        a = np.ascontiguousarray(a)
        arrays[f"in_{name}"] = a
        io[name] = nc.dram_tensor(f"in_{name}", a.shape, mybir.dt.from_np(a.dtype), kind="ExternalInput").ap()
    out = nc.dram_tensor("out_0", (NP, D), F32, kind="ExternalOutput").ap()
    build(nc, io, out, KINDS, UPTO)
    r = _run(nc, [arrays], core_ids=[0])
    return r.results[0]["out_0"][:N]
```

```python
from contextlib import ExitStack

import concourse.bass as bass
import numpy as np
from concourse import mybir

F32 = mybir.dt.float32
BF16 = mybir.dt.bfloat16
I32 = mybir.dt.int32
ALU = mybir.AluOpType
ACT = mybir.ActivationFunctionType
AX = mybir.AxisListType

P = 128
D = 256
N = 12500
T = -(-N // P)
NP = T * P
GE = 212500
K = 18
KG = 6
NG = K // KG
KX = 2
GC = -(-(GE + P * K) // P) + 1
GRP = 8
FE = 131072
FC = FE // P
HB = 12
RB = 4
RB1, RB2 = 2, 1
FCP = T * HB
L = 40
QT = 4
TE = -(-T // QT) * QT
NY = 14
TW = 20
H, DH = 8, 32
E, EH = 4, 4
FH = 512
EPS = 1e-5
NO_NODE = 128 * 127
SLOT = D + 1

CONST = {}


def shape_constants():
    p = np.arange(P)[:, None]
    f = np.arange(P)[None, :]
    parts = {
        "iota": np.broadcast_to(f, (P, P)),
        "ident": (p == f),
        "before": (p < f),
        "ones": np.ones((P, P)),
        "wbase": np.broadcast_to(-128 * np.arange(T + 1)[None, :], (P, T + 1)),
        "wend": 128 * (p + 1),
        "real": (np.arange(T)[None, :] * P + p) < N,
        "kvmask": np.concatenate([(p // DH == f // DH), (p // DH == np.arange(4)[None, :])], 1),
        "rankmask": np.concatenate([(np.arange(RB * P)[None, :] < k * P + p) for k in range(RB)], 1),
        "slot": np.broadcast_to(np.arange(L)[None, :], (P, L)),
        "eps": np.full((P, 1), EPS),
    }
    at = 0
    for k, v in parts.items():
        CONST[k] = (at, v.shape[1])
        at += v.shape[1]
    return np.ascontiguousarray(np.concatenate([v.astype(np.float32) for v in parts.values()], 1))


ROWS = {}


def row_layout(sizes):
    at = 0
    for k, n in sizes:
        ROWS[k] = (at, n)
        at += n
    return at


ROW_SIZES = [("gnn_b1", D), ("gnn_b2", D), ("ln1_g", D), ("ln1_b", D), ("mix_b2", D), ("ln2_g", D), ("ln2_b", D),
             ("att_src", 16), ("att_dst", 16), ("b_gat", 16), ("gamma", 16), ("beta", 16), ("ffn_b2", E * D)]
NROW = row_layout(ROW_SIZES)


class Step:

    def __init__(self, sem, unit=1, ahead=1):
        self.sem, self.unit, self.ahead = sem, unit, ahead

    def start(self, eng):
        assert self.ahead
        eng.sem_inc(self.sem, self.unit * self.ahead)

    def done(self, t):
        return self.sem, (t + 1 + self.ahead) * self.unit

    def before(self, t):
        assert self.ahead
        return self.sem, (t + self.ahead) * self.unit

    def before2(self, t):
        assert self.ahead == 2
        return self.sem, (t + 1) * self.unit


def flat(ap):
    return ap.rearrange("p a b -> p (a b)")


def build(nc, io, out, kinds, upto=9):
    ctx = ExitStack()
    with ctx:
        def scratch(name, shape, dt):
            return nc.dram_tensor(name, shape, dt, kind=kinds).ap()

        in_use = []

        def sem(name):
            in_use.append(nc.alloc_semaphore(name))
            return in_use[-1]

        def clear_semaphores():
            nc.clear_and_free_semaphores(list(in_use))
            nc.all_engine_barrier()
            in_use.clear()

        def steps(prefix, names, unit=1, ahead=1):
            return {n: Step(sem(f"{prefix}_{n}"), unit, ahead) for n in names}

        def sbuf(stack, name, shape, dt):
            return stack.enter_context(nc.sbuf_tensor(name, shape, dt))

        def psum(stack, name, dt=F32):
            return stack.enter_context(nc.psum_tensor(name, [P, 512 if dt == F32 else 1024], dt))

        table = [scratch(f"message_rows{i}", (NP, D), F32) for i in range(2)]
        own = [scratch(f"own_rows{i}", (NP, D), F32) for i in range(2)]
        qT_d = scratch("q_transposed", (T, P, 2 * P), F32)
        x2_d = scratch("x_second", (NP, D), F32)
        x2nT_d = scratch("x_second_norm_transposed", (T, P, 2 * P), F32)
        heads_d = scratch("attention_rows", (NP, TW), F32)
        sorted_d = scratch("sorted_edge_rows", (FE + 2 * P, TW), F32)
        experts_d = scratch("expert_rows", (T, P, E * D), F32)
        windows_d = scratch("window_starts", (T + 1, 1), I32)
        degrees_d = scratch("largest_degrees", (T, 1), I32)

        const = sbuf(ctx, "const", [P, io["consts"].shape[1]], F32)
        rows = sbuf(ctx, "rows", [P, NROW], F32)
        ident16 = sbuf(ctx, "ident16", [P, P], BF16)
        zeros16 = sbuf(ctx, "zeros16", [P, 512], BF16)
        wtab = sbuf(ctx, "wtab", [1, T + 1], I32)
        xtab = sbuf(ctx, "xtab", [1, T], I32)
        dtab = sbuf(ctx, "dtab", [1, T], I32)
        etab = sbuf(ctx, "etab", [1, 2], I32)
        deg = sbuf(ctx, "deg", [P, TE], F32)
        first = sbuf(ctx, "first", [P, TE + QT], F32)
        trow = sbuf(ctx, "trow", [P, T, TW], F32)
        adst = sbuf(ctx, "adst", [P, TE, EH], F32)
        pos = sbuf(ctx, "pos", [P, T * RB * (RB1 + RB2)], I32)

        def c(name):
            at, n = CONST[name]
            return const[:, at:at + n]

        def r(name):
            at, n = ROWS[name]
            return rows[:, at:at + n]

        def tile_rows(ap, w):
            return ap.rearrange("(t p) d -> t p d", p=P)[bass.ds(w, 1)].rearrange("t p d -> (t p) d")

        load = sem("load")
        setup = sem("setup")

        early = ctx.enter_context(ExitStack())
        rstd = sbuf(early, "rstd", [P, T], F32)
        nmr = sbuf(early, "nmr", [P, T], F32)
        xs = sbuf(early, "xs", [P, D], F32)
        flo = sbuf(early, "flo", [P, FCP], F32)
        fhi = sbuf(early, "fhi", [P, FCP], F32)
        fdst = sbuf(early, "fdst", [P, FCP], F32)
        wlr2 = sbuf(early, "wlr2", [P, 2, 2 * D], F32)
        kvbd = sbuf(early, "kvbd", [P, 2, P + 4], F32)
        bAGG = psum(early, "bAGG")
        bT = psum(early, "bT")
        bMM = psum(early, "bMM")
        bQ = psum(early, "bQ")
        bKV = psum(early, "bKV")
        bC = psum(early, "bC")
        bP = psum(early, "bP")
        bOT = psum(early, "bOT", BF16)

        with ExitStack() as a:
            X = sbuf(a, "X", [P, T, D], F32)
            wlr1 = sbuf(a, "wlr1", [P, 2, 2 * D], F32)
            stat = sbuf(a, "stat", [P, T, 6], F32)
            mean = sbuf(a, "mean", [P, T], F32)
            var = sbuf(a, "var", [P, T], F32)
            tmp = sbuf(a, "tmp", [P, T], F32)
            xT = sbuf(a, "xT", [P, 2, P], F32)
            us = sbuf(a, "us", [P, 2, D], F32)
            rs = sbuf(a, "rs", [P, 2, D], F32)
            Olo = sbuf(a, "Olo", [P, 2, P, HB], BF16)
            Ohi = sbuf(a, "Ohi", [P, 2, T, HB], BF16)
            iota16 = sbuf(a, "iota16", [P, P, HB], BF16)
            flo16 = sbuf(a, "flo16", [P, FCP], BF16)
            fhi16 = sbuf(a, "fhi16", [P, FCP], BF16)
            sc = [sbuf(a, f"scan{i}", [P, T], F32) for i in range(2)]
            part = sbuf(a, "part", [P, T], F32)
            lastd = sbuf(a, "lastd", [T, GC], F32)
            ifd, ilo, ihi, lasti = (v[:].bitcast(I32) for v in (fdst, flo, fhi, lastd))
            endrow = sbuf(a, "endrow", [T, P], F32)
            iend = endrow[:].bitcast(I32)
            inend = sbuf(a, "inend", [T, 1], F32)
            endf = sbuf(a, "endf", [T, 1], F32)
            endi = sbuf(a, "endi", [T, 1], I32)
            s_endrow = sem("a_endrow")
            s_over = sem("a_over")
            cef = sbuf(a, "cef", [T, 1], F32)
            cei = sbuf(a, "cei", [T, 1], I32)
            mdi = sbuf(a, "mdi", [T, 1], I32)
            zi = sbuf(a, "zi", [1, 1], I32)
            last_f = sbuf(a, "last_f", [1, 2], F32)

            XP = 7
            s_x = [sem(f"a_x{k}") for k in range(XP)]
            s_idx = sem("a_idx")
            chain = sem("a_chain")
            s_std = sem("a_std")
            a_turns = sem("a_turns")
            s_bn = sem("a_bn")
            A = steps("a", ["xn", "xnT", "xTs", "ur", "rev", "onehot"])
            A.update(steps("a", ["uev", "hist"], ahead=2))
            AD = steps("a", ["stU", "stR"], 16, ahead=2)
            s_pre = sem("a_prefix")
            s_tr = sem("a_degT")
            s_out = sem("a_tables")
            s_ready = sem("a_ready")
            bUR = [bMM, bKV]
            A_IDX = 4
            with nc.Block() as block:
                @block.sync
                def _(sp):
                    for s in AD.values():
                        s.start(sp)
                    sp.dma_start(const[:], io["consts"]).then_inc(s_idx, 16)
                    sp.dma_start(ifd, io["ffn_dst"]).then_inc(s_idx, 16)
                    sp.dma_start(lasti, io["gnn_dst_ends"].partition_broadcast(T)).then_inc(s_idx, 16)
                    x_v = io["x"].rearrange("(t p) d -> p t d", p=P)
                    for k in range(XP):
                        n = T // XP
                        sp.dma_start(X[:, k * n:(k + 1) * n, :], x_v[:, k * n:(k + 1) * n, :]).then_inc(s_x[k], 16)
                    sp.dma_start(wlr1[:], io["wlr1"]).then_inc(load, 16)
                    sp.dma_start(wlr2[:], io["wlr2"]).then_inc(load, 16)
                    sp.dma_start(rows[:], io["rows"].partition_broadcast(P)).then_inc(load, 16)
                    with sp.Fori(0, T) as t:
                        sp.wait_ge(*A["rev"].done(t))
                        sp.sem_inc(a_turns, 1)
                        sp.wait_ge(*AD["stR"].before(t))
                        sp.sem_inc(a_turns, 1)
                        sp.dma_start(tile_rows(own[0], t), flat(rs[:, bass.ds(t % 2, 1), :])).then_inc(AD["stR"].sem, 16)
                        sp.wait_ge(*A["uev"].done(t))
                        sp.sem_inc(a_turns, 1)
                        sp.wait_ge(*AD["stU"].before(t))
                        sp.sem_inc(a_turns, 1)
                        sp.dma_start(tile_rows(table[0], t), flat(us[:, bass.ds(t % 2, 1), :])).then_inc(AD["stU"].sem, 16)
                    sp.wait_ge(s_ready, 3)
                    sp.dma_start(windows_d[0:1, :], zi[:]).then_inc(s_out, 16)
                    sp.dma_start(windows_d[1:T + 1, :], endi[:]).then_inc(s_out, 16)
                    sp.dma_start(degrees_d[:, :], mdi[:]).then_inc(s_out, 16)
                    sp.wait_ge(s_out, 48)
                    sp.dma_start(wtab[:], windows_d.rearrange("t o -> o t")).then_inc(s_out, 16)
                    sp.dma_start(dtab[:], degrees_d.rearrange("t o -> o t")).then_inc(s_out, 16)
                    sp.wait_ge(s_out, 80)
                    for s in AD.values():
                        sp.wait_ge(s.sem, (T + 2) * 16)

                @block.gpsimd
                def _(pool):
                    pool.wait_ge(s_ready, 1)
                    pool.indirect_dma_start(out=iend, out_offset=None, in_=io["gnn_dst"].rearrange("o (c p) -> (o c) p", p=P),
                                            in_offset=bass.IndirectOffsetOnAxis(ap=cei[:], axis=0)).then_inc(s_endrow, 16)

                @block.scalar
                def _(act):
                    for s in ("xn", "xTs", "uev"):
                        A[s].start(act)
                    act.wait_ge(s_idx, 49)
                    act.activation(ident16[:], c("ident"), ACT.Copy).then_inc(setup, 1)
                    act.wait_ge(chain, 4 + A_IDX)
                    act.activation(tmp[:], var[:], ACT.Sqrt, bias=c("eps")).then_inc(s_std, 1)
                    act.wait_ge(chain, 6 + A_IDX)

                    def normalise(t):
                        act.wait_ge(*A["xnT"].before(t))
                        act.activation(xs[:], flat(X[:, bass.ds(t, 1), :]), ACT.Identity, bias=nmr[:, bass.ds(t, 1)],
                                       scale=rstd[:, bass.ds(t, 1)]).then_inc(A["xn"].sem, 1)

                    def turned(t):
                        act.wait_ge(*A["xnT"].done(t))
                        act.wait_ge(*A["ur"].before(t))
                        act.activation(flat(xT[:]), bT[:, 0:D], ACT.Copy).then_inc(A["xTs"].sem, 1)

                    def evict(t, i):
                        act.wait_ge(*A["rev"].done(t))
                        act.wait_ge(*AD["stU"].before2(t))
                        act.activation(us[:, i, :], bUR[i][:, 0:D], ACT.Copy).then_inc(A["uev"].sem, 1)

                    def turn(t, i, more):
                        turned(t)
                        if more:
                            normalise(t + 1)
                        evict(t - 1, 1 - i)

                    normalise(0)
                    turned(0)
                    normalise(1)
                    turn(1, 1, True)
                    with act.Fori(1, T // 2 - 1) as t2:
                        turn(t2 * 2, 0, True)
                        turn(t2 * 2 + 1, 1, True)
                    turn(T - 2, 0, True)
                    turn(T - 1, 1, False)
                    evict(T - 1, 1)

                @block.tensor
                def _(pe):
                    for s in ("xnT", "ur", "hist"):
                        A[s].start(pe)
                    pe.wait_ge(load, 48)
                    pe.wait_ge(setup, 1)
                    pe.wait_ge(s_idx, 49)
                    pe.matmul(bC[:, 0:T], zeros16[:, 0:P], zeros16[:, 0:T], start=True, stop=False, skip_group_check=True)
                    with pe.Fori(0, T // 2) as t2:
                        for i in range(2):
                            t = t2 * 2 + i
                            pe.wait_ge(*A["xn"].done(t))
                            pe.wait_ge(*A["xTs"].before(t))
                            for j in range(2):
                                last = pe.transpose(bT[:, j * P:(j + 1) * P], xs[:, j * P:(j + 1) * P], c("ident"))
                            last.then_inc(A["xnT"].sem, 1)
                            pe.wait_ge(*A["onehot"].done(t))
                            for k in range(HB):
                                last = pe.matmul(bC[:, 0:T], Olo[:, i, :, k], Ohi[:, i, :, k], start=False, stop=False, skip_group_check=True)
                            last.then_inc(A["hist"].sem, 1)
                            pe.wait_ge(*A["xTs"].done(t))
                            pe.wait_ge(*A["uev"].before2(t))
                            for j in range(2):
                                last = pe.matmul(bUR[i][:], xT[:, j, :], wlr1[:, j, :], start=(j == 0), stop=(j == 1))
                            last.then_inc(A["ur"].sem, 1)
                    pe.wait_ge(s_pre, 1)
                    pe.matmul(bP[:, 0:T], c("before"), deg[:, 0:T], start=True, stop=True)
                    pe.matmul(bP[:, T:2 * T], c("ones"), deg[:, 0:T], start=True, stop=True)
                    pe.transpose(bQ[0:T, 0:P], deg[:, 0:T], c("ident")).then_inc(s_tr, 1)

                @block.vector
                def _(dve):
                    for s in ("rev", "onehot"):
                        A[s].start(dve)
                    n = [0]

                    def link(ins):
                        n[0] += 1
                        ins.then_inc(chain, 1)
                        dve.wait_ge(chain, n[0])
                    dve.memset(zeros16[:], 0.0)
                    dve.memset(zi[:], 0).then_inc(s_idx, 1)
                    dve.wait_ge(s_idx, 49)
                    dve.tensor_copy(lastd[:], lasti)
                    dve.tensor_scalar(ilo, ifd, 127, None, ALU.bitwise_and)
                    link(dve.tensor_scalar(ihi, ifd, 7, None, ALU.logical_shift_right))
                    dve.tensor_copy(fdst[:], ifd)
                    dve.tensor_copy(flo[:], ilo)
                    link(dve.tensor_copy(fhi[:], ihi))
                    dve.tensor_copy(iota16[:], c("iota").unsqueeze(2).broadcast_to([P, P, HB]))
                    dve.tensor_copy(flo16[:], flo[:])
                    link(dve.tensor_copy(fhi16[:], fhi[:]))
                    link(dve.tensor_scalar(lastd[:], lastd[:], c("wend")[0:T], None, ALU.is_lt, ALU.add, accum_out=cef[:]))
                    dve.tensor_copy(cei[:], cef[:]).then_inc(s_ready, 1)
                    for k in range(XP):
                        dve.wait_ge(s_x[k], 16)
                        for t in range(k * (T // XP), (k + 1) * (T // XP)):
                            dve.bn_stats(stat[:, t, :], X[:, t, :]).then_inc(s_bn, 1)
                    dve.wait_ge(s_bn, T)
                    link(dve.tensor_tensor(mean[:], stat[:, :, 1], stat[:, :, 4], ALU.add))
                    dve.tensor_tensor(tmp[:], stat[:, :, 1], stat[:, :, 4], ALU.subtract)
                    link(dve.tensor_tensor(var[:], stat[:, :, 2], stat[:, :, 5], ALU.add))
                    link(dve.scalar_tensor_tensor(tmp[:], tmp[:], 0.25, tmp[:], ALU.mult, ALU.mult))
                    link(dve.scalar_tensor_tensor(var[:], var[:], 1.0 / D, tmp[:], ALU.mult, ALU.add))
                    dve.wait_ge(s_std, 1)
                    link(dve.reciprocal(rstd[:], tmp[:]))
                    link(dve.scalar_tensor_tensor(nmr[:], mean[:], -0.5, rstd[:], ALU.mult, ALU.mult))

                    def count_lo(t, i):
                        dve.wait_ge(*A["hist"].before2(t))
                        dve.tensor_tensor(Olo[:, i], iota16[:], flo16[:, bass.ds(t * HB, HB)].unsqueeze(1).broadcast_to([P, P, HB]),
                                          ALU.is_equal)

                    def count_hi(t, i):
                        dve.tensor_tensor(Ohi[:, i], iota16[:, 0:T, :], fhi16[:, bass.ds(t * HB, HB)].unsqueeze(1).broadcast_to([P, T, HB]),
                                          ALU.is_equal)\
                           .then_inc(A["onehot"].sem, 1)

                    def evict(t, i, more):
                        dve.wait_ge(*A["ur"].done(t))
                        dve.wait_ge(*AD["stR"].before2(t))
                        dve.tensor_tensor(rs[:, i], bUR[i][:, D:2 * D], r("gnn_b1"), ALU.add).then_inc(A["rev"].sem, 1)
                        if more:
                            count_lo(t + 2, i)
                            count_hi(t + 2, i)

                    for t in range(2):
                        count_lo(t, t)
                        count_hi(t, t)
                    dve.wait_ge(load, 48)
                    with dve.Fori(0, T // 2 - 1) as t2:
                        for i in range(2):
                            evict(t2 * 2 + i, i, True)
                    evict(T - 2, 0, False)
                    evict(T - 1, 1, False)
                    dve.wait_ge(s_endrow, 16)
                    link(dve.tensor_copy(endrow[:], iend))
                    link(dve.tensor_scalar(endrow[:], endrow[:], c("wend")[0:T], None, ALU.is_lt, ALU.add, accum_out=inend[:]))
                    link(dve.scalar_tensor_tensor(endf[:], cef[:], float(P), inend[:], ALU.mult, ALU.add))
                    dve.tensor_copy(endi[:], endf[:]).then_inc(s_ready, 1)
                    dve.wait_ge(A["hist"].sem, T + 2)
                    dve.memset(deg[:, T:TE], 0.0)
                    dve.tensor_copy(deg[:, 0:T], bC[:, 0:T]).then_inc(s_pre, 1)
                    dve.wait_ge(s_tr, 1)
                    dve.tensor_reduce(mdi[:], bQ[0:T, 0:P], AX.X, ALU.max).then_inc(s_ready, 1)
                    link(dve.memset(sc[0][:, 0:1], 0.0))
                    link(dve.tensor_copy(sc[0][:, 1:T], bP[:, T:2 * T - 1]))
                    link(dve.tensor_copy(part[:], bP[:, 0:T]))
                    a_, b_ = sc
                    k = 1
                    while k < T:
                        dve.tensor_copy(b_[:, 0:k], a_[:, 0:k])
                        link(dve.tensor_tensor(b_[:, k:T], a_[:, k:T], a_[:, 0:T - k], ALU.add))
                        a_, b_ = b_, a_
                        k *= 2
                    dve.memset(first[:, T:TE + QT], 0.0)
                    link(dve.tensor_tensor(first[:, 0:T], part[:], a_[:], ALU.add))
                    over = [b_[0:1, 0:T], a_[0:1, 0:T]]
                    dve.wait_ge(s_out, 80)
                    dve.tensor_tensor(over[0], wtab[:, 1:T + 1], wtab[:, 0:T], ALU.subtract).then_inc(s_over, 1)
                    dve.wait_ge(s_over, 1)
                    dve.tensor_scalar(over[1], over[0], float(P * K), 0.0, ALU.subtract, ALU.max).then_inc(s_over, 1)
                    dve.wait_ge(s_over, 2)
                    dve.tensor_copy(xtab[:], over[1]).then_inc(s_over, 1)
                    dve.tensor_scalar(over[0], dtab[:], 0.0, None, ALU.is_gt).then_inc(s_over, 1)
                    dve.tensor_reduce(last_f[:, 1:2], dtab[:], AX.X, ALU.max).then_inc(s_over, 1)
                    dve.wait_ge(s_over, 5)
                    dve.scalar_tensor_tensor(over[1], c("iota")[0:1, 0:T], 1.0, over[0], ALU.add, ALU.mult).then_inc(s_over, 1)
                    dve.wait_ge(s_over, 6)
                    dve.tensor_reduce(last_f[:, 0:1], over[1], AX.X, ALU.max).then_inc(s_over, 1)
                    dve.wait_ge(s_over, 7)
                    dve.tensor_scalar(etab[:], last_f[:], 1.0, None, ALU.max).then_inc(s_over, 1)
                    dve.wait_ge(s_over, 8)
        clear_semaphores()
        if upto <= 1:
            return

        def gather_state(stack, prefix):
            G = {"ring": sbuf(stack, f"{prefix}ring", [P, 2, K, SLOT], F32),
                 "hot": sbuf(stack, f"{prefix}hot", [P, 2 * K, P], F32),
                 "src": sbuf(stack, f"{prefix}src", [P, 2 * K], I32),
                 "dst": sbuf(stack, f"{prefix}dst", [P, 2 * K], I32),
                 "rel": sbuf(stack, f"{prefix}rel", [P, K], F32),
                 "landed": [[sem(f"{prefix}landed{i}{g}") for g in range(NG)] for i in range(2)],
                 "have_src": sem(f"{prefix}have_src"), "have_dst": sem(f"{prefix}have_dst"),
                 "rel_s": Step(sem(f"{prefix}rel")), "hot_s": Step(sem(f"{prefix}onehot")),
                 "used": sem(f"{prefix}used"), "go": sem(f"{prefix}go"), "sp_go": sem(f"{prefix}sp_go"),
                 "sum": Step(sem(f"{prefix}sum")),
                 "ones_s": sem(f"{prefix}ones_set"),
                 "xring": sbuf(stack, f"{prefix}xring", [P, KX, SLOT], F32),
                 "xhot": sbuf(stack, f"{prefix}xhot", [P, KX, P], F32),
                 "xsrc": sbuf(stack, f"{prefix}xsrc", [P, KX], I32),
                 "xdst": sbuf(stack, f"{prefix}xdst", [P, KX], I32),
                 "xrel": sbuf(stack, f"{prefix}xrel", [P, KX], F32),
                 "xhave_src": sem(f"{prefix}xhave_src"), "xhave_dst": sem(f"{prefix}xhave_dst"),
                 "xlanded": sem(f"{prefix}xlanded"), "xrel_s": sem(f"{prefix}xrel"),
                 "xhot_s": sem(f"{prefix}xonehot"), "xused": Step(sem(f"{prefix}xused"))}
            return G

        def edges_over(eng, w):
            return eng.value_load(xtab[0:1, bass.ds(w, 1)], min_val=0, max_val=GE)

        def extra_rounds(eng, seen, over, body):
            with eng.If(over > 0):
                with eng.Fori(0, (over + (P * KX - 1)) // (P * KX)) as k:
                    body(k, eng.snap(seen, min_val=0, max_val=GE))
                    eng.reg_add(seen, seen, 1)

        def counter(eng, name):
            seen = eng.alloc_register(name)
            eng.reg_mov(seen, 0)
            return seen

        def gather_sync(sp, G, prefix):
            seen = counter(sp, f"{prefix}sp_rounds")
            at_round = counter(sp, f"{prefix}sp_at")

            def edges(name, at, k):
                return io[name][0:1, bass.ds(at, P * k)].rearrange("o (p c) -> (o p) c", p=P)

            def stage(i, w, turn):
                at = sp.value_load(wtab[0:1, bass.ds(w, 1)], min_val=0, max_val=GE)
                if turn is not None:
                    for g in range(NG):
                        sp.wait_ge(G["landed"][i][g], turn * KG * 16)
                    sp.sem_inc(G["sp_go"], 1)
                    sp.wait_ge(*G["hot_s"].before(w - 1))
                    sp.sem_inc(G["sp_go"], 1)
                    sp.wait_ge(G["have_src"], w * 16)
                    sp.wait_ge(G["have_dst"], w * 16)
                elif i:
                    sp.wait_ge(G["have_src"], 16)
                    sp.wait_ge(G["have_dst"], 16)
                sp.sem_inc(G["sp_go"], 1)
                sp.dma_start(G["src"][:, i * K:(i + 1) * K], edges("gnn_src", at, K)).then_inc(G["have_src"], 16)
                sp.dma_start(G["dst"][:, i * K:(i + 1) * K], edges("gnn_dst", at, K)).then_inc(G["have_dst"], 16)

            def extra(w):
                at = sp.value_load(wtab[0:1, bass.ds(w, 1)], min_val=0, max_val=GE)

                def body(k, n):
                    sp.wait_ge(*G["xused"].before(n))
                    sp.sem_inc(G["sp_go"], 1)
                    sp.reg_mov(at_round, sp.snap(at + k * (P * KX) + P * K))
                    place = sp.snap(at_round, min_val=0, max_val=GE)
                    sp.dma_start(G["xsrc"][:], edges("gnn_src", place, KX)).then_inc(G["xhave_src"], 16)
                    sp.dma_start(G["xdst"][:], edges("gnn_dst", place, KX)).then_inc(G["xhave_dst"], 16)
                    sp.wait_ge(G["xhave_src"], (n + 1) * 16)
                    sp.wait_ge(G["xhave_dst"], (n + 1) * 16)
                    sp.sem_inc(G["sp_go"], 1)
                extra_rounds(sp, seen, edges_over(sp, w), body)

            stage(0, 0, None)
            stage(1, 1, None)
            extra(0)
            with sp.Fori(1, T // 2) as t2:
                for i in range(2):
                    stage(i, t2 * 2 + i, t2)
                    extra(t2 * 2 + i - 1)
            extra(T - 1)
            sp.wait_ge(G["have_src"], T * 16)
            sp.wait_ge(G["have_dst"], T * 16)

        def gather_pool(pool, G, tab, prefix):
            seen = counter(pool, f"{prefix}pool_rounds")

            def gather(out, idx, s):
                pool.indirect_dma_start(out=out, out_offset=None, in_=tab,
                                        in_offset=bass.IndirectOffsetOnAxis(ap=idx, axis=0)).then_inc(s, 16)

            def body(k, n):
                pool.wait_ge(G["xhave_src"], (n + 1) * 16)
                pool.sem_inc(G["go"], 1)
                for x in range(KX):
                    gather(G["xring"][:, x, 0:D], G["xsrc"][:, x:x + 1], G["xlanded"])

            pool.wait_ge(G["ones_s"], 1)
            with pool.Fori(0, T // 2) as t2:
                for i in range(2):
                    w = t2 * 2 + i
                    over = edges_over(pool, w)
                    pool.wait_ge(G["have_src"], (w + 1) * 16)
                    pool.wait_ge(G["used"], w + 1)
                    pool.sem_inc(G["go"], 1)
                    for k in range(K):
                        gather(G["ring"][:, i, k, 0:D], G["src"][:, i * K + k:i * K + k + 1], G["landed"][i][k // KG])
                    extra_rounds(pool, seen, over, body)

        def hot_start(dve, G):
            dve.memset(G["ring"][:, :, :, D:SLOT], 1.0)
            dve.memset(G["xring"][:, :, D:SLOT], 1.0).then_inc(G["ones_s"], 1)
            G["rel_s"].start(dve)
            G["hot_s"].start(dve)

        def onehots(dve, G, w):
            at = (w % 2) * K
            dve.wait_ge(G["have_dst"], (w + 1) * 16)
            dve.wait_ge(*G["hot_s"].before(w))
            dve.tensor_scalar(G["rel"][:], G["dst"][:, bass.ds(at, K)], c("wbase")[:, bass.ds(w, 1)], None, ALU.add)\
               .then_inc(G["rel_s"].sem, 1)
            dve.wait_ge(*G["rel_s"].done(w))
            dve.wait_ge(G["used"], w + 1)
            dve.tensor_tensor(G["hot"][:, bass.ds(at, K), :], c("iota").unsqueeze(1).broadcast_to([P, K, P]),
                              G["rel"][:].unsqueeze(2).broadcast_to([P, K, P]), ALU.is_equal).then_inc(G["hot_s"].sem, 1)

        def extra_onehots(dve, G, seen, w, over):
            def body(k, n):
                dve.wait_ge(G["xhave_dst"], (n + 1) * 16)
                dve.wait_ge(*G["xused"].before(n))
                dve.tensor_scalar(G["xrel"][:], G["xdst"][:], c("wbase")[:, bass.ds(w, 1)], None, ALU.add).then_inc(G["xrel_s"], 1)
                dve.wait_ge(G["xrel_s"], n + 1)
                dve.tensor_tensor(G["xhot"][:], c("iota").unsqueeze(1).broadcast_to([P, KX, P]),
                                  G["xrel"][:].unsqueeze(2).broadcast_to([P, KX, P]), ALU.is_equal).then_inc(G["xhot_s"], 1)
            extra_rounds(dve, seen, over, body)

        def add_rows(pe, hot, row, first_one):
            return pe.matmul(bAGG[:, 0:D + 1], hot, row, start=first_one, stop=False, skip_group_check=True)

        def aggregate(pe, G, w, i, turn, g):
            if g == 0:
                pe.wait_ge(*G["evict"].before(w))
                pe.wait_ge(*G["hot_s"].done(w))
            pe.wait_ge(G["landed"][i][g], (turn + 1) * KG * 16)
            for k in range(g * KG, (g + 1) * KG):
                last = add_rows(pe, G["hot"][:, i * K + k, :], G["ring"][:, i, k, :], k == 0)
            if g == NG - 1:
                last.then_inc(G["used"], 1)

        def aggregate_end(pe, G, seen, w, over):
            def body(k, n):
                pe.wait_ge(G["xhot_s"], n + 1)
                pe.wait_ge(G["xlanded"], (n + 1) * KX * 16)
                for x in range(KX):
                    last = add_rows(pe, G["xhot"][:, x, :], G["xring"][:, x, :], False)
                last.then_inc(G["xused"].sem, 1)
            extra_rounds(pe, seen, over, body)
            pe.matmul(bAGG[:, D:D + 1], zeros16[:, 0:P], zeros16[:, 0:1], start=False, stop=True, skip_group_check=True)\
                .then_inc(G["sum"].sem, 1)

        def gather_start(pe, G):
            G["sum"].start(pe)
            G["xused"].start(pe)
            pe.sem_inc(G["used"], 2)

        def over_windows(eng, body):
            with eng.Fori(0, T - 2) as w:
                body(w, w + 1, True)
            body(T - 2, T - 1, False)
            body(T - 1, None, False)

        def rank_state(stack, prefix, n):
            R = {"n": n, "count": sbuf(stack, f"{prefix}count", [P, T], F32)}
            R["b"] = [dict(
                lo=sbuf(stack, f"{prefix}lo{b}", [P, RB, P], BF16), hi=sbuf(stack, f"{prefix}hi{b}", [P, RB, T], BF16),
                loT=sbuf(stack, f"{prefix}loT{b}", [P, RB * P], F32), row=sbuf(stack, f"{prefix}row{b}", [P, RB * P], I32),
                near=sbuf(stack, f"{prefix}near{b}", [P, RB], F32), far=sbuf(stack, f"{prefix}far{b}", [P, RB], F32),
                prod=sbuf(stack, f"{prefix}prod{b}", [P, RB, T], F32), eq=sbuf(stack, f"{prefix}eq{b}", [P, RB * (RB + 1) // 2 * P], BF16),
                s=steps(f"{prefix}rank{b}", ["hot", "count", "turned", "loT", "far", "counted", "prod", "farsum", "near", "pos"]),
                row_in=Step(sem(f"{prefix}row_in{b}"), 16)) for b in range(n)]
            return R

        def rank_start(eng, R, names):
            for B in R["b"]:
                for nme in names:
                    B["s"][nme].start(eng)

        def rank_hot(dve, R, b, w, batch):
            B, s = R["b"][b], R["b"][b]["s"]
            dve.wait_ge(*s["counted"].before(w))
            dve.tensor_tensor(B["lo"][:], c("iota").unsqueeze(1).broadcast_to([P, RB, P]),
                              flo[:, bass.ds(batch * RB, RB)].unsqueeze(2).broadcast_to([P, RB, P]), ALU.is_equal)
            dve.tensor_tensor(B["hi"][:], c("iota")[:, 0:T].unsqueeze(1).broadcast_to([P, RB, T]),
                              fhi[:, bass.ds(batch * RB, RB)].unsqueeze(2).broadcast_to([P, RB, T]), ALU.is_equal)\
               .then_inc(s["hot"].sem, 1)

        def rank_base(dve, R, b, w):
            s = R["b"][b]["s"]
            prev = R["b"][b - 1]["s"]["counted"].done(w) if b else R["b"][-1]["s"]["counted"].before(w)
            dve.wait_ge(*prev)
            dve.tensor_tensor(R["count"][:], bC[:, 0:T], first[:, 0:T], ALU.add).then_inc(s["count"].sem, 1)

        def rank_turn(pe, R, b, w):
            B, s = R["b"][b], R["b"][b]["s"]
            pe.wait_ge(*s["hot"].done(w))
            pe.wait_ge(*(R["b"][b - 1]["s"]["loT"].done(w) if b else R["b"][-1]["s"]["loT"].before(w)))
            for k in range(RB):
                last = pe.transpose(bOT[:, k * P:(k + 1) * P], B["lo"][:, k, :], ident16[:])
            last.then_inc(s["turned"].sem, 1)

        def rank_turned(act, R, b, w):
            B, s = R["b"][b], R["b"][b]["s"]
            act.wait_ge(*s["turned"].done(w))
            act.wait_ge(*s["far"].before(w))
            act.activation(B["loT"][:], bOT[:, 0:RB * P], ACT.Copy).then_inc(s["loT"].sem, 1)

        def rank_count(pe, R, b, w):
            B, s = R["b"][b], R["b"][b]["s"]
            pe.wait_ge(*s["loT"].done(w))
            pe.wait_ge(*s["count"].done(w))
            pe.wait_ge(*(R["b"][b - 1]["s"]["prod"].done(w) if b else R["b"][-1]["s"]["prod"].before(w)))
            for k in range(RB):
                last = pe.matmul(bP[:, k * T:(k + 1) * T], B["loT"][:, k * P:(k + 1) * P], R["count"][:], start=True, stop=True, skip_group_check=True)
            last.then_inc(s["far"].sem, 1)
            for k in range(RB):
                last = pe.matmul(bC[:, 0:T], B["lo"][:, k, :], B["hi"][:, k, :], start=False, stop=False, skip_group_check=True)
            last.then_inc(s["counted"].sem, 1)

        def rank_near(dve, R, b, w, batch):
            B, s = R["b"][b], R["b"][b]["s"]
            dve.wait_ge(*B["row_in"].done(w))
            dve.wait_ge(*s["pos"].before(w))
            for k in range(RB):
                n = (k + 1) * P
                at = k * (k + 1) // 2 * P
                last = dve.scalar_tensor_tensor(B["eq"][:, at:at + n], B["row"][:, 0:n], fdst[:, bass.ds(batch * RB + k, 1)],
                                                c("rankmask")[:, k * RB * P:k * RB * P + n], ALU.is_equal, ALU.mult,
                                                accum_out=B["near"][:, k:k + 1])
            last.then_inc(s["near"].sem, 1)

        def rank_place(dve, R, b, w, batch):
            B, s = R["b"][b], R["b"][b]["s"]
            dve.wait_ge(*s["far"].done(w))
            dve.tensor_tensor(flat(B["prod"][:]), bP[:, 0:RB * T], flat(B["hi"][:]), ALU.mult).then_inc(s["prod"].sem, 1)
            dve.wait_ge(*s["prod"].done(w))
            dve.tensor_reduce(B["far"][:], B["prod"][:], AX.X, ALU.add).then_inc(s["farsum"].sem, 1)
            dve.wait_ge(*s["farsum"].done(w))
            dve.wait_ge(*s["near"].done(w))
            dve.tensor_tensor(pos[:, bass.ds(batch * RB, RB)], B["near"][:], B["far"][:], ALU.add).then_inc(s["pos"].sem, 1)

        def rank_load(act, R, b, w, batch):
            B, s = R["b"][b], R["b"][b]["s"]
            act.wait_ge(*s["near"].before(w))
            act.dma_start(B["row"][:], io["ffn_dst_rows"][0:1, bass.ds(batch * RB * P, RB * P)].partition_broadcast(P))\
                .then_inc(B["row_in"].sem, 16)

        DVE_RANK = ("hot", "count", "prod", "farsum", "near", "pos")
        PE_RANK = ("turned", "far", "counted")

        with ExitStack() as b:
            G = gather_state(b, "b_")
            R = rank_state(b, "b_", RB1)
            wkv = sbuf(b, "wkv", [P, 2, 2 * D], F32)
            wq = sbuf(b, "wq", [P, 2, D], F32)
            xw = sbuf(b, "xw", [P, D], F32)
            xT = sbuf(b, "xT_b", [P, 2 * P], F32)
            r1 = sbuf(b, "r1", [P, D], F32)
            dg = sbuf(b, "dg", [P, 1], F32)
            rinv = sbuf(b, "rinv", [P, 1], F32)
            h0 = sbuf(b, "h0", [P, D], F32)
            hh = sbuf(b, "hh", [P, D], F32)
            hT = sbuf(b, "hT", [P, 2 * P], F32)
            km = sbuf(b, "km", [P, D], F32)
            ke = sbuf(b, "ke", [P, D], F32)
            kf = sbuf(b, "kf", [P, D], F32)
            vx = sbuf(b, "vx", [P, 2, P + 1], F32)
            qm = sbuf(b, "qm", [P, D], F32)
            qe = sbuf(b, "qe", [P, D], F32)
            qf = sbuf(b, "qf", [P, D], F32)
            us = sbuf(b, "us_b", [P, D], F32)
            rs = sbuf(b, "rs_b", [P, D], F32)
            S = steps("b", ["xs", "xTp", "xT", "kv", "q", "km", "qm", "vx", "ke", "qe", "kf", "qf", "KV", "dg", "rinv", "h0", "h",
                            "hTp", "hT", "ur", "rs", "us"])
            SD = steps("b", ["inx", "inR", "outq", "outU", "outR"], 16)
            b_load = sem("b_load")
            G["evict"] = S["h0"]
            with nc.Block() as block:
                @block.gpsimd
                def _(pool):
                    gather_pool(pool, G, table[0], "b_")

                @block.sync
                def _(sp):
                    sp.dma_start(wkv[:], io["wkv"]).then_inc(b_load, 16)
                    sp.dma_start(wq[:], io["wq"]).then_inc(b_load, 16)
                    gather_sync(sp, G, "b_")

                @block.scalar
                def _(act):
                    for n in ("xs", "xT", "ke", "qe", "h", "hT", "us"):
                        S[n].start(act)
                    for s in SD.values():
                        s.start(act)
                    for B in R["b"]:
                        B["row_in"].start(act)
                    rank_start(act, R, ("loT",))

                    def load_x(t):
                        act.wait_ge(*S["xs"].before(t))
                        act.dma_start(xw[:], tile_rows(io["x"], t)).then_inc(SD["inx"].sem, 16)

                    def load_own(t):
                        act.wait_ge(*S["h0"].before(t))
                        act.dma_start(r1[:], tile_rows(own[0], t)).then_inc(SD["inR"].sem, 16)

                    def normalise(t):
                        act.wait_ge(*S["xTp"].before(t))
                        act.wait_ge(*SD["inx"].done(t))
                        act.activation(xs[:], xw[:], ACT.Identity, bias=nmr[:, bass.ds(t, 1)],
                                       scale=rstd[:, bass.ds(t, 1)]).then_inc(S["xs"].sem, 1)

                    def turned(t):
                        act.wait_ge(*S["xTp"].done(t))
                        act.wait_ge(*S["q"].before(t))
                        act.activation(xT[:], bT[:, 0:D], ACT.Copy).then_inc(S["xT"].sem, 1)

                    def body(w, v, more):
                        if v is not None:
                            load_x(v)
                        act.wait_ge(*S["h0"].done(w))
                        act.wait_ge(*S["hTp"].before(w))
                        act.activation(hh[:], h0[:], ACT.Relu).then_inc(S["h"].sem, 1)
                        if v is not None:
                            load_own(v)
                        act.wait_ge(*S["km"].done(w))
                        act.activation(ke[:], km[:], ACT.Exp).then_inc(S["ke"].sem, 1)
                        act.wait_ge(*S["qm"].done(w))
                        act.activation(qe[:], qm[:], ACT.Exp).then_inc(S["qe"].sem, 1)
                        rank_turned(act, R, 0, w)
                        act.wait_ge(*S["hTp"].done(w))
                        act.activation(hT[:], bT[:, 0:D], ACT.Copy).then_inc(S["hT"].sem, 1)
                        if v is not None:
                            normalise(v)
                        act.wait_ge(*S["qf"].done(w))
                        act.dma_start(qT_d[bass.ds(w, 1)].rearrange("t p d -> (t p) d"), qf[:]).then_inc(SD["outq"].sem, 16)
                        rank_turned(act, R, 1, w)
                        if v is not None:
                            turned(v)
                            rank_load(act, R, 0, v, v * RB1)
                        act.wait_ge(*S["rs"].done(w))
                        act.wait_ge(*SD["outU"].before(w))
                        act.activation(us[:], bMM[:, 0:D], ACT.Copy).then_inc(S["us"].sem, 1)
                        act.dma_start(tile_rows(own[1], w), rs[:]).then_inc(SD["outR"].sem, 16)
                        act.wait_ge(*S["us"].done(w))
                        act.dma_start(tile_rows(table[1], w), us[:]).then_inc(SD["outU"].sem, 16)
                        if v is not None:
                            rank_load(act, R, 1, v, v * RB1 + 1)

                    load_x(0)
                    load_own(0)
                    rank_load(act, R, 0, 0, 0)
                    rank_load(act, R, 1, 0, 1)
                    normalise(0)
                    turned(0)
                    over_windows(act, body)
                    for s in SD.values():
                        act.wait_ge(s.sem, (T + 1) * 16)

                @block.tensor
                def _(pe):
                    for n in ("xTp", "kv", "q", "KV", "hTp", "ur"):
                        S[n].start(pe)
                    rank_start(pe, R, ("turned", "far"))
                    R["b"][0]["s"]["counted"].start(pe)
                    gather_start(pe, G)
                    seen = counter(pe, "b_pe_rounds")
                    pe.wait_ge(b_load, 32)
                    pe.matmul(bC[:, 0:T], zeros16[:, 0:P], zeros16[:, 0:T], start=True, stop=False, skip_group_check=True)\
                        .then_inc(R["b"][-1]["s"]["counted"].sem, 1)
                    pe.matmul(bKV[:, 0:2 * (P + 1)], zeros16[:, 0:P], zeros16[:, 0:2 * (P + 1)], start=True, stop=False, skip_group_check=True)

                    def turn_x(t):
                        pe.wait_ge(*S["xs"].done(t))
                        pe.wait_ge(*S["hT"].before(t))
                        for j in range(2):
                            last = pe.transpose(bT[:, j * P:(j + 1) * P], xs[:, j * P:(j + 1) * P], c("ident"))
                        last.then_inc(S["xTp"].sem, 1)

                    def body(w, v, i, turn):
                        over = edges_over(pe, v) if v is not None else None
                        pe.wait_ge(*S["xT"].done(w))
                        pe.wait_ge(*S["us"].before(w))
                        for j in range(2):
                            last = pe.matmul(bMM[:], xT[:, j * P:(j + 1) * P], wkv[:, j, :], start=(j == 0), stop=(j == 1))
                        last.then_inc(S["kv"].sem, 1)
                        pe.wait_ge(*S["qf"].before(w))
                        for o in range(2):
                            for j in range(2):
                                last = pe.matmul(bQ[:, o * P:(o + 1) * P], wq[:, j, o * P:(o + 1) * P],
                                                 xT[:, j * P:(j + 1) * P], start=(j == 0), stop=(j == 1))
                        last.then_inc(S["q"].sem, 1)
                        if v is not None:
                            aggregate(pe, G, v, i, turn, 0)
                        rank_turn(pe, R, 0, w)
                        pe.wait_ge(*S["h"].done(w))
                        for j in range(2):
                            last = pe.transpose(bT[:, j * P:(j + 1) * P], hh[:, j * P:(j + 1) * P], c("ident"))
                        last.then_inc(S["hTp"].sem, 1)
                        if v is not None:
                            aggregate(pe, G, v, i, turn, 1)
                        rank_count(pe, R, 0, w)
                        pe.wait_ge(*S["kf"].done(w))
                        pe.wait_ge(*S["vx"].done(w))
                        for j in range(2):
                            last = pe.matmul(bKV[:, j * (P + 1):(j + 1) * (P + 1)], kf[:, j * P:(j + 1) * P], vx[:, j, :],
                                             start=False, stop=False, skip_group_check=True)
                        last.then_inc(S["KV"].sem, 1)
                        pe.wait_ge(*S["hT"].done(w))
                        for j in range(2):
                            last = pe.matmul(bMM[:], hT[:, j * P:(j + 1) * P], wlr2[:, j, :], start=(j == 0), stop=(j == 1))
                        last.then_inc(S["ur"].sem, 1)
                        rank_turn(pe, R, 1, w)
                        if v is not None:
                            turn_x(v)
                            aggregate(pe, G, v, i, turn, 2)
                        rank_count(pe, R, 1, w)
                        if v is not None:
                            aggregate_end(pe, G, seen, v, over)

                    turn_x(0)
                    for g in range(NG):
                        aggregate(pe, G, 0, 0, 0, g)
                    aggregate_end(pe, G, seen, 0, edges_over(pe, 0))
                    with pe.Fori(0, T // 2 - 1) as t2:
                        body(t2 * 2, t2 * 2 + 1, 1, t2)
                        body(t2 * 2 + 1, t2 * 2 + 2, 0, t2 + 1)
                    body(T - 2, T - 1, 1, T // 2 - 1)
                    body(T - 1, None, None, None)

                @block.vector
                def _(dve):
                    for n in ("km", "qm", "vx", "kf", "qf", "dg", "rinv", "h0", "rs"):
                        S[n].start(dve)
                    rank_start(dve, R, DVE_RANK)
                    hot_start(dve, G)
                    seen = counter(dve, "b_dve_rounds")

                    def body(w, v, more):
                        over = edges_over(dve, v) if v is not None else None
                        dve.wait_ge(*G["sum"].done(w))
                        dve.tensor_scalar(dg[:], bAGG[:, D:D + 1], 1.0, None, ALU.max).then_inc(S["dg"].sem, 1)
                        dve.wait_ge(*S["dg"].done(w))
                        dve.reciprocal(rinv[:], dg[:]).then_inc(S["rinv"].sem, 1)
                        dve.wait_ge(*S["rinv"].done(w))
                        dve.wait_ge(*SD["inR"].done(w))
                        dve.wait_ge(*S["h"].before(w))
                        dve.scalar_tensor_tensor(h0[:], bAGG[:, 0:D], rinv[:], r1[:], ALU.mult, ALU.add).then_inc(S["h0"].sem, 1)
                        dve.wait_ge(*S["kv"].done(w))
                        dve.wait_ge(*S["ke"].before(w))
                        dve.tensor_scalar(km[:], bMM[:, 0:D], 0.0, None, ALU.min).then_inc(S["km"].sem, 1)
                        dve.wait_ge(*S["KV"].before(w))
                        dve.tensor_copy(vx[:, :, 0:P], bMM[:, D:2 * D].rearrange("p (a b) -> p a b", a=2))
                        dve.tensor_copy(vx[:, :, P:P + 1], c("real")[:, bass.ds(w, 1)].unsqueeze(1).broadcast_to([P, 2, 1])).then_inc(S["vx"].sem, 1)
                        dve.wait_ge(*S["ke"].done(w))
                        dve.scalar_tensor_tensor(kf[:], bMM[:, 0:D], 0.0, ke[:], ALU.max, ALU.add).then_inc(S["kf"].sem, 1)
                        dve.wait_ge(*S["q"].done(w))
                        dve.wait_ge(*S["qe"].before(w))
                        dve.tensor_scalar(qm[:], bQ[:, 0:D], 0.0, None, ALU.min).then_inc(S["qm"].sem, 1)
                        rank_hot(dve, R, 0, w, w * RB1)
                        rank_base(dve, R, 0, w)
                        if more:
                            onehots(dve, G, w + 2)
                        dve.wait_ge(*S["qe"].done(w))
                        dve.wait_ge(*SD["outq"].before(w))
                        dve.scalar_tensor_tensor(qf[:], bQ[:, 0:D], 0.0, qe[:], ALU.max, ALU.add).then_inc(S["qf"].sem, 1)
                        rank_hot(dve, R, 1, w, w * RB1 + 1)
                        rank_near(dve, R, 0, w, w * RB1)
                        rank_place(dve, R, 0, w, w * RB1)
                        rank_base(dve, R, 1, w)
                        dve.wait_ge(*S["ur"].done(w))
                        dve.wait_ge(*SD["outR"].before(w))
                        dve.tensor_tensor(rs[:], bMM[:, D:2 * D], r("gnn_b2"), ALU.add).then_inc(S["rs"].sem, 1)
                        rank_near(dve, R, 1, w, w * RB1 + 1)
                        rank_place(dve, R, 1, w, w * RB1 + 1)
                        if v is not None:
                            extra_onehots(dve, G, seen, v, over)

                    onehots(dve, G, 0)
                    onehots(dve, G, 1)
                    extra_onehots(dve, G, seen, 0, edges_over(dve, 0))
                    over_windows(dve, body)
        clear_semaphores()
        if upto <= 2:
            return

        with ExitStack() as b:
            G = gather_state(b, "c_")
            R = rank_state(b, "c_", RB2)
            w1 = sbuf(b, "w1", [P, 2, D], F32)
            w2 = sbuf(b, "w2", [P, 2, D], F32)
            wg = sbuf(b, "wg", [P, 2, 16], F32)
            mb1 = sbuf(b, "mb1", [P, 2], F32)

            def row_buffer(name, n=D):
                return sbuf(b, name, [P, n], F32)
            xw, r2, qT = row_buffer("xw_c", 2 * D), row_buffer("r2"), row_buffer("qT")
            dg, rinv, lg, lx = row_buffer("dg_c", 1), row_buffer("rinv_c", 1), row_buffer("lg"), row_buffer("lx")
            den, rden, tz, s1, a1, x1, x1b = (row_buffer("den", 8), row_buffer("rden", 8), row_buffer("tz"), row_buffer("s1"),
                                              row_buffer("a1"), row_buffer("x1"), row_buffer("x1b"))
            x1T, gT, s2, a2, mix = row_buffer("x1T"), row_buffer("gT"), row_buffer("s2"), row_buffer("a2"), row_buffer("mix")
            x2, x2n, x2nT = row_buffer("x2"), row_buffer("x2n"), row_buffer("x2nT")
            LN = [dict(st=row_buffer(f"lnst{i}", 6), mv=row_buffer(f"lnmv{i}", 2), sd=row_buffer(f"lnsd{i}", 1),
                       rs=row_buffer(f"lnrs{i}", 1), s=steps(f"c_ln{i}", ["st", "mv", "sd", "rs"])) for i in range(3)]
            atp = sbuf(b, "atp", [P, T, 16], F32)
            S = steps("c", ["xs", "t", "den", "rden", "tz", "s1", "a1", "x1", "x1b", "x1Tp", "x1T", "h", "g", "y", "s2", "a2", "mix",
                            "dg", "rinv", "lg", "lx", "x2", "x2n", "x2Tp", "x2T", "gat", "gatev"])
            SD = steps("c", ["inx", "inr", "inq", "outx2", "outT"], 16)
            G["evict"] = S["lg"]
            c_load = sem("c_load")
            s_kv = sem("c_kvbd")
            turns = sem("c_turns")
            s_tab = sem("c_table")
            c_out = sem("c_out")

            def norm_stats(dve, i, t, v):
                n = LN[i]
                dve.bn_stats(n["st"][:], v).then_inc(n["s"]["st"].sem, 1)
                dve.wait_ge(*n["s"]["st"].done(t))
                dve.sem_inc(turns, 1)
                dve.bn_aggr(n["mv"][:], n["st"][:]).then_inc(n["s"]["mv"].sem, 1)

            def norm_scale(dve, i, t):
                n = LN[i]
                dve.wait_ge(*n["s"]["sd"].done(t))
                dve.reciprocal(n["rs"][:], n["sd"][:]).then_inc(n["s"]["rs"].sem, 1)

            def norm_root(act, i, t):
                n = LN[i]
                act.wait_ge(*n["s"]["mv"].done(t))
                act.activation(n["sd"][:], n["mv"][:, 1:2], ACT.Sqrt, bias=c("eps")).then_inc(n["s"]["sd"].sem, 1)

            with nc.Block() as block:
                @block.gpsimd
                def _(pool):
                    gather_pool(pool, G, table[1], "c_")

                @block.sync
                def _(sp):
                    sp.dma_start(w1[:], io["w1"]).then_inc(c_load, 16)
                    sp.dma_start(w2[:], io["w2"]).then_inc(c_load, 16)
                    sp.dma_start(wg[:], io["wgat"]).then_inc(c_load, 16)
                    sp.dma_start(mb1[:], io["mix_b1"]).then_inc(c_load, 16)
                    sp.dma_start(sorted_d[FE:FE + 2 * P, :].rearrange("(p k) d -> p (k d)", p=P),
                                 zeros16[:, 0:4 * TW].bitcast(F32)).then_inc(c_out, 16)
                    gather_sync(sp, G, "c_")
                    sp.wait_ge(s_tab, 3)
                    sp.dma_start(heads_d.rearrange("(t p) d -> p t d", p=P), trow[:]).then_inc(c_out, 16)
                    sp.wait_ge(c_out, 32)

                @block.scalar
                def _(act):
                    for n in ("xs", "x1T", "g", "x2T"):
                        S[n].start(act)
                    for s in SD.values():
                        s.start(act)
                    for n in LN:
                        n["s"]["sd"].start(act)
                    for B in R["b"]:
                        B["row_in"].start(act)
                    rank_start(act, R, ("loT",))

                    def x_at(t):
                        return xw[:, bass.ds((t % 2) * D, D)]

                    def load_x(t):
                        act.dma_start(x_at(t), tile_rows(io["x"], t)).then_inc(SD["inx"].sem, 16)

                    def load_q(t):
                        act.dma_start(qT[:], qT_d[bass.ds(t, 1)].rearrange("t p d -> (t p) d")).then_inc(SD["inq"].sem, 16)

                    def load_r(t):
                        act.dma_start(r2[:], tile_rows(own[1], t)).then_inc(SD["inr"].sem, 16)

                    def body(w, v, more):
                        if v is not None:
                            act.wait_ge(*SD["inx"].done(v))
                            act.wait_ge(*S["s1"].before(v))
                            act.activation(xs[:], x_at(v), ACT.Identity, bias=nmr[:, bass.ds(v, 1)],
                                           scale=rstd[:, bass.ds(v, 1)]).then_inc(S["xs"].sem, 1)
                        if w is not None:
                            norm_root(act, 1, w)
                        if v is not None:
                            norm_root(act, 0, v)
                        if w is not None:
                            norm_root(act, 2, w)
                            rank_turned(act, R, 0, w)
                        if v is not None:
                            act.wait_ge(*S["x1Tp"].done(v))
                            act.activation(x1T[:], bT[:, 0:D], ACT.Copy).then_inc(S["x1T"].sem, 1)
                            act.wait_ge(*S["h"].done(v))
                            act.activation(gT[:, 0:P], bMM[:, 0:P], ACT.Gelu, bias=mb1[:, 0:1])
                            act.activation(gT[:, P:2 * P], bMM[:, P:2 * P], ACT.Gelu, bias=mb1[:, 1:2]).then_inc(S["g"].sem, 1)
                        if w is not None:
                            act.dma_start(tile_rows(x2_d, w), x2[:]).then_inc(SD["outx2"].sem, 16)
                            if more:
                                act.wait_ge(*S["lx"].done(w))
                                act.wait_ge(*SD["inx"].done(v))
                                load_x(w + 2)
                        if v is not None:
                            act.wait_ge(*S["lx"].before(v))
                            load_r(v)
                            if w is None or more:
                                act.wait_ge(*S["t"].done(v))
                                load_q(v + 1)
                            if w is not None:
                                rank_load(act, R, 0, v, v + T * RB1)
                        if w is not None:
                            act.wait_ge(*S["x2Tp"].done(w))
                            act.wait_ge(*SD["outT"].before(w))
                            act.activation(x2nT[:], bT[:, 0:D], ACT.Copy).then_inc(S["x2T"].sem, 1)
                            act.wait_ge(*S["x2T"].done(w))
                            act.dma_start(x2nT_d[bass.ds(w, 1)].rearrange("t p d -> (t p) d"), x2nT[:]).then_inc(SD["outT"].sem, 16)

                    act.wait_ge(c_load, 64)
                    load_x(0)
                    act.wait_ge(*SD["inx"].done(0))
                    load_x(1)
                    load_q(0)
                    rank_load(act, R, 0, 0, T * RB1)
                    body(None, 0, False)
                    over_windows(act, body)
                    for s in SD.values():
                        act.wait_ge(s.sem, (T + 1) * 16)

                @block.tensor
                def _(pe):
                    for n in ("t", "x1Tp", "h", "y", "x2Tp", "gat"):
                        S[n].start(pe)
                    rank_start(pe, R, PE_RANK)
                    gather_start(pe, G)
                    seen = counter(pe, "c_pe_rounds")
                    pe.wait_ge(c_load, 64)
                    pe.wait_ge(s_kv, 1)

                    def body(w, v, i, turn):
                        over = edges_over(pe, v) if v is not None else None
                        prev = 0 if w is None else w
                        if v is not None:
                            pe.wait_ge(*SD["inq"].done(v))
                            pe.wait_ge(*S["tz"].before(v))
                            for j in range(2):
                                last = pe.matmul(bQ[:, j * (P + 4):(j + 1) * (P + 4)], qT[:, j * P:(j + 1) * P], kvbd[:, j, :],
                                                 start=True, stop=True, skip_group_check=True)
                            last.then_inc(S["t"].sem, 1)
                            aggregate(pe, G, v, i, turn, 0)
                        if w is not None:
                            rank_turn(pe, R, 0, w)
                        if v is not None:
                            pe.wait_ge(*S["x1"].done(v))
                            pe.wait_ge(*S["x2T"].before(prev))
                            for j in range(2):
                                last = pe.transpose(bT[:, j * P:(j + 1) * P], x1[:, j * P:(j + 1) * P], c("ident"))
                            last.then_inc(S["x1Tp"].sem, 1)
                        if w is not None:
                            rank_count(pe, R, 0, w)
                        if v is not None:
                            pe.wait_ge(*S["x1T"].done(v))
                            pe.wait_ge(*S["gatev"].before(prev))
                            for o in range(2):
                                for j in range(2):
                                    last = pe.matmul(bMM[:, o * P:(o + 1) * P], w1[:, j, o * P:(o + 1) * P],
                                                     x1T[:, j * P:(j + 1) * P], start=(j == 0), stop=(j == 1))
                            last.then_inc(S["h"].sem, 1)
                            aggregate(pe, G, v, i, turn, 1)
                            pe.wait_ge(*S["g"].done(v))
                            pe.wait_ge(*S["s2"].before(v))
                            for j in range(2):
                                last = pe.matmul(bKV[:, 0:D], gT[:, j * P:(j + 1) * P], w2[:, j, :], start=(j == 0), stop=(j == 1))
                            last.then_inc(S["y"].sem, 1)
                        if w is not None:
                            pe.wait_ge(*S["x2n"].done(w))
                            for j in range(2):
                                last = pe.transpose(bT[:, j * P:(j + 1) * P], x2n[:, j * P:(j + 1) * P], c("ident"))
                            last.then_inc(S["x2Tp"].sem, 1)
                        if v is not None:
                            aggregate(pe, G, v, i, turn, 2)
                        if w is not None:
                            pe.wait_ge(*S["x2T"].done(w))
                            for j in range(2):
                                last = pe.matmul(bMM[:, 0:16], x2nT[:, j * P:(j + 1) * P], wg[:, j, :], start=(j == 0), stop=(j == 1))
                            last.then_inc(S["gat"].sem, 1)
                        if v is not None:
                            aggregate_end(pe, G, seen, v, over)

                    body(None, 0, 0, 0)
                    with pe.Fori(0, T // 2 - 1) as t2:
                        body(t2 * 2, t2 * 2 + 1, 1, t2)
                        body(t2 * 2 + 1, t2 * 2 + 2, 0, t2 + 1)
                    body(T - 2, T - 1, 1, T // 2 - 1)
                    body(T - 1, None, None, None)

                @block.vector
                def _(dve):
                    for n in ("den", "rden", "tz", "s1", "a1", "x1", "x1b", "s2", "a2", "mix", "dg", "rinv", "lg", "lx", "x2", "x2n", "gatev"):
                        S[n].start(dve)
                    for n in LN:
                        for k in ("st", "mv", "rs"):
                            n["s"][k].start(dve)
                    rank_start(dve, R, DVE_RANK)
                    hot_start(dve, G)
                    seen = counter(dve, "c_dve_rounds")
                    for j in range(2):
                        at = j * (P + 1)
                        dve.tensor_tensor(kvbd[:, j, 0:P], bKV[:, at:at + P], c("kvmask")[:, 0:P], ALU.mult)
                        last = dve.tensor_tensor(kvbd[:, j, P:P + 4], bKV[:, at + P:at + P + 1].broadcast_to([P, 4]), c("kvmask")[:, P:P + 4], ALU.mult)
                    last.then_inc(s_kv, 1)
                    bq = bQ[:, 0:2 * (P + 4)].rearrange("p (j n) -> p j n", j=2)

                    def body(w, v, more):
                        over = edges_over(dve, v) if v is not None else None
                        if w is not None:
                            dve.wait_ge(*S["y"].done(w))
                            dve.wait_ge(*S["x1b"].done(w))
                            dve.tensor_tensor(s2[:], bKV[:, 0:D], x1b[:], ALU.add).then_inc(S["s2"].sem, 1)
                            dve.wait_ge(*G["sum"].done(w))
                            dve.tensor_scalar(dg[:], bAGG[:, D:D + 1], 1.0, None, ALU.max).then_inc(S["dg"].sem, 1)
                            dve.wait_ge(*S["s2"].done(w))
                            dve.bn_stats(LN[1]["st"][:], s2[:]).then_inc(LN[1]["s"]["st"].sem, 1)
                            dve.wait_ge(*S["dg"].done(w))
                            dve.reciprocal(rinv[:], dg[:]).then_inc(S["rinv"].sem, 1)
                            dve.wait_ge(*LN[1]["s"]["st"].done(w))
                            dve.sem_inc(turns, 1)
                            dve.bn_aggr(LN[1]["mv"][:], LN[1]["st"][:]).then_inc(LN[1]["s"]["mv"].sem, 1)
                            rank_hot(dve, R, 0, w, w + T * RB1)
                            dve.wait_ge(*S["rinv"].done(w))
                            dve.wait_ge(*SD["inr"].done(w))
                            dve.scalar_tensor_tensor(lg[:], bAGG[:, 0:D], rinv[:], r2[:], ALU.mult, ALU.add).then_inc(S["lg"].sem, 1)
                        if v is not None:
                            dve.wait_ge(*S["t"].done(v))
                            dve.tensor_scalar(den[:].rearrange("p (j n) -> p j n", j=2), bq[:, :, P:P + 4], 1e-6, None, ALU.add).then_inc(S["den"].sem, 1)
                        if w is not None:
                            dve.wait_ge(*LN[1]["s"]["mv"].done(w))
                            dve.scalar_tensor_tensor(a2[:], s2[:], LN[1]["mv"][:, 0:1], r("ln2_g"), ALU.subtract, ALU.mult).then_inc(S["a2"].sem, 1)
                        if v is not None:
                            dve.wait_ge(*S["den"].done(v))
                            dve.reciprocal(rden[:], den[:]).then_inc(S["rden"].sem, 1)
                        if w is not None:
                            norm_scale(dve, 1, w)
                        if v is not None:
                            dve.wait_ge(*S["rden"].done(v))
                            dve.tensor_tensor(tz[:].rearrange("p (j h n) -> p j h n", j=2, h=4),
                                              bq[:, :, 0:P].rearrange("p j (h n) -> p j h n", h=4),
                                              rden[:].rearrange("p (j h) -> p j h", j=2).unsqueeze(3).broadcast_to([P, 2, 4, DH]),
                                              ALU.mult).then_inc(S["tz"].sem, 1)
                        if w is not None:
                            dve.wait_ge(*S["lg"].done(w))
                            dve.wait_ge(*SD["inx"].done(w))
                            dve.tensor_tensor(lx[:], lg[:], xw[:, bass.ds((w % 2) * D, D)], ALU.add).then_inc(S["lx"].sem, 1)
                            dve.wait_ge(*S["a2"].done(w))
                            dve.wait_ge(*LN[1]["s"]["rs"].done(w))
                            dve.scalar_tensor_tensor(mix[:], a2[:], LN[1]["rs"][:], r("ln2_b"), ALU.mult, ALU.add).then_inc(S["mix"].sem, 1)
                        if v is not None:
                            dve.wait_ge(*S["tz"].done(v))
                            dve.wait_ge(*S["xs"].done(v))
                            dve.tensor_tensor(s1[:], tz[:], xs[:], ALU.add).then_inc(S["s1"].sem, 1)
                        if w is not None:
                            dve.wait_ge(*S["mix"].done(w))
                            dve.wait_ge(*S["lx"].done(w))
                            dve.wait_ge(*SD["outx2"].before(w))
                            dve.tensor_tensor(x2[:], mix[:], lx[:], ALU.add).then_inc(S["x2"].sem, 1)
                        if v is not None:
                            dve.wait_ge(*S["s1"].done(v))
                            norm_stats(dve, 0, v, s1[:])
                        if w is not None:
                            dve.wait_ge(*S["x2"].done(w))
                            norm_stats(dve, 2, w, x2[:])
                        if v is not None:
                            dve.wait_ge(*LN[0]["s"]["mv"].done(v))
                            dve.scalar_tensor_tensor(a1[:], s1[:], LN[0]["mv"][:, 0:1], r("ln1_g"), ALU.subtract, ALU.mult).then_inc(S["a1"].sem, 1)
                            norm_scale(dve, 0, v)
                            dve.wait_ge(*S["a1"].done(v))
                            dve.wait_ge(*S["x1Tp"].before(v))
                            dve.wait_ge(*LN[0]["s"]["rs"].done(v))
                            dve.scalar_tensor_tensor(x1[:], a1[:], LN[0]["rs"][:], r("ln1_b"), ALU.mult, ALU.add).then_inc(S["x1"].sem, 1)
                        if w is not None:
                            norm_scale(dve, 2, w)
                            rank_base(dve, R, 0, w)
                            dve.wait_ge(*LN[2]["s"]["rs"].done(w))
                            dve.wait_ge(*S["x2Tp"].before(w))
                            dve.tensor_scalar(x2n[:], x2[:], LN[2]["mv"][:, 0:1], LN[2]["rs"][:], ALU.subtract, ALU.mult).then_inc(S["x2n"].sem, 1)
                        if v is not None:
                            dve.wait_ge(*S["x1"].done(v))
                            dve.wait_ge(*S["s2"].before(v))
                            dve.tensor_tensor(x1b[:], x1[:], r("mix_b2"), ALU.add).then_inc(S["x1b"].sem, 1)
                        if more:
                            onehots(dve, G, w + 2)
                        if w is not None:
                            rank_near(dve, R, 0, w, w + T * RB1)
                            rank_place(dve, R, 0, w, w + T * RB1)
                            dve.wait_ge(*S["gat"].done(w))
                            dve.tensor_scalar(trow[:, bass.ds(w, 1), 0:16], bMM[:, 0:16].unsqueeze(1), 1.0, None, ALU.mult).then_inc(S["gatev"].sem, 1)
                        if v is not None:
                            extra_onehots(dve, G, seen, v, over)

                    onehots(dve, G, 0)
                    onehots(dve, G, 1)
                    body(None, 0, False)
                    over_windows(dve, body)
                    dve.wait_ge(S["gatev"].sem, T + 1)
                    dve.tensor_tensor(atp[:], trow[:, :, 0:16], r("att_src").unsqueeze(1).broadcast_to([P, T, 16]), ALU.mult).then_inc(s_tab, 1)
                    dve.wait_ge(s_tab, 1)
                    dve.tensor_reduce(trow[:, :, 16:20], atp[:].rearrange("p t (h e) -> p t h e", h=EH), AX.X, ALU.add).then_inc(s_tab, 1)
                    dve.wait_ge(s_tab, 2)
                    dve.tensor_tensor(atp[:], trow[:, :, 0:16], r("att_dst").unsqueeze(1).broadcast_to([P, T, 16]), ALU.mult).then_inc(s_tab, 1)
                    dve.wait_ge(s_tab, 3)
                    dve.memset(adst[:, T:TE, :], 0.0)
                    dve.tensor_reduce(adst[:, 0:T, :], atp[:].rearrange("p t (h e) -> p t h e", h=EH), AX.X, ALU.add).then_inc(s_tab, 1)
        early.close()
        clear_semaphores()
        if upto <= 3:
            return

        with ExitStack() as b:
            HALF = 2
            EI = FC // (HALF * GRP)
            got = [sbuf(b, f"got{h}", [P, GRP, TW], F32) for h in range(HALF)]
            isrc = [sbuf(b, f"isrc{h}", [P, GRP], I32) for h in range(HALF)]
            ipos = [sbuf(b, f"ipos{h}", [P, GRP], I32) for h in range(HALF)]
            s_isrc = [sem(f"d_isrc{h}") for h in range(HALF)]
            s_ipos = [sem(f"d_ipos{h}") for h in range(HALF)]
            s_got = [Step(sem(f"d_got{h}"), 16 * GRP, 0) for h in range(HALF)]
            s_put = [Step(sem(f"d_put{h}"), 16 * GRP, 0) for h in range(HALF)]
            go = sem("d_go")
            mw1 = sbuf(b, "mw1", [P, E * 2, FH], F32)
            mw2 = sbuf(b, "mw2", [P, E * 4, D], F32)
            fb1 = sbuf(b, "fb1", [P, E * 4], F32)
            xT = sbuf(b, "xT_d", [P, 2 * P], F32)
            gh = [sbuf(b, f"gh{e}", [P, FH], F32) for e in range(E)]
            Y = sbuf(b, "Y", [P, E * D], F32)
            bH = [psum(b, f"bH{e}") for e in range(E)]
            bY = [psum(b, f"bY{i}") for i in range(2)]
            S = steps("d", [f"h{e}" for e in range(E)] + [f"g{e}" for e in range(E)] + ["y0", "y1", "Y0", "Y1"])
            SD = steps("d", ["in", "out"], 16)
            d_load = sem("d_load")
            with nc.Block() as block:
                @block.gpsimd
                def _(pool):
                    with pool.Fori(0, EI) as i:
                        for h in range(HALF):
                            pool.wait_ge(s_isrc[h], (i + 1) * 16)
                            pool.wait_ge(s_ipos[h], (i + 1) * 16)
                            pool.sem_inc(go, 1)
                            for k in range(GRP):
                                pool.indirect_dma_start(
                                    out=got[h][:, k, :], out_offset=None, in_=heads_d,
                                    in_offset=bass.IndirectOffsetOnAxis(ap=isrc[h][:, k:k + 1], axis=0)).then_inc(s_got[h].sem, 16)
                        for h in range(HALF):
                            pool.wait_ge(s_ipos[h], (i + 1) * 16)
                            pool.wait_ge(*s_got[h].done(i))
                            pool.sem_inc(go, 1)
                            for k in range(GRP):
                                pool.indirect_dma_start(
                                    out=sorted_d, out_offset=bass.IndirectOffsetOnAxis(ap=ipos[h][:, k:k + 1], axis=0),
                                    in_=got[h][:, k, :], in_offset=None).then_inc(s_put[h].sem, 16)
                    for h in range(HALF):
                        pool.wait_ge(s_put[h].sem, EI * 16 * GRP)

                @block.sync
                def _(sp):
                    for h in range(HALF):
                        sp.dma_start(isrc[h][:], io["ffn_src"][h]).then_inc(s_isrc[h], 16)
                        sp.dma_start(ipos[h][:], pos[:, h * GRP:(h + 1) * GRP]).then_inc(s_ipos[h], 16)
                    sp.dma_start(mw1[:], io["moe_w1"]).then_inc(d_load, 16)
                    sp.dma_start(mw2[:], io["moe_w2"]).then_inc(d_load, 16)
                    sp.dma_start(fb1[:], io["moe_b1"]).then_inc(d_load, 16)
                    with sp.Fori(0, EI) as i:
                        for h in range(HALF):
                            sp.wait_ge(*s_got[h].done(i))
                            sp.dma_start(isrc[h][:], io["ffn_src"][bass.ds((i + 1) * HALF + h, 1)].rearrange("g p k -> (g p) k"))\
                                .then_inc(s_isrc[h], 16)
                        for h in range(HALF):
                            sp.wait_ge(*s_put[h].done(i))
                            sp.dma_start(ipos[h][:], pos[:, bass.ds((i + 1) * HALF * GRP + h * GRP, GRP)]).then_inc(s_ipos[h], 16)
                    for h in range(HALF):
                        sp.wait_ge(s_isrc[h], (EI + 1) * 16)
                        sp.wait_ge(s_ipos[h], (EI + 1) * 16)

                @block.scalar
                def _(act):
                    for e in range(E):
                        S[f"g{e}"].start(act)
                    for s in SD.values():
                        s.start(act)
                    act.wait_ge(d_load, 48)
                    with act.Fori(0, T) as t:
                        act.wait_ge(*S[f"h{E - 1}"].before(t))
                        act.dma_start(xT[:], x2nT_d[bass.ds(t, 1)].rearrange("t p d -> (t p) d")).then_inc(SD["in"].sem, 16)
                        for e in range(E):
                            act.wait_ge(*S[f"h{e}"].done(t))
                            act.wait_ge(*S[f"y{e // 2}"].before(t))
                            for f in range(4):
                                last = act.activation(gh[e][:, f * P:(f + 1) * P], bH[e][:, f * P:(f + 1) * P], ACT.Gelu,
                                                      bias=fb1[:, e * 4 + f:e * 4 + f + 1])
                            last.then_inc(S[f"g{e}"].sem, 1)
                        act.wait_ge(*S["Y0"].done(t))
                        act.wait_ge(*S["Y1"].done(t))
                        act.dma_start(experts_d[bass.ds(t, 1)].rearrange("t p d -> (t p) d"), Y[:]).then_inc(SD["out"].sem, 16)
                    act.wait_ge(SD["in"].sem, (T + 1) * 16)
                    act.wait_ge(SD["out"].sem, (T + 1) * 16)

                @block.tensor
                def _(pe):
                    for e in range(E):
                        S[f"h{e}"].start(pe)
                    S["y0"].start(pe)
                    S["y1"].start(pe)
                    pe.wait_ge(d_load, 48)
                    with pe.Fori(0, T) as t:
                        pe.wait_ge(*SD["in"].done(t))
                        for e in range(E):
                            pe.wait_ge(*S[f"g{e}"].before(t))
                            for f in range(4):
                                for j in range(2):
                                    last = pe.matmul(bH[e][:, f * P:(f + 1) * P], mw1[:, e * 2 + j, f * P:(f + 1) * P],
                                                     xT[:, j * P:(j + 1) * P], start=(j == 0), stop=(j == 1))
                            last.then_inc(S[f"h{e}"].sem, 1)
                        for e in range(E):
                            pe.wait_ge(*S[f"g{e}"].done(t))
                            if e % 2 == 0:
                                pe.wait_ge(*S[f"Y{e // 2}"].before(t))
                            for f in range(4):
                                last = pe.matmul(bY[e // 2][:, (e % 2) * D:(e % 2 + 1) * D], gh[e][:, f * P:(f + 1) * P],
                                                 mw2[:, e * 4 + f, :], start=(f == 0), stop=(f == 3))
                            if e % 2:
                                last.then_inc(S[f"y{e // 2}"].sem, 1)

                @block.vector
                def _(dve):
                    S["Y0"].start(dve)
                    S["Y1"].start(dve)
                    with dve.Fori(0, T) as t:
                        dve.wait_ge(*SD["out"].before(t))
                        for i in range(2):
                            dve.wait_ge(*S[f"y{i}"].done(t))
                            dve.tensor_tensor(Y[:, i * 2 * D:(i + 1) * 2 * D], bY[i][:],
                                              r("ffn_b2")[:, i * 2 * D:(i + 1) * 2 * D], ALU.add).then_inc(S[f"Y{i}"].sem, 1)
        clear_semaphores()
        if upto <= 4:
            return

        with ExitStack() as b:
            m = sbuf(b, "m", [P, TE, EH], F32)
            den = sbuf(b, "den_e", [P, TE, EH], F32)
            agg = sbuf(b, "agg", [P, TE, 16], F32)
            Yt = [sbuf(b, f"Yt{k}", [P, E * D], F32) for k in range(NY)]
            xt = [sbuf(b, f"xt{k}", [P, D], F32) for k in range(NY)]
            idx = [sbuf(b, f"idx_e{i}", [P, 1], I32) for i in range(QT + 1)]
            got = [sbuf(b, f"got_e{i}", [P, L * TW], F32) for i in range(QT)]
            W = []
            for i in range(2):
                B = {k: sbuf(b, f"{k}_e{i}", [P, L, EH], F32) for k in ("e0", "e1", "e2", "e3", "ee")}
                B.update({k: sbuf(b, f"{k}_e{i}", [P, EH], F32) for k in ("mr", "mn", "dm", "corr", "sr", "dc")})
                B.update({k: sbuf(b, f"{k}_e{i}", [P, 16], F32) for k in ("ar", "ac")})
                B["pen"] = sbuf(b, f"pen{i}", [P, L], F32)
                B["prod"] = sbuf(b, f"prod_e{i}", [P, L, 16], F32)
                W.append(B)
            XR = QT
            S = steps("e", [f"idx{i}" for i in range(QT + 1)] + ["first", "left"])
            SG = [Step(sem(f"e_got{i}"), 16, 0) for i in range(QT + 1)]
            s_init = sem("e_init")
            s_ahead = sem("e_ahead")
            s_turns = sem("e_turns")
            go = sem("e_go")
            names = ["e0", "e1", "pen", "e2", "mr", "mn", "dm", "m", "e3", "corr", "ee", "sr", "dc", "den", "prod", "ar", "ac", "agg"]
            ACT_STEPS = ("corr", "ee")
            SR = [steps(f"e_{i}", names) for i in range(QT + 1)]

            def gather_block(pool, i, n):
                pool.wait_ge(*S[f"idx{i}"].done(n))
                pool.sem_inc(go, 1)
                pool.indirect_dma_start(out=got[i % QT][:], out_offset=None, in_=sorted_d,
                                        in_offset=bass.IndirectOffsetOnAxis(ap=idx[i][:], axis=0)).then_inc(SG[i].sem, 16)

            def fold(dve, i, t, n, next_idx=None):
                s, B = SR[i], W[i % 2]
                g3 = got[i % QT][:].rearrange("p (l f) -> p l f", f=TW)
                mt = flat(m[:, bass.ds(t, 1), :])
                dt_ = flat(den[:, bass.ds(t, 1), :])
                at = flat(agg[:, bass.ds(t, 1), :])

                def logits():
                    dve.wait_ge(*SG[i].done(n))
                    dve.tensor_tensor(B["e0"][:], g3[:, :, 16:20], adst[:, bass.ds(t, 1), :].broadcast_to([P, L, EH]), ALU.add).then_inc(s["e0"].sem, 1)

                def absent():
                    dve.tensor_scalar(B["pen"][:], c("slot"), deg[:, bass.ds(t, 1)], -1e30, ALU.is_ge, ALU.mult).then_inc(s["pen"].sem, 1)

                def leaky():
                    dve.wait_ge(*s["e0"].done(n))
                    dve.scalar_tensor_tensor(B["e1"][:], B["e0"][:], 0.2, B["e0"][:], ALU.mult, ALU.max).then_inc(s["e1"].sem, 1)

                def masked():
                    dve.wait_ge(*s["e1"].done(n))
                    dve.wait_ge(*s["pen"].done(n))
                    dve.tensor_tensor(B["e2"][:], B["e1"][:], B["pen"][:].unsqueeze(2).broadcast_to([P, L, EH]), ALU.add).then_inc(s["e2"].sem, 1)

                def largest():
                    dve.wait_ge(*s["e2"].done(n))
                    dve.tensor_reduce(B["mr"][:], B["e2"][:].rearrange("p l h -> p h l"), AX.X, ALU.max).then_inc(s["mr"].sem, 1)

                def new_max():
                    dve.wait_ge(*s["mr"].done(n))
                    dve.tensor_tensor(B["mn"][:], B["mr"][:], mt, ALU.max).then_inc(s["mn"].sem, 1)

                def shifted():
                    dve.wait_ge(*s["mn"].done(n))
                    dve.tensor_tensor(B["e3"][:], B["e2"][:], B["mn"][:].unsqueeze(1).broadcast_to([P, L, EH]), ALU.subtract).then_inc(s["e3"].sem, 1)

                def max_change():
                    dve.tensor_tensor(B["dm"][:], mt, B["mn"][:], ALU.subtract).then_inc(s["dm"].sem, 1)

                def keep_max():
                    dve.wait_ge(*s["dm"].done(n))
                    dve.tensor_scalar(mt, B["mn"][:], 1.0, None, ALU.mult).then_inc(s["m"].sem, 1)

                def rescale():
                    dve.wait_ge(*s["corr"].done(n))
                    dve.tensor_tensor(B["dc"][:], dt_, B["corr"][:], ALU.mult).then_inc(s["dc"].sem, 1)
                    dve.tensor_tensor(B["ac"][:].rearrange("p (h e) -> p h e", h=EH), at.rearrange("p (h e) -> p h e", h=EH),
                                      B["corr"][:].unsqueeze(2).broadcast_to([P, EH, E]), ALU.mult).then_inc(s["ac"].sem, 1)

                def weigh():
                    dve.wait_ge(*s["ee"].done(n))
                    dve.tensor_tensor(B["prod"][:].rearrange("p l (h e) -> p l h e", h=EH), g3[:, :, 0:16].rearrange("p l (h e) -> p l h e", h=EH),
                                      B["ee"][:].unsqueeze(3).broadcast_to([P, L, EH, E]), ALU.mult).then_inc(s["prod"].sem, 1)

                def sum_weights():
                    dve.tensor_reduce(B["sr"][:], B["ee"][:].rearrange("p l h -> p h l"), AX.X, ALU.add).then_inc(s["sr"].sem, 1)

                def sum_rows():
                    dve.wait_ge(*s["prod"].done(n))
                    if next_idx:
                        next_idx()
                    dve.tensor_reduce(B["ar"][:], B["prod"][:].rearrange("p l f -> p f l"), AX.X, ALU.add).then_inc(s["ar"].sem, 1)

                def add_weights():
                    dve.wait_ge(*s["sr"].done(n))
                    dve.wait_ge(*s["dc"].done(n))
                    dve.tensor_tensor(dt_, B["dc"][:], B["sr"][:], ALU.add).then_inc(s["den"].sem, 1)

                def add_rows():
                    dve.wait_ge(*s["ar"].done(n))
                    dve.wait_ge(*s["ac"].done(n))
                    dve.tensor_tensor(at, B["ac"][:], B["ar"][:], ALU.add).then_inc(s["agg"].sem, 1)

                return [logits, absent, leaky, masked, largest, new_max, shifted, max_change, keep_max, rescale, weigh,
                        sum_weights, sum_rows, add_weights, add_rows]

            def folded(dve, i, n):
                for k in ("m", "den", "agg"):
                    dve.wait_ge(*SR[i][k].done(n))

            def exps(act, i, n):
                s, B = SR[i], W[i % 2]
                act.wait_ge(*s["dm"].done(n))
                act.activation(B["corr"][:], B["dm"][:], ACT.Exp).then_inc(s["corr"].sem, 1)
                act.wait_ge(*s["e3"].done(n))
                act.activation(flat(B["ee"][:]), flat(B["e3"][:]), ACT.Exp).then_inc(s["ee"].sem, 1)

            def turns(eng):
                tiles = eng.value_load(etab[0:1, 0:1], min_val=1, max_val=T)
                return (tiles + (QT - 1)) // QT

            def node_rounds(eng, body):
                seen = counter(eng, "rounds")
                largest = eng.value_load(etab[0:1, 1:2], min_val=0, max_val=FE)
                with eng.If(largest > L):
                    with eng.Fori(0, T) as t:
                        most = eng.value_load(dtab[0:1, bass.ds(t, 1)], min_val=0, max_val=FE)
                        with eng.If(most > L):
                            with eng.Fori(1, (most + (L - 1)) // L) as k:
                                body(t, k, eng.snap(seen, min_val=0, max_val=FE))
                                eng.reg_add(seen, seen, 1)

            with nc.Block() as block:
                @block.gpsimd
                def _(pool):
                    with pool.Fori(0, turns(pool)) as t4:
                        for i in range(QT):
                            gather_block(pool, i, t4)
                    node_rounds(pool, lambda t, k, n: gather_block(pool, XR, n))

                @block.sync
                def _(sp):
                    for k in range(NY):
                        sp.dma_start(Yt[k][:], experts_d[k]).then_inc(s_ahead, 16)
                        sp.dma_start(xt[k][:], x2_d[k * P:(k + 1) * P, :]).then_inc(s_ahead, 16)
                    sp.wait_ge(s_ahead, NY * 32)

                @block.scalar
                def _(act):
                    for s in SR:
                        for k in ACT_STEPS:
                            s[k].start(act)
                    with act.Fori(0, turns(act)) as t4:
                        for i in range(QT):
                            exps(act, i, t4)
                    node_rounds(act, lambda t, k, n: exps(act, XR, n))

                @block.vector
                def _(dve):
                    for s in list(S.values()):
                        s.start(dve)
                    for s in SR:
                        for k in names:
                            if k not in ACT_STEPS:
                                s[k].start(dve)
                    dve.memset(agg[:, T:TE, :], 0.0)
                    dve.memset(m[:, T:TE, :], 0.0)
                    dve.tensor_copy(agg[:, 0:T, :], trow[:, :, 0:16])
                    dve.memset(den[:], 1.0)
                    dve.tensor_tensor(m[:, 0:T, :], trow[:, :, 16:20], adst[:, 0:T, :], ALU.add).then_inc(s_init, 1)
                    dve.wait_ge(s_init, 1)
                    dve.scalar_tensor_tensor(m[:, 0:T, :], m[:, 0:T, :], 0.2, m[:, 0:T, :], ALU.mult, ALU.max).then_inc(s_init, 1)
                    for i in range(QT):
                        dve.tensor_copy(idx[i][:], first[:, i:i + 1]).then_inc(S[f"idx{i}"].sem, 1)
                    dve.wait_ge(s_init, 2)
                    dve.sem_inc(s_turns, 1)

                    def next_places(i, t):
                        def write():
                            dve.tensor_scalar(idx[i][:], first[:, bass.ds(t + QT, 1)], 1.0, None, ALU.mult).then_inc(S[f"idx{i}"].sem, 1)
                        return write

                    with dve.Fori(0, turns(dve)) as t4:
                        for i in range(0, QT, 2):
                            t = t4 * QT + i
                            last = [(i - 2 + j, t4 + 1) for j in range(2)] if i else [(QT - 2 + j, t4) for j in range(2)]
                            for j, n in last:
                                for k in ("m", "den", "agg"):
                                    dve.wait_ge(SR[j][k].sem, n + 1)
                            for pair in zip(*(fold(dve, i + j, t + j, t4, next_places(i + j, t + j)) for j in range(2))):
                                for stage in pair:
                                    stage()

                    def body(t, k, n):
                        ft, dt_ = first[:, bass.ds(t, 1)], deg[:, bass.ds(t, 1)]
                        for name in ("m", "den", "agg"):
                            dve.wait_ge(*SR[XR][name].before(n))
                        dve.tensor_scalar(ft, ft, float(L), float(FE), ALU.add, ALU.min).then_inc(S["first"].sem, 1)
                        dve.tensor_scalar(dt_, dt_, float(L), None, ALU.subtract).then_inc(S["left"].sem, 1)
                        dve.wait_ge(*S["first"].done(n))
                        dve.tensor_scalar(idx[XR][:], ft, 1.0, None, ALU.mult).then_inc(S[f"idx{XR}"].sem, 1)
                        dve.wait_ge(*S["left"].done(n))
                        for stage in fold(dve, XR, t, n):
                            stage()
                    done = turns(dve)
                    for i in range(QT):
                        for k in ("m", "den", "agg"):
                            dve.wait_ge(SR[i][k].sem, done + 1)
                    dve.sem_inc(s_turns, 1)
                    node_rounds(dve, body)
            clear_semaphores()
            if upto <= 5:
                return

            sc = sbuf(b, "sc_f", [P, T, 16], F32)
            sq = sbuf(b, "sq_f", [P, T, 16], F32)
            rd = sbuf(b, "rd_f", [P, T, EH], F32)
            mu, vr, sd, rs = (sbuf(b, f"stat_f{i}", [P, T], F32) for i in range(4))
            score, gate, rank = (sbuf(b, f"score_f{i}", [P, T, E], F32) for i in range(3))
            beats = sbuf(b, "beats", [P, T, E, E], F32)
            chain = sem("f_chain")
            s_sd, s_ex, s_sp = sem("f_sd"), sem("f_ex"), sem("f_sp_turns")
            SF = [Step(sem(f"f_acc{k}"), E) for k in range(NY)]
            SIN = [Step(sem(f"f_in{k}"), 32) for k in range(NY)]
            SOUT = [Step(sem(f"f_out{k}"), 16) for k in range(NY)]
            TN = T // NY

            with nc.Block() as block:
                @block.sync
                def _(sp):
                    for k in range(NY):
                        SIN[k].start(sp)
                    with sp.Fori(1, TN) as n:
                        for k in range(NY):
                            sp.wait_ge(*SOUT[k].before(n))
                            sp.sem_inc(s_sp, 1)
                            sp.dma_start(Yt[k][:], experts_d[bass.ds(n * NY + k, 1)].rearrange("t p d -> (t p) d")).then_inc(SIN[k].sem, 16)
                            sp.dma_start(xt[k][:], tile_rows(x2_d, n * NY + k)).then_inc(SIN[k].sem, 16)

                @block.scalar
                def _(act):
                    for k in range(NY):
                        SOUT[k].start(act)
                    act.wait_ge(chain, 7)
                    act.activation(sd[:], vr[:], ACT.Sqrt, bias=c("eps")).then_inc(s_sd, 1)
                    act.wait_ge(chain, 16)
                    act.activation(flat(gate[:]), flat(score[:]), ACT.Exp).then_inc(s_ex, 1)
                    with act.Fori(0, TN) as n:
                        for k in range(NY):
                            act.wait_ge(*SF[k].done(n))
                            act.dma_start(tile_rows(out, n * NY + k), xt[k][:]).then_inc(SOUT[k].sem, 16)
                    for k in range(NY):
                        act.wait_ge(SOUT[k].sem, (TN + 1) * 16)

                @block.vector
                def _(dve):
                    n = [0]

                    def link(ins):
                        n[0] += 1
                        ins.then_inc(chain, 1)
                        dve.wait_ge(chain, n[0])

                    def wide(ap, k):
                        return ap.unsqueeze(2).broadcast_to([P, T, k])

                    for k in range(NY):
                        SF[k].start(dve)
                    dve.memset(beats[:], 0.0)
                    link(dve.tensor_scalar(den[:, 0:T, :], den[:, 0:T, :], 1e-16, None, ALU.add))
                    link(dve.reciprocal(rd[:], den[:, 0:T, :]))
                    link(dve.tensor_tensor(sc[:].rearrange("p t (h e) -> p t h e", h=EH), agg[:, 0:T, :].rearrange("p t (h e) -> p t h e", h=EH),
                                           rd[:].unsqueeze(3).broadcast_to([P, T, EH, E]), ALU.mult))
                    link(dve.tensor_tensor(sc[:], sc[:], r("b_gat").unsqueeze(1).broadcast_to([P, T, 16]), ALU.add))
                    link(dve.tensor_reduce(mu[:], sc[:], AX.X, ALU.add))
                    link(dve.scalar_tensor_tensor(sc[:], wide(mu[:], 16), -1.0 / 16, sc[:], ALU.mult, ALU.add))
                    dve.tensor_tensor(sq[:], sc[:], sc[:], ALU.mult).then_inc(s_ex, 1)
                    dve.wait_ge(s_ex, 1)
                    dve.tensor_reduce(mu[:], sq[:], AX.X, ALU.add).then_inc(s_ex, 1)
                    dve.wait_ge(s_ex, 2)
                    link(dve.tensor_scalar(vr[:], mu[:], 1.0 / 16, None, ALU.mult))
                    dve.wait_ge(s_sd, 1)
                    link(dve.reciprocal(rs[:], sd[:]))
                    link(dve.tensor_tensor(sc[:], sc[:], wide(rs[:], 16), ALU.mult))
                    link(dve.tensor_tensor(sc[:], sc[:], r("gamma").unsqueeze(1).broadcast_to([P, T, 16]), ALU.mult))
                    link(dve.tensor_tensor(sc[:], sc[:], r("beta").unsqueeze(1).broadcast_to([P, T, 16]), ALU.add))
                    link(dve.tensor_reduce(rank[:], sc[:].rearrange("p t (h e) -> p t e h", h=EH), AX.X, ALU.add))
                    link(dve.tensor_scalar(score[:], rank[:], 1.0 / EH, None, ALU.mult))
                    for e in range(E):
                        for j in range(E):
                            if j != e:
                                last = dve.tensor_tensor(beats[:, :, e, j], score[:, :, j], score[:, :, e], ALU.is_ge if j < e else ALU.is_gt)
                    link(last)
                    link(dve.tensor_reduce(mu[:], score[:], AX.X, ALU.max))
                    link(dve.tensor_tensor(score[:], score[:], wide(mu[:], E), ALU.subtract))
                    link(dve.tensor_reduce(rank[:], beats[:], AX.X, ALU.add))
                    link(dve.tensor_scalar(rank[:], rank[:], 2.0, None, ALU.is_lt))
                    dve.wait_ge(s_ex, 3)
                    link(dve.tensor_tensor(gate[:], gate[:], rank[:], ALU.mult))
                    link(dve.tensor_reduce(mu[:], gate[:], AX.X, ALU.add))
                    link(dve.reciprocal(rs[:], mu[:]))
                    link(dve.tensor_tensor(gate[:], gate[:], wide(rs[:], E), ALU.mult))
                    with dve.Fori(0, TN) as n:
                        for k in range(0, NY, 2):
                            for i in (k, k + 1):
                                dve.wait_ge(SIN[i].sem, (n + 1) * 32)
                            for e in range(E):
                                for i in (k, k + 1):
                                    if e:
                                        dve.wait_ge(SF[i].sem, (n + 1) * E + e)
                                    dve.scalar_tensor_tensor(xt[i][:], Yt[i][:, e * D:(e + 1) * D], flat(gate[:, bass.ds(n * NY + i, 1), e:e + 1]),
                                                             xt[i][:], ALU.mult, ALU.add).then_inc(SF[i].sem, 1)


def layouts(x, src, dst, L0_gnn_W_l1, L0_gnn_b1, L0_gnn_W_r1, L0_gnn_W_l2, L0_gnn_b2, L0_gnn_W_r2, L0_mix_Wqkv,
            L0_mix_ln1_g, L0_mix_ln1_b, L0_mix_W1, L0_mix_b1, L0_mix_W2, L0_mix_b2, L0_mix_ln2_g, L0_mix_ln2_b,
            L0_ffn_W_gat, L0_ffn_att_src, L0_ffn_att_dst, L0_ffn_b_gat, L0_ffn_ln_gamma, L0_ffn_ln_beta,
            L0_ffn_W1, L0_ffn_b1, L0_ffn_W2, L0_ffn_b2, L0_ffn_edge_index):
    def chunks(v, count, fill):
        v = np.concatenate([v, np.full(count * P - v.shape[0], fill, v.dtype)])
        return v.reshape(count, P).T

    def halves(w):
        return w.reshape(2, P, -1).transpose(1, 0, 2)

    gdst = chunks(dst, GC, NO_NODE)
    fdst = chunks(L0_ffn_edge_index[1], FCP, NO_NODE)
    rows = {"gnn_b1": L0_gnn_b1, "gnn_b2": L0_gnn_b2, "ln1_g": L0_mix_ln1_g, "ln1_b": L0_mix_ln1_b,
            "mix_b2": L0_mix_b2, "ln2_g": L0_mix_ln2_g, "ln2_b": L0_mix_ln2_b, "att_src": L0_ffn_att_src,
            "att_dst": L0_ffn_att_dst, "b_gat": L0_ffn_b_gat, "gamma": L0_ffn_ln_gamma, "beta": L0_ffn_ln_beta,
            "ffn_b2": L0_ffn_b2}
    return {
        "consts": shape_constants(),
        "x": np.pad(x, ((0, NP - N), (0, 0))),
        "gnn_src": chunks(src, GC, 0).T.reshape(1, -1),
        "gnn_dst": gdst.T.reshape(1, -1),
        "gnn_dst_ends": gdst[P - 1:P],
        "ffn_src": chunks(L0_ffn_edge_index[0], FC + 2 * GRP, 0).reshape(P, FC // GRP + 2, GRP).transpose(1, 0, 2),
        "ffn_dst": fdst,
        "ffn_dst_rows": fdst.T.reshape(1, FCP * P),
        "wlr1": halves(np.concatenate([L0_gnn_W_l1, L0_gnn_W_r1], 1)),
        "wlr2": halves(np.concatenate([L0_gnn_W_l2, L0_gnn_W_r2], 1)),
        "wkv": halves(L0_mix_Wqkv[D:].T),
        "wq": halves(L0_mix_Wqkv[:D].T),
        "w1": halves(L0_mix_W1.T),
        "w2": halves(L0_mix_W2.T),
        "mix_b1": L0_mix_b1.reshape(2, P).T,
        "wgat": halves(L0_ffn_W_gat),
        "moe_w1": L0_ffn_W1.reshape(E, 2, P, FH).transpose(2, 0, 1, 3).reshape(P, E * 2, FH),
        "moe_w2": L0_ffn_W2.reshape(E, 4, P, D).transpose(2, 0, 1, 3).reshape(P, E * 4, D),
        "moe_b1": L0_ffn_b1.reshape(E * 4, P).T,
        "rows": np.concatenate([rows[k].reshape(-1) for k, _ in ROW_SIZES])[None, :],
    }


KINDS = "Internal"
UPTO = 9


def kernel(**inputs):
    import concourse.bacc as _bacc
    from concourse.bass_utils import run_bass_kernel_spmd as _run

    nc = _bacc.Bacc("TRN2", target_bir_lowering=False, num_devices=1)
    arrays, io = {}, {}
    for name, a in layouts(**{k: np.asarray(v) for k, v in inputs.items()}).items():
        a = np.ascontiguousarray(a)
        arrays[f"in_{name}"] = a
        io[name] = nc.dram_tensor(f"in_{name}", a.shape, mybir.dt.from_np(a.dtype), kind="ExternalInput").ap()
    out = nc.dram_tensor("out_0", (NP, D), F32, kind="ExternalOutput").ap()
    build(nc, io, out, KINDS, UPTO)
    r = _run(nc, [arrays], core_ids=[0])
    return r.results[0]["out_0"][:N]
```
